# Optimizing a Trainium2 kernel written in Bass

```python
import numpy as np
import jax
import jax.numpy as jnp

def _softmax(x, axis=-1):
    return jax.nn.softmax(x, axis=axis)

def _gelu(x):
    return jax.nn.gelu(x, approximate=True)

def _silu(x):
    return jax.nn.silu(x)

def _sigmoid(x):
    return jax.nn.sigmoid(x)

def _layernorm(x, axis=-1, eps=1e-05):
    m = jnp.mean(x, axis=axis, keepdims=True)
    v = jnp.var(x, axis=axis, keepdims=True)
    return (x - m) / jnp.sqrt(v + eps)

def _scatter_add(tgt, idx, src, axis=0):
    return tgt.at[idx].add(src)

def _segment_sum(src, seg, n):
    return jax.ops.segment_sum(src, seg, n)
kernel_name = 'mk_seq_postln_d4_jaxref_r8_d5fde8'

def setup_inputs(seed: int=0):
    np.random.seed(seed)
    _w = jnp.asarray

    def _L0_attn_setup():
        import jax, jax.numpy as jnp
        import numpy as np
        B, S, D = (2, 256, 128)
        H, DH = (16, 64)
        DQL, DKVL = (64, 64)
        DR = 64
        TOPK = 64
        LN_EPS = 1e-05
        ROPE_BASE = 10000.0

        def _rope_tables(seq_len, dim):
            inv_freq = 1.0 / ROPE_BASE ** (np.arange(0, dim, 2, dtype=np.float32) / dim)
            t = np.arange(seq_len, dtype=np.float32)
            freqs = np.outer(t, inv_freq)
            cos = np.concatenate([np.cos(freqs), np.cos(freqs)], -1)[:, ::2]
            sin = np.concatenate([np.sin(freqs), np.sin(freqs)], -1)[:, ::2]
            return (jnp.asarray(cos), jnp.asarray(sin))

        def _apply_rope_subspace(x, d_rope):
            s = x.shape[-2]
            cos, sin = _rope_tables(s, d_rope)
            xr, xp = (x[..., :d_rope], x[..., d_rope:])
            e, o = (xr[..., 0::2], xr[..., 1::2])
            rot = jnp.stack([e * cos - o * sin, e * sin + o * cos], axis=-1).reshape(xr.shape)
            return jnp.concatenate([rot, xp], axis=-1)

        def _reference_tuple_inner(x, w_down_q, w_down_kv, w_up_q, w_up_k, w_up_v, w_out, ln_scale, ln_bias):
            b, s, d = x.shape
            residual = x
            mu = jnp.mean(x, axis=-1, keepdims=True)
            var = jnp.mean((x - mu) ** 2, axis=-1, keepdims=True)
            h = (x - mu) * jax.lax.rsqrt(var + LN_EPS) * ln_scale + ln_bias
            c_q = h @ w_down_q.T
            c_kv = h @ w_down_kv.T
            q = (c_q @ w_up_q.T).reshape(b, s, H, DH).transpose(0, 2, 1, 3)
            k = (c_kv @ w_up_k.T).reshape(b, s, H, DH).transpose(0, 2, 1, 3)
            v = (c_kv @ w_up_v.T).reshape(b, s, H, DH).transpose(0, 2, 1, 3)
            q = _apply_rope_subspace(q, DR)
            k = _apply_rope_subspace(k, DR)
            scale = 1.0 / np.sqrt(DH).astype(np.float32)
            scores = jnp.einsum('bhqd,bhkd->bhqk', q, k) * scale
            _, indices = jax.lax.top_k(scores, min(TOPK, s))
            attn = jax.nn.softmax(scores, axis=-1)
            out = jnp.einsum('bhqk,bhkd->bhqd', attn, v)
            out = out.transpose(0, 2, 1, 3).reshape(b, s, H * DH)
            out = out @ w_out.T + residual
            return (out, indices.astype(jnp.int64))
        key = jax.random.key(seed)
        ks = jax.random.split(key, 7)
        init = lambda k, shape: jax.random.normal(k, shape, jnp.float32) * 0.02
        return {'x': jax.random.normal(ks[0], (B, S, D), jnp.float32), 'w_down_q': init(ks[1], (DQL, D)), 'w_down_kv': init(ks[2], (DKVL, D)), 'w_up_q': init(ks[3], (H * DH, DQL)), 'w_up_k': init(ks[4], (H * DH, DKVL)), 'w_up_v': init(ks[5], (H * DH, DKVL)), 'w_out': init(ks[6], (D, H * DH)), 'ln_scale': jnp.ones((D,), jnp.float32), 'ln_bias': jnp.zeros((D,), jnp.float32)}
    _L0_attn_in = _L0_attn_setup()

    def _L0_ffn_setup():
        import jax, jax.numpy as jnp
        import numpy as np
        DIM = 128
        HIDDEN = 256
        N_EXPERTS = 8
        TOP_K = 2
        EPS = 1e-06

        def rms_norm(x, scale, eps=EPS):
            ms = jnp.mean(jnp.square(x.astype(jnp.float32)), axis=-1, keepdims=True)
            s = scale.astype(jnp.float32) * jax.lax.rsqrt(ms + eps)
            return x * s.astype(x.dtype)

        def moe_linear(xf, ids, W):
            E = W.shape[0]
            out = jnp.zeros((xf.shape[0], W.shape[1]), dtype=xf.dtype)
            for e in range(E):
                out = out + jnp.where((ids == e)[:, None], xf @ W[e].T, 0.0)
            return out
        key = jax.random.key(seed)
        k1, k2, k3, k4 = jax.random.split(key, 4)
        x = jax.random.normal(k1, (4, 512, DIM), dtype=jnp.float32)
        norm_scale = jnp.ones((DIM,), dtype=jnp.float32)
        w_router = jax.random.normal(k2, (N_EXPERTS, DIM), dtype=jnp.float32) / np.sqrt(DIM)
        lim_up = np.sqrt(6.0 / (DIM + 2 * HIDDEN))
        w_up = jax.random.uniform(k3, (N_EXPERTS, 2 * HIDDEN, DIM), dtype=jnp.float32, minval=-lim_up, maxval=lim_up)
        lim_dn = np.sqrt(6.0 / (HIDDEN + DIM))
        w_down = jax.random.uniform(k4, (N_EXPERTS, DIM, HIDDEN), dtype=jnp.float32, minval=-lim_dn, maxval=lim_dn)
        return {'x': x, 'norm_scale': norm_scale, 'w_router': w_router, 'w_up': w_up, 'w_down': w_down}
    _L0_ffn_in = _L0_ffn_setup()

    def _L1_attn_setup():
        import jax, jax.numpy as jnp
        import numpy as np
        B, S, D = (4, 512, 128)
        H = 16
        HD = D // H

        def feature_map(x):
            return jnp.exp(-jnp.square(x) * 0.5)
        key = jax.random.key(seed)
        ks = jax.random.split(key, 9)
        s = 1.0 / np.sqrt(D)
        return {'x': jax.random.normal(ks[0], (B, S, D), dtype=jnp.float32), 'Wq': jax.random.normal(ks[1], (D, D), dtype=jnp.float32) * s, 'bq': jax.random.normal(ks[2], (D,), dtype=jnp.float32) * s, 'Wk': jax.random.normal(ks[3], (D, D), dtype=jnp.float32) * s, 'bk': jax.random.normal(ks[4], (D,), dtype=jnp.float32) * s, 'Wv': jax.random.normal(ks[5], (D, D), dtype=jnp.float32) * s, 'bv': jax.random.normal(ks[6], (D,), dtype=jnp.float32) * s, 'Wo': jax.random.normal(ks[7], (D, D), dtype=jnp.float32) * s, 'bo': jax.random.normal(ks[8], (D,), dtype=jnp.float32) * s}
    _L1_attn_in = _L1_attn_setup()

    def _L1_ffn_setup():
        import jax, jax.numpy as jnp
        import numpy as np
        D = 128
        F = 4 * D
        E = 8
        NS = 2
        TOP_K = 2
        B, S = (2, 128)
        key = jax.random.key(seed)
        ks = jax.random.split(key, 7)
        w = 1.0 / np.sqrt(D)
        wf = 1.0 / np.sqrt(F)
        return {'x': jax.random.normal(ks[0], (B, S, D), jnp.float32), 'centroids': jax.random.normal(ks[1], (E, D), jnp.float32) * w, 'routing_bias': jnp.zeros((E,), jnp.float32), 'Wfc_r': jax.random.normal(ks[2], (E, F, D), jnp.float32) * w, 'Wproj_r': jax.random.normal(ks[3], (E, D, F), jnp.float32) * wf, 'Wfc_sh': jax.random.normal(ks[4], (NS, F, D), jnp.float32) * w, 'Wproj_sh': jax.random.normal(ks[5], (NS, D, F), jnp.float32) * wf}
    _L1_ffn_in = _L1_ffn_setup()

    def _L2_attn_setup():
        import jax, jax.numpy as jnp
        import numpy as np
        D_MODEL = 128
        N_HEADS = 16
        D_HEAD = D_MODEL // N_HEADS
        SCALE = 1.0 / np.sqrt(D_HEAD).astype(np.float32)

        def _feature_map(x):
            return jax.nn.elu(x) + 1.0
        key = jax.random.key(seed)
        ks = jax.random.split(key, 7)
        b, s = (4, 256)
        w = 1.0 / np.sqrt(D_MODEL).astype(np.float32)
        return {'x': jax.random.normal(ks[0], (b, s, D_MODEL), dtype=jnp.float32), 'Wq': jax.random.normal(ks[1], (D_MODEL, D_MODEL), dtype=jnp.float32) * w, 'Wk': jax.random.normal(ks[2], (D_MODEL, D_MODEL), dtype=jnp.float32) * w, 'Wv': jax.random.normal(ks[3], (D_MODEL, D_MODEL), dtype=jnp.float32) * w, 'Wo': jax.random.normal(ks[4], (D_MODEL, D_MODEL), dtype=jnp.float32) * w, 'Wg': jax.random.normal(ks[5], (N_HEADS, D_MODEL), dtype=jnp.float32) * w, 'bg': jax.random.normal(ks[6], (N_HEADS,), dtype=jnp.float32) * 0.02}
    _L2_attn_in = _L2_attn_setup()

    def _L2_ffn_setup():
        import jax, jax.numpy as jnp
        import numpy as np
        B, S, D, E, H, K = (4, 256, 128, 8, 128, 2)
        CAPACITY_FACTOR = 1.25
        MIN_CAPACITY = 4
        key = jax.random.key(seed)
        ks = jax.random.split(key, 5)
        return {'inputs': jax.random.normal(ks[0], (B, S, D), jnp.float32), 'router_w': jax.random.normal(ks[1], (D, E), jnp.float32) / np.sqrt(D), 'router_b': jnp.zeros((E,), jnp.float32), 'w1': jax.random.normal(ks[2], (E, D, H), jnp.float32) / np.sqrt(D), 'b1': jnp.zeros((E, H), jnp.float32), 'w2': jax.random.normal(ks[3], (E, H, D), jnp.float32) / np.sqrt(H), 'b2': jnp.zeros((E, D), jnp.float32)}
    _L2_ffn_in = _L2_ffn_setup()

    def _L3_attn_setup():
        import jax, jax.numpy as jnp
        import numpy as np
        DIM = 128
        H = 16
        DH = DIM // H
        K = 4
        B = 8
        N = 256
        EPS = 1e-06

        def _depthwise_conv_silu(x, w, n):
            pad = K // 2
            y = jax.lax.conv_general_dilated(x.transpose(0, 2, 1), w, window_strides=(1,), padding=[(pad, pad)], dimension_numbers=('NCH', 'OIH', 'NCH'), feature_group_count=x.shape[-1])
            y = y[..., :n]
            return jax.nn.silu(y).transpose(0, 2, 1)

        def _l2norm(x):
            return x / (jnp.linalg.norm(x, axis=-1, keepdims=True) + EPS)

        def _forward(x, Wq, bq, Wk, bk, Wv, bv, Wa, ba, Wb, bb, conv_q, conv_k, conv_v, Wo, bo):
            b_, n_, c_ = x.shape
            q = _l2norm(_depthwise_conv_silu(jax.nn.silu(x @ Wq.T + bq), conv_q, n_))
            k = _l2norm(_depthwise_conv_silu(jax.nn.silu(x @ Wk.T + bk), conv_k, n_))
            v = _depthwise_conv_silu(jax.nn.silu(x @ Wv.T + bv), conv_v, n_)
            a = jax.nn.sigmoid(x @ Wa.T + ba)
            bgate = jax.nn.sigmoid(x @ Wb.T + bb)
            q = q.reshape(b_, n_, H, DH).transpose(1, 0, 2, 3)
            k = k.reshape(b_, n_, H, DH).transpose(1, 0, 2, 3)
            v = v.reshape(b_, n_, H, DH).transpose(1, 0, 2, 3)
            a = a.transpose(1, 0, 2)
            bgate = bgate.transpose(1, 0, 2)
            S0 = jnp.zeros((b_, H, DH, DH), x.dtype)

            def step(S, inp):
                qt, kt, vt, at, bt = inp
                at = at[..., None, None]
                bt = bt[..., None, None]
                Sk = jnp.einsum('bhde,bhe->bhd', S, kt)
                outer_Sk_k = Sk[..., :, None] * kt[..., None, :]
                outer_v_k = vt[..., :, None] * kt[..., None, :]
                S_new = at * S - at * bt * outer_Sk_k + bt * outer_v_k
                ot = jnp.einsum('bhd,bhde->bhe', qt, S_new)
                return (S_new, ot)
            _, O = jax.lax.scan(step, S0, (q, k, v, a, bgate))
            O = O.transpose(1, 0, 2, 3).reshape(b_, n_, c_)
            return O @ Wo.T + bo
        key = jax.random.key(seed)
        ks = jax.random.split(key, 16)
        s = 1.0 / np.sqrt(DIM)
        d = dict(x=jax.random.normal(ks[0], (B, N, DIM), jnp.float32), Wq=jax.random.normal(ks[1], (DIM, DIM), jnp.float32) * s, bq=jnp.zeros((DIM,), jnp.float32), Wk=jax.random.normal(ks[2], (DIM, DIM), jnp.float32) * s, bk=jnp.zeros((DIM,), jnp.float32), Wv=jax.random.normal(ks[3], (DIM, DIM), jnp.float32) * s, bv=jnp.zeros((DIM,), jnp.float32), Wa=jax.random.normal(ks[4], (H, DIM), jnp.float32) * s, ba=jnp.zeros((H,), jnp.float32), Wb=jax.random.normal(ks[5], (H, DIM), jnp.float32) * s, bb=jnp.zeros((H,), jnp.float32), conv_q=jax.random.normal(ks[6], (DIM, 1, K), jnp.float32) * 0.5, conv_k=jax.random.normal(ks[7], (DIM, 1, K), jnp.float32) * 0.5, conv_v=jax.random.normal(ks[8], (DIM, 1, K), jnp.float32) * 0.5, Wo=jax.random.normal(ks[9], (DIM, DIM), jnp.float32) * s, bo=jnp.zeros((DIM,), jnp.float32))
        return d
    _L3_attn_in = _L3_attn_setup()

    def _L3_ffn_setup():
        import jax, jax.numpy as jnp
        import numpy as np
        B, S, D, E, H, K = (4, 256, 128, 8, 64, 2)
        key = jax.random.key(seed)
        ks = jax.random.split(key, 11)
        sc = 0.02
        return {'x': jax.random.normal(ks[0], (B, S, D), dtype=jnp.float32), 'gate_W': jax.random.normal(ks[1], (D, E), dtype=jnp.float32) * sc, 'W1': jax.random.normal(ks[2], (E, D, H), dtype=jnp.float32) * sc, 'b1': jnp.zeros((E, H), dtype=jnp.float32), 'W2': jax.random.normal(ks[3], (E, H, D), dtype=jnp.float32) * sc, 'b2': jnp.zeros((E, D), dtype=jnp.float32), 'Ws1': jax.random.normal(ks[4], (D, H), dtype=jnp.float32) * sc, 'bs1': jnp.zeros((H,), dtype=jnp.float32), 'Ws2': jax.random.normal(ks[5], (H, D), dtype=jnp.float32) * sc, 'bs2': jnp.zeros((D,), dtype=jnp.float32), 'route_scale': jnp.ones((), dtype=jnp.float32)}
    _L3_ffn_in = _L3_ffn_setup()
    _d = {'L0_attn_x': _L0_attn_in['x'], 'L0_attn_w_down_q': _L0_attn_in['w_down_q'], 'L0_attn_w_down_kv': _L0_attn_in['w_down_kv'], 'L0_attn_w_up_q': _L0_attn_in['w_up_q'], 'L0_attn_w_up_k': _L0_attn_in['w_up_k'], 'L0_attn_w_up_v': _L0_attn_in['w_up_v'], 'L0_attn_w_out': _L0_attn_in['w_out'], 'L0_attn_ln_scale': _L0_attn_in['ln_scale'], 'L0_attn_ln_bias': _L0_attn_in['ln_bias'], 'L0_ffn_norm_scale': _L0_ffn_in['norm_scale'], 'L0_ffn_w_router': _L0_ffn_in['w_router'], 'L0_ffn_w_up': _L0_ffn_in['w_up'], 'L0_ffn_w_down': _L0_ffn_in['w_down'], 'L1_attn_Wq': _L1_attn_in['Wq'], 'L1_attn_bq': _L1_attn_in['bq'], 'L1_attn_Wk': _L1_attn_in['Wk'], 'L1_attn_bk': _L1_attn_in['bk'], 'L1_attn_Wv': _L1_attn_in['Wv'], 'L1_attn_bv': _L1_attn_in['bv'], 'L1_attn_Wo': _L1_attn_in['Wo'], 'L1_attn_bo': _L1_attn_in['bo'], 'L1_ffn_centroids': _L1_ffn_in['centroids'], 'L1_ffn_routing_bias': _L1_ffn_in['routing_bias'], 'L1_ffn_Wfc_r': _L1_ffn_in['Wfc_r'], 'L1_ffn_Wproj_r': _L1_ffn_in['Wproj_r'], 'L1_ffn_Wfc_sh': _L1_ffn_in['Wfc_sh'], 'L1_ffn_Wproj_sh': _L1_ffn_in['Wproj_sh'], 'L2_attn_Wq': _L2_attn_in['Wq'], 'L2_attn_Wk': _L2_attn_in['Wk'], 'L2_attn_Wv': _L2_attn_in['Wv'], 'L2_attn_Wo': _L2_attn_in['Wo'], 'L2_attn_Wg': _L2_attn_in['Wg'], 'L2_attn_bg': _L2_attn_in['bg'], 'L2_ffn_router_w': _L2_ffn_in['router_w'], 'L2_ffn_router_b': _L2_ffn_in['router_b'], 'L2_ffn_w1': _L2_ffn_in['w1'], 'L2_ffn_b1': _L2_ffn_in['b1'], 'L2_ffn_w2': _L2_ffn_in['w2'], 'L2_ffn_b2': _L2_ffn_in['b2'], 'L3_attn_Wq': _L3_attn_in['Wq'], 'L3_attn_bq': _L3_attn_in['bq'], 'L3_attn_Wk': _L3_attn_in['Wk'], 'L3_attn_bk': _L3_attn_in['bk'], 'L3_attn_Wv': _L3_attn_in['Wv'], 'L3_attn_bv': _L3_attn_in['bv'], 'L3_attn_Wa': _L3_attn_in['Wa'], 'L3_attn_ba': _L3_attn_in['ba'], 'L3_attn_Wb': _L3_attn_in['Wb'], 'L3_attn_bb': _L3_attn_in['bb'], 'L3_attn_conv_q': _L3_attn_in['conv_q'], 'L3_attn_conv_k': _L3_attn_in['conv_k'], 'L3_attn_conv_v': _L3_attn_in['conv_v'], 'L3_attn_Wo': _L3_attn_in['Wo'], 'L3_attn_bo': _L3_attn_in['bo'], 'L3_ffn_gate_W': _L3_ffn_in['gate_W'], 'L3_ffn_W1': _L3_ffn_in['W1'], 'L3_ffn_b1': _L3_ffn_in['b1'], 'L3_ffn_W2': _L3_ffn_in['W2'], 'L3_ffn_b2': _L3_ffn_in['b2'], 'L3_ffn_Ws1': _L3_ffn_in['Ws1'], 'L3_ffn_bs1': _L3_ffn_in['bs1'], 'L3_ffn_Ws2': _L3_ffn_in['Ws2'], 'L3_ffn_bs2': _L3_ffn_in['bs2'], 'L3_ffn_route_scale': _L3_ffn_in['route_scale']}
    _x0 = _d['L0_attn_x']
    _d['L0_attn_x'] = jax.random.normal(jax.random.fold_in(jax.random.key(seed), 1), (16, 256, 128), dtype=_x0.dtype)
    del _x0
    return _d

def reference(L0_attn_x, L0_attn_w_down_q, L0_attn_w_down_kv, L0_attn_w_up_q, L0_attn_w_up_k, L0_attn_w_up_v, L0_attn_w_out, L0_attn_ln_scale, L0_attn_ln_bias, L0_ffn_norm_scale, L0_ffn_w_router, L0_ffn_w_up, L0_ffn_w_down, L1_attn_Wq, L1_attn_bq, L1_attn_Wk, L1_attn_bk, L1_attn_Wv, L1_attn_bv, L1_attn_Wo, L1_attn_bo, L1_ffn_centroids, L1_ffn_routing_bias, L1_ffn_Wfc_r, L1_ffn_Wproj_r, L1_ffn_Wfc_sh, L1_ffn_Wproj_sh, L2_attn_Wq, L2_attn_Wk, L2_attn_Wv, L2_attn_Wo, L2_attn_Wg, L2_attn_bg, L2_ffn_router_w, L2_ffn_router_b, L2_ffn_w1, L2_ffn_b1, L2_ffn_w2, L2_ffn_b2, L3_attn_Wq, L3_attn_bq, L3_attn_Wk, L3_attn_bk, L3_attn_Wv, L3_attn_bv, L3_attn_Wa, L3_attn_ba, L3_attn_Wb, L3_attn_bb, L3_attn_conv_q, L3_attn_conv_k, L3_attn_conv_v, L3_attn_Wo, L3_attn_bo, L3_ffn_gate_W, L3_ffn_W1, L3_ffn_b1, L3_ffn_W2, L3_ffn_b2, L3_ffn_Ws1, L3_ffn_bs1, L3_ffn_Ws2, L3_ffn_bs2, L3_ffn_route_scale):

    def _L0_attn_ref(x, w_down_q, w_down_kv, w_up_q, w_up_k, w_up_v, w_out, ln_scale, ln_bias):
        import jax, jax.numpy as jnp
        import numpy as np
        B, S, D = (2, 256, 128)
        H, DH = (16, 64)
        DQL, DKVL = (64, 64)
        DR = 64
        TOPK = 64
        LN_EPS = 1e-05
        ROPE_BASE = 10000.0

        def _rope_tables(seq_len, dim):
            inv_freq = 1.0 / ROPE_BASE ** (np.arange(0, dim, 2, dtype=np.float32) / dim)
            t = np.arange(seq_len, dtype=np.float32)
            freqs = np.outer(t, inv_freq)
            cos = np.concatenate([np.cos(freqs), np.cos(freqs)], -1)[:, ::2]
            sin = np.concatenate([np.sin(freqs), np.sin(freqs)], -1)[:, ::2]
            return (jnp.asarray(cos), jnp.asarray(sin))

        def _apply_rope_subspace(x, d_rope):
            s = x.shape[-2]
            cos, sin = _rope_tables(s, d_rope)
            xr, xp = (x[..., :d_rope], x[..., d_rope:])
            e, o = (xr[..., 0::2], xr[..., 1::2])
            rot = jnp.stack([e * cos - o * sin, e * sin + o * cos], axis=-1).reshape(xr.shape)
            return jnp.concatenate([rot, xp], axis=-1)

        def _reference_tuple_inner(x, w_down_q, w_down_kv, w_up_q, w_up_k, w_up_v, w_out, ln_scale, ln_bias):
            b, s, d = x.shape
            residual = x
            mu = jnp.mean(x, axis=-1, keepdims=True)
            var = jnp.mean((x - mu) ** 2, axis=-1, keepdims=True)
            h = (x - mu) * jax.lax.rsqrt(var + LN_EPS) * ln_scale + ln_bias
            c_q = h @ w_down_q.T
            c_kv = h @ w_down_kv.T
            q = (c_q @ w_up_q.T).reshape(b, s, H, DH).transpose(0, 2, 1, 3)
            k = (c_kv @ w_up_k.T).reshape(b, s, H, DH).transpose(0, 2, 1, 3)
            v = (c_kv @ w_up_v.T).reshape(b, s, H, DH).transpose(0, 2, 1, 3)
            q = _apply_rope_subspace(q, DR)
            k = _apply_rope_subspace(k, DR)
            scale = 1.0 / np.sqrt(DH).astype(np.float32)
            scores = jnp.einsum('bhqd,bhkd->bhqk', q, k) * scale
            _, indices = jax.lax.top_k(scores, min(TOPK, s))
            attn = jax.nn.softmax(scores, axis=-1)
            out = jnp.einsum('bhqk,bhkd->bhqd', attn, v)
            out = out.transpose(0, 2, 1, 3).reshape(b, s, H * DH)
            out = out @ w_out.T + residual
            return (out, indices.astype(jnp.int64))
        return _reference_tuple_inner(x, w_down_q, w_down_kv, w_up_q, w_up_k, w_up_v, w_out, ln_scale, ln_bias)[0]

    def _L0_ffn_ref(x, norm_scale, w_router, w_up, w_down):
        import jax, jax.numpy as jnp
        import numpy as np
        DIM = 128
        HIDDEN = 256
        N_EXPERTS = 8
        TOP_K = 2
        EPS = 1e-06

        def rms_norm(x, scale, eps=EPS):
            ms = jnp.mean(jnp.square(x.astype(jnp.float32)), axis=-1, keepdims=True)
            s = scale.astype(jnp.float32) * jax.lax.rsqrt(ms + eps)
            return x * s.astype(x.dtype)

        def moe_linear(xf, ids, W):
            E = W.shape[0]
            out = jnp.zeros((xf.shape[0], W.shape[1]), dtype=xf.dtype)
            for e in range(E):
                out = out + jnp.where((ids == e)[:, None], xf @ W[e].T, 0.0)
            return out
        B, S, D = x.shape
        skip = x
        xn = rms_norm(x, norm_scale)
        scores = (xn @ w_router.T).astype(jnp.float32)
        scores_topk, idx = jax.lax.top_k(scores, TOP_K)
        weights = jax.nn.softmax(scores_topk, axis=-1)
        xf = jnp.broadcast_to(xn[..., None, :], (B, S, TOP_K, D)).reshape(-1, D)
        ids = idx.reshape(-1)
        up = moe_linear(xf, ids, w_up)
        u, gate = jnp.split(up, 2, axis=-1)
        h = u * jax.nn.silu(gate)
        down = moe_linear(h, ids, w_down)
        down = down.reshape(B, S, TOP_K, D)
        out = jnp.sum(down * weights[..., None].astype(down.dtype), axis=-2)
        return out + skip

    def _L1_attn_ref(x, Wq, bq, Wk, bk, Wv, bv, Wo, bo):
        import jax, jax.numpy as jnp
        import numpy as np
        B, S, D = (4, 512, 128)
        H = 16
        HD = D // H

        def feature_map(x):
            return jnp.exp(-jnp.square(x) * 0.5)
        b, s, _ = x.shape
        q = feature_map((x @ Wq + bq).reshape(b, s, H, HD))
        k = feature_map((x @ Wk + bk).reshape(b, s, H, HD))
        v = (x @ Wv + bv).reshape(b, s, H, HD)
        coeff = jnp.sum(q * k, axis=-1, keepdims=True)
        qkv = coeff * v
        out = qkv.reshape(b, s, H * HD)
        return out @ Wo + bo

    def _L1_ffn_ref(x, centroids, routing_bias, Wfc_r, Wproj_r, Wfc_sh, Wproj_sh):
        import jax, jax.numpy as jnp
        import numpy as np
        D = 128
        F = 4 * D
        E = 8
        NS = 2
        TOP_K = 2
        B, S = (2, 128)
        raw = jnp.einsum('bsd,ed->bse', x, centroids)
        routing_scores = jax.nn.sigmoid(raw)
        balanced = jax.nn.sigmoid(raw + routing_bias)
        _, top_idx = jax.lax.top_k(balanced, TOP_K)
        gathered = jnp.take_along_axis(routing_scores, top_idx, axis=-1)
        top_w = jax.nn.softmax(gathered, axis=-1)
        combine = jnp.sum(jax.nn.one_hot(top_idx, E, dtype=x.dtype) * top_w[..., None], axis=-2)
        h_sh = jax.nn.gelu(jnp.einsum('bsd,nfd->bsnf', x, Wfc_sh), approximate=False)
        shared_out = jnp.einsum('bsnf,ndf->bsd', h_sh, Wproj_sh)
        h_r = jax.nn.gelu(jnp.einsum('bsd,efd->bsef', x, Wfc_r), approximate=False)
        expert_out = jnp.einsum('bsef,edf->bsed', h_r, Wproj_r)
        routed_out = jnp.einsum('bsed,bse->bsd', expert_out, combine)
        return x + shared_out + routed_out

    def _L2_attn_ref(x, Wq, Wk, Wv, Wo, Wg, bg):
        import jax, jax.numpy as jnp
        import numpy as np
        D_MODEL = 128
        N_HEADS = 16
        D_HEAD = D_MODEL // N_HEADS
        SCALE = 1.0 / np.sqrt(D_HEAD).astype(np.float32)

        def _feature_map(x):
            return jax.nn.elu(x) + 1.0
        b, s, _ = x.shape
        q = (x @ Wq.T).reshape(b, s, N_HEADS, D_HEAD)
        k = (x @ Wk.T).reshape(b, s, N_HEADS, D_HEAD)
        v = (x @ Wv.T).reshape(b, s, N_HEADS, D_HEAD)
        q = _feature_map(q * SCALE)
        k = _feature_map(k)
        gate = jax.nn.sigmoid(x @ Wg.T + bg)
        qt = jnp.moveaxis(q, 1, 0)
        kt = jnp.moveaxis(k, 1, 0)
        vt = jnp.moveaxis(v, 1, 0)
        gt = jnp.moveaxis(gate, 1, 0)
        S0 = jnp.zeros((b, N_HEADS, D_HEAD, D_HEAD), dtype=x.dtype)

        def step(S, inp):
            q_t, k_t, v_t, g_t = inp
            S = g_t[:, :, None, None] * S + k_t[..., :, None] * v_t[..., None, :]
            y_t = jnp.einsum('bhi,bhij->bhj', q_t, S)
            return (S, y_t)
        _, ys = jax.lax.scan(step, S0, (qt, kt, vt, gt))
        y = jnp.moveaxis(ys, 0, 1).reshape(b, s, D_MODEL)
        return y @ Wo.T

    def _L2_ffn_ref(inputs, router_w, router_b, w1, b1, w2, b2):
        import jax, jax.numpy as jnp
        import numpy as np
        B, S, D, E, H, K = (4, 256, 128, 8, 128, 2)
        CAPACITY_FACTOR = 1.25
        MIN_CAPACITY = 4
        b, s, d = inputs.shape
        n = b * s
        flat = inputs.reshape(n, d)
        logits = flat @ router_w + router_b
        probs = jax.nn.softmax(logits, axis=-1)
        top_p, top_i = jax.lax.top_k(probs, K)
        top_p = top_p / jnp.sum(top_p, axis=-1, keepdims=True)
        expert_capacity = max(int(n * CAPACITY_FACTOR / E), MIN_CAPACITY)
        rows = jnp.arange(n)[:, None]
        mask = jnp.zeros((n, E), inputs.dtype).at[rows, top_i].set(top_p)
        mask = mask.at[top_i, jnp.arange(K)[None, :]].add(top_p)
        mask = jnp.minimum(mask, expert_capacity)
        xin = mask[:, :, None] * flat[:, None, :]
        h = jax.nn.gelu(jnp.einsum('ned,edh->neh', xin, w1) + b1, approximate=False)
        out = jnp.einsum('neh,ehd->ned', h, w2) + b2
        final = jnp.einsum('ne,ned->nd', mask, out)
        return final.reshape(b, s, d)

    def _L3_attn_ref(x, Wq, bq, Wk, bk, Wv, bv, Wa, ba, Wb, bb, conv_q, conv_k, conv_v, Wo, bo):
        import jax, jax.numpy as jnp
        import numpy as np
        DIM = 128
        H = 16
        DH = DIM // H
        K = 4
        B = 8
        N = 256
        EPS = 1e-06

        def _depthwise_conv_silu(x, w, n):
            pad = K // 2
            y = jax.lax.conv_general_dilated(x.transpose(0, 2, 1), w, window_strides=(1,), padding=[(pad, pad)], dimension_numbers=('NCH', 'OIH', 'NCH'), feature_group_count=x.shape[-1])
            y = y[..., :n]
            return jax.nn.silu(y).transpose(0, 2, 1)

        def _l2norm(x):
            return x / (jnp.linalg.norm(x, axis=-1, keepdims=True) + EPS)

        def _forward(x, Wq, bq, Wk, bk, Wv, bv, Wa, ba, Wb, bb, conv_q, conv_k, conv_v, Wo, bo):
            b_, n_, c_ = x.shape
            q = _l2norm(_depthwise_conv_silu(jax.nn.silu(x @ Wq.T + bq), conv_q, n_))
            k = _l2norm(_depthwise_conv_silu(jax.nn.silu(x @ Wk.T + bk), conv_k, n_))
            v = _depthwise_conv_silu(jax.nn.silu(x @ Wv.T + bv), conv_v, n_)
            a = jax.nn.sigmoid(x @ Wa.T + ba)
            bgate = jax.nn.sigmoid(x @ Wb.T + bb)
            q = q.reshape(b_, n_, H, DH).transpose(1, 0, 2, 3)
            k = k.reshape(b_, n_, H, DH).transpose(1, 0, 2, 3)
            v = v.reshape(b_, n_, H, DH).transpose(1, 0, 2, 3)
            a = a.transpose(1, 0, 2)
            bgate = bgate.transpose(1, 0, 2)
            S0 = jnp.zeros((b_, H, DH, DH), x.dtype)

            def step(S, inp):
                qt, kt, vt, at, bt = inp
                at = at[..., None, None]
                bt = bt[..., None, None]
                Sk = jnp.einsum('bhde,bhe->bhd', S, kt)
                outer_Sk_k = Sk[..., :, None] * kt[..., None, :]
                outer_v_k = vt[..., :, None] * kt[..., None, :]
                S_new = at * S - at * bt * outer_Sk_k + bt * outer_v_k
                ot = jnp.einsum('bhd,bhde->bhe', qt, S_new)
                return (S_new, ot)
            _, O = jax.lax.scan(step, S0, (q, k, v, a, bgate))
            O = O.transpose(1, 0, 2, 3).reshape(b_, n_, c_)
            return O @ Wo.T + bo
        return _forward(x, Wq, bq, Wk, bk, Wv, bv, Wa, ba, Wb, bb, conv_q, conv_k, conv_v, Wo, bo)

    def _L3_ffn_ref(x, gate_W, W1, b1, W2, b2, Ws1, bs1, Ws2, bs2, route_scale):
        import jax, jax.numpy as jnp
        import numpy as np
        B, S, D, E, H, K = (4, 256, 128, 8, 64, 2)
        scores = jax.nn.sigmoid(x @ gate_W) * route_scale
        topk_scores, topk_idx = jax.lax.top_k(scores, K)
        topk_w = topk_scores / topk_scores.sum(-1, keepdims=True)
        onehot = jax.nn.one_hot(topk_idx, E, dtype=x.dtype)
        gate_full = jnp.einsum('bsk,bske->bse', topk_w, onehot)
        h = jax.nn.gelu(jnp.einsum('bsd,edh->bseh', x, W1) + b1, approximate=False)
        y = jnp.einsum('bseh,ehd->bsed', h, W2) + b2
        expert_out = jnp.einsum('bse,bsed->bsd', gate_full, y)
        shared = jax.nn.gelu(x @ Ws1 + bs1, approximate=False) @ Ws2 + bs2
        return expert_out + shared
    x = L0_attn_x
    x = _layernorm(x + _L0_attn_ref(x, L0_attn_w_down_q, L0_attn_w_down_kv, L0_attn_w_up_q, L0_attn_w_up_k, L0_attn_w_up_v, L0_attn_w_out, L0_attn_ln_scale, L0_attn_ln_bias), axis=-1)
    x = _layernorm(x + _L0_ffn_ref(x, L0_ffn_norm_scale, L0_ffn_w_router, L0_ffn_w_up, L0_ffn_w_down), axis=-1)
    x = _layernorm(x + _L1_attn_ref(x, L1_attn_Wq, L1_attn_bq, L1_attn_Wk, L1_attn_bk, L1_attn_Wv, L1_attn_bv, L1_attn_Wo, L1_attn_bo), axis=-1)
    x = _layernorm(x + _L1_ffn_ref(x, L1_ffn_centroids, L1_ffn_routing_bias, L1_ffn_Wfc_r, L1_ffn_Wproj_r, L1_ffn_Wfc_sh, L1_ffn_Wproj_sh), axis=-1)
    x = _layernorm(x + _L2_attn_ref(x, L2_attn_Wq, L2_attn_Wk, L2_attn_Wv, L2_attn_Wo, L2_attn_Wg, L2_attn_bg), axis=-1)
    x = _layernorm(x + _L2_ffn_ref(x, L2_ffn_router_w, L2_ffn_router_b, L2_ffn_w1, L2_ffn_b1, L2_ffn_w2, L2_ffn_b2), axis=-1)
    x = _layernorm(x + _L3_attn_ref(x, L3_attn_Wq, L3_attn_bq, L3_attn_Wk, L3_attn_bk, L3_attn_Wv, L3_attn_bv, L3_attn_Wa, L3_attn_ba, L3_attn_Wb, L3_attn_bb, L3_attn_conv_q, L3_attn_conv_k, L3_attn_conv_v, L3_attn_Wo, L3_attn_bo), axis=-1)
    x = _layernorm(x + _L3_ffn_ref(x, L3_ffn_gate_W, L3_ffn_W1, L3_ffn_b1, L3_ffn_W2, L3_ffn_b2, L3_ffn_Ws1, L3_ffn_bs1, L3_ffn_Ws2, L3_ffn_bs2, L3_ffn_route_scale), axis=-1)
    return x

_drawn_inputs = setup_inputs


def setup_inputs(seed=0):
    import zlib

    import numpy as np

    out = dict(_drawn_inputs(seed))
    spreads = {'L0_attn_ln_scale': (1.0, 0.6),
     'L0_attn_ln_bias': (0.0, 0.785),
     'L0_ffn_norm_scale': (1.0, 0.2),
     'L1_ffn_routing_bias': (0.0, 0.1),
     'L2_ffn_router_b': (0.0, 0.1),
     'L2_ffn_b1': (0.0, 0.1),
     'L2_ffn_b2': (0.0, 0.1),
     'L3_attn_bq': (0.0, 0.8),
     'L3_attn_bk': (0.0, 0.8),
     'L3_attn_bv': (0.0, 0.8),
     'L3_attn_ba': (0.0, 0.8),
     'L3_attn_bb': (0.0, 0.8),
     'L3_attn_bo': (0.0, 0.1),
     'L3_ffn_b1': (0.0, 0.8),
     'L3_ffn_b2': (0.0, 0.1),
     'L3_ffn_bs1': (0.0, 0.8),
     'L3_ffn_bs2': (0.0, 0.1)}
    factors = {'L0_attn_w_down_q': 8.0,
     'L0_attn_w_down_kv': 5.339,
     'L0_attn_w_up_q': 8.0,
     'L0_attn_w_up_k': 8.0,
     'L0_attn_w_up_v': 5.105,
     'L0_attn_w_out': 4.269,
     'L2_attn_bg': 4.282,
     'L3_attn_Wq': 8.0,
     'L3_attn_Wk': 8.0,
     'L3_attn_Wv': 8.0,
     'L3_attn_Wa': 8.0,
     'L3_attn_Wb': 8.0,
     'L3_attn_conv_q': 8.0,
     'L3_attn_conv_k': 7.582,
     'L3_attn_conv_v': 7.836,
     'L3_attn_Wo': 7.052,
     'L3_ffn_W1': 4.283,
     'L3_ffn_W2': 3.819,
     'L3_ffn_Ws1': 2.913,
     'L3_ffn_Ws2': 2.727}
    for name, (base, spread) in spreads.items():
        noise = np.random.default_rng([zlib.crc32(name.encode()), seed]).standard_normal(out[name].shape)
        drawn = base * np.exp(spread * noise) if base else spread * noise
        out[name] = jnp.asarray(drawn.astype(out[name].dtype))
    for name, factor in factors.items():
        out[name] = (out[name] * factor).astype(out[name].dtype)
    return out
```

```python
from contextlib import ExitStack

import concourse.bass as bass
from concourse import mybir
from concourse.alu_op_type import AluOpType as ALU

F32 = mybir.dt.float32
U32 = mybir.dt.uint32
ACT = mybir.ActivationFunctionType
AX_X = mybir.AxisListType.X

P = 128
D = 128
SEQS, SEQ = 16, 256
TOK = SEQS * SEQ
BLK = 512
TPB = BLK // P
NBLK = TOK // BLK
SPB = BLK // SEQ
E = 8
HEADS0, DH0, RANK0 = 16, 64, 64
PAIRS = HEADS0 // 2
UNITS = PAIRS * 2 * SPB
DH = 8
CH0 = 4
CH1 = 4
NSH = 2
CAP = max(int(TOK * 1.25 / E), 4)
STEPS = 8
CPT = 2
TURNS = SEQ // (STEPS * CPT)
NSTEP = STEPS * CPT
LN_EPS = 1e-5
RMS_EPS = 1e-6
L2_EPS = 1e-6
NEG = -1.0e30


VPER1, VPER2, VPER3, VPER4 = 280, 52, 48, 45
PPER1, PPER2, PPER4 = 7, 2, 2


class Count:

    def __init__(self, sem, per=1):
        self.sem, self.per = sem, per

    def at(self, turn, n=0):
        return turn * self.per + (n + 1)


class Steps:

    def __init__(self, eng, sem, turn, per):
        self.eng, self.sem, self.turn, self.per, self.n = eng, sem, turn, per, 0

    def do(self, instruction):
        instruction.then_inc(self.sem, 1)
        self.n += 1

    def sync(self):
        self.eng.wait_ge(self.sem, self.turn * self.per + self.n)

    def end(self):
        assert self.n == self.per, (self.n, self.per)


def build(nc, t, out):
    with ExitStack() as ctx:
        def sb(name, shape, dt=F32):
            return ctx.enter_context(nc.sbuf_tensor(name, shape, dt))

        def sem(name):
            return ctx.enter_context(nc.semaphore(name))

        ident = sb("ident", [P, P])
        rope_sin = sb("rope_sin", [P, SEQ])
        head_ones = sb("head_ones", [P, P])
        iota8 = sb("iota8", [P, E])
        sel_pair = sb("sel_pair", [E, E // 2, P])
        cols = sb("cols", [P, 24])
        wd0 = sb("wd0", [P, P])
        big1 = sb("big1", [P, CPT * STEPS * SEQS * (DH + 1)])
        wup0 = big1[:, 0:HEADS0 * DH0]
        vo0 = big1[:, HEADS0 * DH0:2 * HEADS0 * DH0].rearrange("p (a m) -> p a m", a=PAIRS)
        rope_cos = big1[:, 2 * HEADS0 * DH0:2 * HEADS0 * DH0 + SEQ]
        gated_keys = [big1[:, h * STEPS * SEQS * (DH + 1):(h + 1) * STEPS * SEQS * (DH + 1)]
                      .rearrange("p (t b e) -> p t b e", t=STEPS, b=SEQS) for h in range(CPT)]
        wr0 = sb("wr0", [P, E])
        big0 = sb("big0", [P, 5 * TOK])
        up0 = big0[:, 0:E * CH0 * P].rearrange("p (e c m) -> p e c m", e=E, c=CH0)
        o = E * CH0 * P
        dn0 = big0[:, o:o + E * 2 * P].rearrange("p (e c m) -> p e c m", e=E, c=2)
        o += E * 2 * P
        NE1 = E + NSH
        up1 = big0[:, o:o + NE1 * CH1 * P].rearrange("p (e c m) -> p e c m", e=NE1, c=CH1)
        o += NE1 * CH1 * P
        dn1 = big0[:, o:o + NE1 * CH1 * P].rearrange("p (e c m) -> p e c m", e=NE1, c=CH1)
        o += NE1 * CH1 * P
        assert o <= 5 * TOK
        hist = [big0[:, n * TOK:(n + 1) * TOK] for n in range(5)]
        w1a = sb("w1a", [P, 4, P])
        bo1 = sb("bo1", [P, P])
        wr1 = sb("wr1", [P, E])
        rb1 = sb("rb1", [P, E])
        w2a = sb("w2a", [P, 2, P])
        wv2 = sb("wv2", [P, DH, P])
        wg2 = sb("wg2", [P, P])
        wo2 = sb("wo2", [P, DH, P])
        wr2 = sb("wr2", [P, E])
        rb2 = sb("rb2", [P, E])
        up2 = sb("up2", [P, E, P])
        dn2 = sb("dn2", [P, E, P])
        b1_2 = sb("b1_2", [P, E])
        b2_2 = sb("b2_2", [E, P])
        w3a = sb("w3a", [P, 3, P])
        wab3 = sb("wab3", [P, 2, P])
        conv3 = sb("conv3", [P, 3, 4])
        wo3 = sb("wo3", [P, DH, P])
        wr3 = sb("wr3", [P, E])
        up3 = sb("up3", [P, E // 2, P])
        dn3 = sb("dn3", [P, E // 2, P])
        b1_3 = sb("b1_3", [P, E // 2])
        b2_3 = sb("b2_3", [E + 1, P])
        ws1_3 = sb("ws1_3", [P, 64])
        ws2_3 = sb("ws2_3", [64, P])
        sel_e = sb("sel_e", [P, DH, P])

        LNS, LNB, RMSW, BQ1, BK1, BV1, BG2, BQ3, BK3, BV3, BA3, BB3, BO3, BS3, RS3 = range(15)

        def col(n):
            return cols[:, n:n + 1]

        x_tok = sb("x_tok", [P, TPB, P])
        x_new = sb("x_new", [P, TPB, P])
        x_t = sb("x_t", [P, BLK])
        x_in = sb("x_in", [P, TPB, P])
        x_out = sb("x_out", [P, TPB, P])
        keep = sb("keep", [P, TOK // P, P])
        gate2 = sb("gate2", [P, TOK // P, E])
        stats = sb("stats", [P, TPB, 6])
        mv = sb("mv", [P, TPB, 2])
        vare = sb("vare", [P, TPB])
        rstd = sb("rstd", [P, TPB])
        eps_ln = sb("eps_ln", [P, TPB])
        eps_rms = sb("eps_rms", [P, TPB])
        mhalf = sb("mhalf", [P, 8])
        phalf = sb("phalf", [P, 8])
        ones = sb("ones", [P, 1])
        gate_scratch = sb("gate_scratch", [P, 1])
        score = sb("score", [P, TPB, E])
        score_r = sb("score_r", [P, TPB, E])
        top8 = sb("top8", [P, TPB, E])
        top8i = sb("top8i", [P, TPB, E], U32)
        top8f = sb("top8f", [P, TPB, 2])
        oh = sb("oh", [P, 2, TPB, E])
        ohs = sb("ohs", [P, 2, TPB, E])
        two = sb("two", [P, 2, TPB])
        dif = sb("dif", [P, TPB])
        wts = sb("wts", [P, 2, TPB])
        gates = sb("gates", [P, TPB, E])
        wides = [sb(f"wide{n}", [P, 2 * BLK]) for n in range(8)]
        room = [wides[n // 2][:, (n % 2) * BLK:(n % 2 + 1) * BLK] for n in range(16)]

        ps = [ctx.enter_context(nc.psum_tensor(f"ps{n}", [P, BLK], F32)) for n in range(8)]

        def tiles(ap):
            return ap.rearrange("p (t m) -> p t m", t=TPB)

        def halves(ap):
            return ap.rearrange("p (s q) -> p s q", s=2)

        loaded_x = Count(sem("loaded_x"))
        w_small = sem("w_small")
        w_l0 = sem("w_l0")
        w_l1 = sem("w_l1")
        w_late = sem("w_late")
        consts = sem("consts")
        vo_mm = sem("vo_mm")
        vo_done = sem("vo_done")
        x_taken = Count(sem("x_taken"))

        class Norms:
            def __init__(self, tag, calls, turned):
                self.var = Count(sem(tag + "_var"), calls)
                self.rstd = Count(sem(tag + "_rstd"), calls)
                self.x = Count(sem(tag + "_x"), calls)
                self.tr = Count(sem(tag + "_tr"), turned)
                self.xt = Count(sem(tag + "_xt"), turned)

        def norm_stats(dve, st, nm, i, c, src):
            for k in range(TPB):
                st.do(dve.bn_stats(stats[:, k, :], src[:, k, :]))
            st.sync()
            st.do(dve.memset(gate_scratch[:, :], 0.0))
            for k in range(TPB):
                last = dve.bn_aggr(mv[:, k, :], stats[:, k, :])
                if k < TPB - 1:
                    st.do(last)
                else:
                    last.then_inc(nm.var.sem, 1)

        def rms_stats(dve, st, nm, i, c, src, sq):
            for k in range(TPB):
                last = dve.tensor_tensor_reduce(out=sq[:, k, :], in0=src[:, k, :], in1=src[:, k, :],
                                                scale=1.0 / D, scalar=0.0, op0=ALU.mult, op1=ALU.add,
                                                accum_out=mv[:, k, 1:2])
                if k < TPB - 1:
                    st.do(last)
                else:
                    last.then_inc(nm.var.sem, 1)

        def norm_rstd(pool, st, nm, i, c, eps):
            pool.wait_ge(nm.var.sem, nm.var.at(i, c))
            st.do(pool.tensor_tensor(vare[:, :], mv[:, :, 1], eps[:, :], ALU.add))
            st.sync()
            pool.tensor_tensor(rstd[:, :], vare[:, :], mhalf[:, 0:TPB], ALU.pow).then_inc(nm.rstd.sem, 1)

        def norm_apply(dve, st, nm, i, c, src, dst, centre=True):
            dve.wait_ge(nm.var.sem, nm.var.at(i, c))
            dve.wait_ge(nm.rstd.sem, nm.rstd.at(i, c))
            for k in range(TPB):
                if centre:
                    last = dve.tensor_scalar(dst[:, k, :], src[:, k, :], mv[:, k, 0:1], rstd[:, k:k + 1],
                                             ALU.subtract, ALU.mult)
                else:
                    last = dve.tensor_scalar(dst[:, k, :], src[:, k, :], rstd[:, k:k + 1], None, ALU.mult)
                if k < TPB - 1:
                    st.do(last)
                else:
                    last.then_inc(nm.x.sem, 1)
            st.sync()
            dve.wait_ge(nm.x.sem, nm.x.at(i, c))

        def norm_transpose(pe, nm, i, c, r, src, bank):
            pe.wait_ge(nm.x.sem, nm.x.at(i, c))
            for k in range(TPB):
                last = pe.transpose(bank[:, k * P:(k + 1) * P], src[:, k, :], ident[:, :])
            last.then_inc(nm.tr.sem, 1)

        def norm_copy(act, nm, i, r, dst, bank, scale=None, bias=None):
            act.wait_ge(nm.tr.sem, nm.tr.at(i, r))
            if scale is None:
                last = act.activation(dst[:, :], bank[:, :], ACT.Copy)
            else:
                last = act.activation(dst[:, :], bank[:, :], ACT.Identity, scale=scale,
                                      bias=0.0 if bias is None else bias)
            last.then_inc(nm.xt.sem, 1)

        def router_mm(pe, src_t, w, bank, done):
            for k in range(TPB):
                last = pe.matmul(bank[:, k * E:(k + 1) * E], src_t[:, k * P:(k + 1) * P], w[:, :],
                                 start=True, stop=True)
            last.then_inc(done.sem, 1)

        def top_two(dve, st, src):
            st.sync()
            st.do(dve.memset(gate_scratch[:, :], 0.0))
            for k in range(TPB):
                st.do(dve.max(top8[:, k, :], src[:, k, :]))
            st.sync()
            st.do(dve.memset(gate_scratch[:, :], 0.0))
            for k in range(TPB):
                st.do(dve.max_index(top8i[:, k, :], top8[:, k, :], src[:, k, :]))
            st.sync()
            st.do(dve.tensor_copy(top8f[:, :, :], top8i[:, :, 0:2]))
            st.sync()
            for n in range(2):
                st.do(dve.tensor_tensor(oh[:, n, :, :], iota8[:, :].unsqueeze(1).to_broadcast([P, TPB, E]),
                                        top8f[:, :, n:n + 1].to_broadcast([P, TPB, E]), ALU.is_equal))

        def pick_two(dve, st, src):
            st.sync()
            for n in range(2):
                st.do(dve.tensor_tensor(ohs[:, n, :, :], oh[:, n, :, :], src[:, :, :], ALU.mult))
            st.sync()
            st.do(dve.tensor_reduce(two[:, :, :].rearrange("p n t -> p (n t)"),
                                    ohs[:, :, :, :].rearrange("p n t e -> p (n t) e"), AX_X, ALU.add))

        def soft_two(dve, st, first, second, done):
            st.sync()
            dve.tensor_tensor(dif[:, :], first, second, ALU.subtract).then_inc(done.sem, 1)

        def soft_act(act, i, dif_done, done):
            act.wait_ge(dif_done.sem, dif_done.at(i))
            act.activation(wts[:, 0, :], dif[:, :], ACT.Sigmoid)
            act.activation(wts[:, 1, :], dif[:, :], ACT.Sigmoid, scale=-1.0).then_inc(done.sem, 1)

        def gate_sum(dve, st, dst):
            for n in range(2):
                st.do(dve.tensor_tensor(ohs[:, n, :, :], oh[:, n, :, :],
                                        wts[:, n, :].unsqueeze(2).to_broadcast([P, TPB, E]), ALU.mult))
            st.sync()
            st.do(dve.tensor_tensor(dst, ohs[:, 0, :, :], ohs[:, 1, :, :], ALU.add))

        def gated_add(dve, st, y, gate, src, dst):
            st.sync()
            for k in range(TPB):
                last = dve.scalar_tensor_tensor(out=dst[:, k, :], in0=y[:, k * P:(k + 1) * P],
                                                scalar=gate[:, k, :], in1=src[:, k, :],
                                                op0=ALU.mult, op1=ALU.add)
                if k < TPB - 1:
                    st.do(last)
            return last

        n1 = Norms("n1", 7, 6)
        c_mm, c_cp = Count(sem("c_mm")), Count(sem("c_cp"))
        qk_mm = Count(sem("qk_mm"), 2 * PAIRS)
        qk_cp = Count(sem("qk_cp"), 2 * PAIRS)
        qk_cos = Count(sem("qk_cos"), 2 * PAIRS)
        qk_sin = Count(sem("qk_sin"), 2 * PAIRS)
        qk_rot = Count(sem("qk_rot"), 2 * PAIRS)
        sc_mm = Count(sem("sc_mm"), UNITS)
        sc_max = Count(sem("sc_max"), UNITS)
        pr_exp = Count(sem("pr_exp"), UNITS)
        pr_norm = Count(sem("pr_norm"), UNITS)
        pt_mm = Count(sem("pt_mm"), UNITS)
        pt_cp = Count(sem("pt_cp"), UNITS)
        pv_mm = Count(sem("pv_mm"), UNITS)
        ov_cp = Count(sem("ov_cp"), PAIRS)
        y0_mm = Count(sem("y0_mm"), PAIRS)
        r0_mm, d0, s0 = Count(sem("r0_mm")), Count(sem("d0")), Count(sem("s0"))
        up0_mm = Count(sem("up0_mm"), 2 * E)
        sl0 = Count(sem("sl0"), 2 * E)
        h0 = Count(sem("h0"), 2 * E)
        dn0_mm = Count(sem("dn0_mm"), E)
        acc0 = Count(sem("acc0"), E)
        qkv1_mm = Count(sem("qkv1_mm"), 3)
        qkv1_sq = Count(sem("qkv1_sq"), 2)
        qkv1_f = Count(sem("qkv1_f"), 3)
        qk1, co1_mm, ov1, y1_mm = Count(sem("qk1")), Count(sem("co1_mm")), Count(sem("ov1")), Count(sem("y1_mm"))
        r1_mm, rt1, rsig1 = Count(sem("r1_mm")), Count(sem("rt1")), Count(sem("rsig1"))
        d1, s1 = Count(sem("d1")), Count(sem("s1"))
        up1_mm = Count(sem("up1_mm"), CH1 * NE1)
        h1 = Count(sem("h1"), CH1 * NE1)
        dn1_mm = Count(sem("dn1_mm"), NE1)
        acc1 = Count(sem("acc1"), E + 1)
        qk2_mm = Count(sem("qk2_mm"), 3)
        qk2_cp = Count(sem("qk2_cp"), 3)
        qk2_min = Count(sem("qk2_min"), 2)
        qk2_exp = Count(sem("qk2_exp"), 2)
        qk2_f = Count(sem("qk2_f"), 2)
        v2_mm = Count(sem("v2_mm"), DH)
        kv2 = Count(sem("kv2"), DH)
        sc2 = Count(sem("sc2"), DH)
        qs2 = Count(sem("qs2"), DH)
        y2_mm = Count(sem("y2_mm"), DH)
        r2_mm, d2, s2 = Count(sem("r2_mm")), Count(sem("d2")), Count(sem("s2"))
        done1 = Count(sem("done1"))
        vstep, pstep = sem("vstep"), sem("pstep")
        
        h_t, c_t, ck = room[0], room[1], room[2]
        qa = [room[3], room[4]]
        cosm = [room[5], room[6]]
        rot = [[room[7], room[8]], [room[9], room[10]]]
        ex = [room[11], room[12]]
        pts = [room[13], room[14]]
        ovs = room[15]
        sinm, sinm2 = sb("sinm", [P, BLK]), sb("sinm2", [P, BLK])
        mx = sb("mx", [P, 4, 2])
        nmx = sb("nmx", [P, 4, 2])
        rsum = sb("rsum", [P, 4, 2])
        rinv = sb("rinv", [P, 4, 2])

        n2 = Norms("n2", 1, 1)
        fix_mm, fixed, s2_done = sem("fix_mm"), sem("fixed"), sem("s2_done")
        taken2 = Count(sem("taken2"))
        gt2_mm, gt2, bias2_mm = Count(sem("gt2_mm")), Count(sem("gt2")), Count(sem("bias2_mm"))
        xm2 = Count(sem("xm2"), E)
        xm2_mm = Count(sem("xm2_mm"), E)
        xm2_cp = Count(sem("xm2_cp"), E)
        up2_mm = Count(sem("up2_mm"), E)
        h2 = Count(sem("h2"), E)
        dn2_mm = Count(sem("dn2_mm"), E)
        acc2 = Count(sem("acc2"), E)
        pre3_mm = Count(sem("pre3_mm"), 5)
        pre3 = Count(sem("pre3"), 5)
        conv = Count(sem("conv"), 3)
        csl = Count(sem("csl"), 3)
        sq3, ss3_mm, ss3 = Count(sem("sq3")), Count(sem("ss3_mm")), Count(sem("ss3"))
        nr3, rn3, rb3_mm = Count(sem("nr3")), Count(sem("rn3")), Count(sem("rb3_mm"), 2)
        bv3, taken3 = Count(sem("bv3")), Count(sem("taken3"))
        rep_mm = Count(sem("rep_mm"), CPT)
        rep_cp = Count(sem("rep_cp"), CPT)
        decay = [Count(sem(f"decay{g}"), NSTEP) for g in range(2)]
        state = [Count(sem(f"state{g}"), NSTEP) for g in range(2)]
        read = Count(sem("read"), NSTEP)
        o3_mm = Count(sem("o3_mm"), CPT)
        o3 = Count(sem("o3"), CPT)
        n4 = Norms("n4", 2, 1)
        o3_st, o3_tr = Count(sem("o3_st")), Count(sem("o3_tr"))
        r3_mm, sig3_in, sig3 = Count(sem("r3_mm")), Count(sem("sig3_in")), Count(sem("sig3"))
        g3, gt3_mm, gt3 = Count(sem("g3")), Count(sem("gt3_mm")), Count(sem("gt3"))
        up3_mm = Count(sem("up3_mm"), E // 2 + 1)
        h3 = Count(sem("h3"), E // 2 + 1)
        gb3_mm = Count(sem("gb3_mm"), E // 2)
        hg3 = Count(sem("hg3"), E // 2)
        dn3_mm = Count(sem("dn3_mm"), E // 2 + 1)
        stored = sem("stored")
        vstep2, vstep4 = sem("vstep2"), sem("vstep4")
        vstep3 = [sem("vstep3a"), sem("vstep3b")]
        pstep2, pstep4 = sem("pstep2"), sem("pstep4")

        padded = [sb(f"padded{w}", [P, SPB, SEQ + 3]) for w in range(3)]
        load2 = sb("load2", [P, 2, E])
        load2_b = sb("load2_b", [P, 2, E])
        gt = sb("gt", [E + 1, BLK])
        ss = sb("ss", [P, 8])
        nr = sb("nr", [P, 8])
        nre = sb("nre", [P, 8])
        rn = sb("rn", [P, 8])
        eps_l2 = sb("eps_l2", [P, 8])
        HS = SEQS // 2
        st3 = [[sb(f"st3_{g}_{n}", [P, HS, DH + 1]) for n in range(2)] for g in range(2)]
        decayed = [sb(f"decayed{g}", [P, HS, DH]) for g in range(2)]
        prod = [sb(f"prod{g}", [P, HS, DH + 1]) for g in range(2)]
        uu = [sb(f"uu{g}", [P, HS]) for g in range(2)]
        upd = [sb(f"upd{g}", [P, HS, DH]) for g in range(2)]

        def wide(n):
            return wides[n][:, :].rearrange("p (t b e) -> p t b e", t=STEPS, b=SEQS)

        block = ctx.enter_context(nc.Block())

        @block.sync
        def _(sp):
            xv = t["x"].rearrange("b s d -> (b s) d").rearrange("(k p) d -> p k d", p=P)
            sp.dma_start(x_in[:, :, :], xv[:, 0:TPB, :]).then_inc(loaded_x.sem, 16)
            for name, dst in (("ident", ident[:, :]), ("cols", cols[:, :]), ("rope_cos", rope_cos[:, :]),
                              ("rope_sin", rope_sin[:, :]), ("iota8", iota8[:, :]), ("wd0", wd0[:, :]),
                              ("wup0", wup0[:, :]), ("wv0", room[0][:, 0:PAIRS * RANK0]),
                              ("wo0a", room[1][:, :]), ("wo0b", room[2][:, :]), ("wr0", wr0[:, :]),
                              ("head_ones", head_ones[:, :]), ("w1a", w1a[:, :, :]), ("bo1", bo1[:, :]),
                              ("wr1", wr1[:, :]), ("rb1", rb1[:, :]), ("w2a", w2a[:, :, :]), ("wv2", wv2[:, :, :]),
                              ("wg2", wg2[:, :]), ("wo2", wo2[:, :, :]), ("wr2", wr2[:, :]), ("rb2", rb2[:, :])):
                sp.dma_start(dst, t[name]).then_inc(w_small, 16)
            sp.dma_start(up0, t["up0"]).then_inc(w_l0, 16)
            sp.dma_start(dn0, t["dn0"]).then_inc(w_l0, 16)
            sp.dma_start(up1, t["up1"]).then_inc(w_l1, 16)
            sp.dma_start(dn1, t["dn1"]).then_inc(w_l1, 16)
            for name, dst in (("up2", up2[:, :, :]), ("dn2", dn2[:, :, :]), ("b1_2", b1_2[:, :]),
                              ("b2_2", b2_2[:, :]), ("w3a", w3a[:, :, :]), ("wab3", wab3[:, :, :]),
                              ("conv3", conv3[:, :, :]), ("wo3", wo3[:, :, :]), ("wr3", wr3[:, :]),
                              ("up3", up3[:, :, :]), ("dn3", dn3[:, :, :]), ("b1_3", b1_3[:, :]),
                              ("b2_3", b2_3[:, :]), ("ws1_3", ws1_3[:, :]), ("ws2_3", ws2_3[:, :]),
                              ("sel_e", sel_e[:, :, :]), ("sel_pair", sel_pair[:, :, :])):
                sp.dma_start(dst, t[name]).then_inc(w_late, 16)
            with sp.Fori(0, NBLK - 1) as i:
                sp.wait_ge(x_taken.sem, x_taken.at(i))
                sp.dma_start(x_in[:, :, :], xv[:, bass.ds(i * TPB + TPB, TPB), :]).then_inc(loaded_x.sem, 16)
            ov = out.rearrange("b s d -> (b s) d").rearrange("(k p) d -> p k d", p=P)
            with sp.Fori(0, NBLK) as i:
                sp.wait_ge(n4.x.sem, n4.x.at(i, 1))
                sp.dma_start(ov[:, bass.ds(i * TPB, TPB), :], x_out[:, :, :]).then_inc(stored, 16)
            sp.wait_ge(stored, 16 * NBLK + 1)

        @block.gpsimd
        def _(pool):
            for buf, value in ((eps_ln, LN_EPS), (eps_rms, RMS_EPS), (mhalf, -0.5), (phalf, 0.5), (ones, 1.0)):
                pool.memset(buf[:, :], value).then_inc(consts, 1)
            pool.memset(eps_l2[:, :], L2_EPS).then_inc(consts, 1)
            for w in range(3):
                pool.memset(padded[w][:, :, :], 0.0).then_inc(consts, 1)
            pool.memset(gt[:, :], 1.0).then_inc(consts, 1)
            pool.memset(load2[:, :, :], 0.0).then_inc(consts, 1)
            pool.wait_ge(consts, 11)
            pool.wait_ge(w_small, 16 * 22)
            with pool.Fori(0, NBLK) as i:
                st = Steps(pool, pstep, i, PPER1)
                norm_rstd(pool, st, n1, i, 0, eps_ln)
                for p in range(PAIRS):
                    for w in range(2):
                        n = 2 * p + w
                        pool.wait_ge(qk_cp.sem, qk_cp.at(i, n))
                        if n >= 2:
                            pool.wait_ge(qk_rot.sem, qk_rot.at(i, n - 2))
                        pool.tensor_tensor(halves(cosm[w][:, :]), halves(qa[w][:, :]),
                                           rope_cos[:, :].unsqueeze(1).to_broadcast([P, SPB, SEQ]),
                                           ALU.mult).then_inc(qk_cos.sem, 1)
                norm_rstd(pool, st, n1, i, 1, eps_ln)
                norm_rstd(pool, st, n1, i, 2, eps_rms)
                norm_rstd(pool, st, n1, i, 3, eps_ln)
                norm_rstd(pool, st, n1, i, 4, eps_ln)
                norm_rstd(pool, st, n1, i, 5, eps_ln)
                q2, sc = room[1], [room[7], room[8]]
                qsb = [room[9], room[10]]
                pool.wait_ge(qk2_f.sem, qk2_f.at(i, 0))
                for j in range(DH):
                    pool.wait_ge(sc2.sem, sc2.at(i, j))
                    if j >= 2:
                        pool.wait_ge(y2_mm.sem, y2_mm.at(i, j - 2))
                    pool.tensor_tensor(qsb[j % 2][:, :], sc[j % 2][:, :], q2[:, :], ALU.mult).then_inc(qs2.sem, 1)
                norm_rstd(pool, st, n1, i, 6, eps_ln)
                st.end()
            with pool.Fori(0, NBLK) as i:
                st = Steps(pool, pstep2, i, PPER2)
                pool.wait_ge(taken2.sem, taken2.at(i))
                for e in range(E):
                    if e >= 2:
                        pool.wait_ge(xm2_mm.sem, xm2_mm.at(i, e - 2))
                    pool.tensor_tensor(tiles(room[e % 2][:, :]), x_tok[:, :, :],
                                       gates[:, :, e:e + 1].to_broadcast([P, TPB, P]),
                                       ALU.mult).then_inc(xm2.sem, 1)
                norm_rstd(pool, st, n2, i, 0, eps_ln)
                pool.wait_ge(csl.sem, csl.at(i, 2))
                pool.wait_ge(pre3.sem, pre3.at(i, 4))
                pool.tensor_tensor(hist[2][:, bass.ds(i * BLK, BLK)], room[5][:, :], room[10][:, :],
                                   ALU.mult).then_inc(bv3.sem, 1)
                pool.wait_ge(ss3.sem, ss3.at(i))
                st.do(pool.tensor_tensor(nr[:, :], ss[:, :], phalf[:, :], ALU.pow))
                st.sync()
                pool.tensor_tensor(nre[:, :], nr[:, :], eps_l2[:, :], ALU.add).then_inc(nr3.sem, 1)
                st.end()

            def per_seq(n, t, g):
                v = hist[n].rearrange("p (b t) -> p b t", b=SEQS)[:, g * HS:(g + 1) * HS, bass.ds(t, 1)]
                return v.to_broadcast([P, HS, DH])

            def read_out(i, n):
                h, k = n // STEPS, n % STEPS
                for g in range(2):
                    last = pool.tensor_tensor(wide(4 + h)[:, k, g * HS:(g + 1) * HS, :],
                                              st3[g][(n + 1) % 2][:, :, 0:DH],
                                              per_seq(0, i * NSTEP + n, g), ALU.mult)
                last.then_inc(read.sem, 1)

            def delta_pool(i):
                for n in range(NSTEP):
                    for g in range(2):
                        pool.wait_ge(state[g].sem, i * NSTEP + (n + 1))
                        pool.tensor_tensor(decayed[g][:, :, :], st3[g][n % 2][:, :, 0:DH],
                                           per_seq(3, i * NSTEP + n, g), ALU.mult).then_inc(decay[g].sem, 1)
                    if n >= 1:
                        read_out(i, n - 1)
                for g in range(2):
                    pool.wait_ge(state[g].sem, i * NSTEP + (NSTEP + 1))
                read_out(i, NSTEP - 1)

            pool.wait_ge(taken3.sem, NBLK)
            with pool.Fori(0, TURNS) as i:
                delta_pool(i)
            with pool.Fori(0, NBLK) as i:
                st = Steps(pool, pstep4, i, PPER4)
                for c in range(2):
                    norm_rstd(pool, st, n4, i, c, eps_ln)
                st.end()

        @block.scalar
        def _(act):
            act.wait_ge(w_small, 16 * 22)
            act.wait_ge(consts, 11)
            act.wait_ge(vo_mm, 1)
            act.activation(vo0[:, 0:4, :].rearrange("p a m -> p (a m)"), ps[0][:, :], ACT.Copy).then_inc(vo_done, 1)
            act.activation(vo0[:, 4:8, :].rearrange("p a m -> p (a m)"), ps[1][:, :], ACT.Copy).then_inc(vo_done, 1)
            with act.Fori(0, NBLK) as i:
                norm_copy(act, n1, i, 0, h_t, ps[6], scale=col(LNS), bias=col(LNB))
                act.wait_ge(c_mm.sem, c_mm.at(i))
                act.activation(c_t[:, :], ps[7][:, :], ACT.Copy)
                act.activation(ck[:, 0:TPB * RANK0], ps[5][:, 0:TPB * RANK0], ACT.Copy).then_inc(c_cp.sem, 1)

                def copy_qk(p):
                    for w in range(2):
                        n = 2 * p + w
                        act.wait_ge(qk_mm.sem, qk_mm.at(i, n))
                        if n >= 2:
                            act.wait_ge(qk_rot.sem, qk_rot.at(i, n - 2))
                            act.wait_ge(qk_cos.sem, qk_cos.at(i, n - 2))
                        act.activation(qa[w][:, :], ps[w][:, :], ACT.Copy).then_inc(qk_cp.sem, 1)

                copy_qk(0)
                for n in range(UNITS + 6):
                    if n >= 4 and (n - 4) % 4 == 3 and n - 4 < UNITS:
                        p = (n - 4) // 4
                        act.wait_ge(pv_mm.sem, pv_mm.at(i, n - 4))
                        if p >= 1:
                            act.wait_ge(y0_mm.sem, y0_mm.at(i, p - 1))
                        act.activation(ovs[:, :], ps[6][:, :], ACT.Copy).then_inc(ov_cp.sem, 1)
                    if n < UNITS:
                        act.wait_ge(sc_max.sem, sc_max.at(i, n))
                        if n >= 2:
                            act.wait_ge(pt_mm.sem, pt_mm.at(i, n - 2))
                        for q in range(2):
                            last = act.activation(ex[n % 2][:, q * SEQ:(q + 1) * SEQ],
                                                  ps[2 + n % 2][:, q * SEQ:(q + 1) * SEQ], ACT.Exp,
                                                  bias=nmx[:, n % 4, q:q + 1], scale=float(DH0) ** -0.5,
                                                  accum_out=rsum[:, n % 4, q:q + 1])
                        last.then_inc(pr_exp.sem, 1)
                        if n % 4 == 0 and n // 4 + 1 < PAIRS:
                            copy_qk(n // 4 + 1)
                    if 0 <= n - 2 < UNITS:
                        m = n - 2
                        act.wait_ge(pt_mm.sem, pt_mm.at(i, m))
                        if m >= 2:
                            act.wait_ge(pv_mm.sem, pv_mm.at(i, m - 2))
                        act.activation(pts[m % 2][:, :], ps[4 + m % 2][:, :], ACT.Copy).then_inc(pt_cp.sem, 1)
                norm_copy(act, n1, i, 1, x_t, ps[6], scale=col(RMSW))
                soft_act(act, i, d0, s0)
                for n in range(2 * E):
                    act.wait_ge(up0_mm.sem, up0_mm.at(i, n))
                    if n >= 2:
                        act.wait_ge(h0.sem, h0.at(i, n - 2))
                    act.activation(room[n % 2][:, :], ps[2 * (n % 2) + 1][:, :], ACT.Silu).then_inc(sl0.sem, 1)
                norm_copy(act, n1, i, 2, x_t, ps[6])
                for w, b in enumerate((BQ1, BK1)):
                    act.wait_ge(qkv1_mm.sem, qkv1_mm.at(i, w))
                    act.activation(room[w][:, :], ps[w][:, :], ACT.Square, bias=col(b)).then_inc(qkv1_sq.sem, 1)
                act.wait_ge(qkv1_sq.sem, qkv1_sq.at(i, 1))
                for w in range(2):
                    act.activation(room[2 + w][:, :], room[w][:, :], ACT.Exp, scale=-0.5).then_inc(qkv1_f.sem, 1)
                act.wait_ge(qkv1_mm.sem, qkv1_mm.at(i, 2))
                act.activation(room[4][:, :], ps[2][:, :], ACT.Identity, bias=col(BV1)).then_inc(qkv1_f.sem, 1)
                norm_copy(act, n1, i, 3, x_t, ps[6])
                act.wait_ge(rt1.sem, rt1.at(i))
                act.activation(score_r[:, :, :], score_r[:, :, :], ACT.Sigmoid)
                act.activation(score[:, :, :], score[:, :, :], ACT.Sigmoid).then_inc(rsig1.sem, 1)
                soft_act(act, i, d1, s1)
                for n in range(CH1 * NE1):
                    act.wait_ge(up1_mm.sem, up1_mm.at(i, n))
                    if n >= 2 * CH1 and n % CH1 == 0:
                        act.wait_ge(dn1_mm.sem, dn1_mm.at(i, n // CH1 - 2))
                    act.activation(room[n % (2 * CH1)][:, :], ps[n % 4][:, :], ACT.Gelu).then_inc(h1.sem, 1)
                norm_copy(act, n1, i, 4, x_t, ps[6])
                for w in range(2):
                    act.wait_ge(qk2_mm.sem, qk2_mm.at(i, w))
                    act.activation(room[3 + w][:, :], ps[w][:, :], ACT.Copy,
                                   scale=(float(DH) ** -0.5 if w == 0 else 1.0)).then_inc(qk2_cp.sem, 1)
                for w in range(2):
                    act.wait_ge(qk2_min.sem, qk2_min.at(i, w))
                    act.activation(room[5 + w][:, :], room[1 + w][:, :], ACT.Exp).then_inc(qk2_exp.sem, 1)
                act.wait_ge(qk2_mm.sem, qk2_mm.at(i, 2))
                act.activation(room[0][:, :], ps[2][:, :], ACT.Sigmoid, bias=col(BG2)).then_inc(qk2_cp.sem, 1)
                norm_copy(act, n1, i, 5, x_t, ps[6])
                soft_act(act, i, d2, s2)
            act.wait_ge(w_late, 16 * 17)
            with act.Fori(0, NBLK) as i:
                act.wait_ge(gt2_mm.sem, gt2_mm.at(i))
                act.activation(gt[0:E, :], ps[4][0:E, :], ACT.Copy).then_inc(gt2.sem, 1)
                for e in range(E):
                    act.wait_ge(xm2_mm.sem, xm2_mm.at(i, e))
                    if e >= 2:
                        act.wait_ge(up2_mm.sem, up2_mm.at(i, e - 2))
                    act.activation(room[2 + e % 2][:, :], ps[6 + e % 2][:, :], ACT.Copy).then_inc(xm2_cp.sem, 1)
                    act.wait_ge(up2_mm.sem, up2_mm.at(i, e))
                    if e >= 2:
                        act.wait_ge(dn2_mm.sem, dn2_mm.at(i, e - 2))
                    act.activation(room[4 + e % 2][:, :], ps[e % 2][:, :], ACT.Gelu,
                                   bias=b1_2[:, e:e + 1]).then_inc(h2.sem, 1)
                norm_copy(act, n2, i, 0, x_t, ps[6])
                for w, b in enumerate((BQ3, BK3, BV3)):
                    act.wait_ge(pre3_mm.sem, pre3_mm.at(i, w))
                    act.activation(padded[w][:, :, 2:2 + SEQ], halves(ps[w][:, :]), ACT.Silu,
                                   bias=col(b)).then_inc(pre3.sem, 1)
                for w in range(3):
                    act.wait_ge(conv.sem, conv.at(i, w))
                    act.activation(room[3 + w][:, :], room[6 + w][:, :], ACT.Silu).then_inc(csl.sem, 1)
                act.wait_ge(csl.sem, csl.at(i, 2))
                act.activation(room[6][:, :], room[3][:, :], ACT.Square)
                act.activation(room[7][:, :], room[4][:, :], ACT.Square).then_inc(sq3.sem, 1)
                for w, b in enumerate((BA3, BB3)):
                    act.wait_ge(pre3_mm.sem, pre3_mm.at(i, 3 + w))
                    act.activation(room[9 + w][:, :], ps[3 + w][:, :], ACT.Sigmoid,
                                   bias=col(b)).then_inc(pre3.sem, 1)

            def copy_rep(i, h):
                act.wait_ge(rep_mm.sem, rep_mm.at(i, h))
                for g in range(2):
                    for e in range(4):
                        for dst, bank in ((wide(h), ps[g]), (gated_keys[h], ps[2 + g])):
                            act.activation(dst[:, :, :, 4 * g + e],
                                           bank[:, e * P:(e + 1) * P].rearrange("p (b t) -> p t b", b=SEQS),
                                           ACT.Copy)
                bvv = hist[2].rearrange("p (b t) -> p t b", b=SEQS)
                act.activation(gated_keys[h][:, :, :, DH], bvv[:, bass.ds(i * NSTEP + h * STEPS, STEPS), :],
                               ACT.Copy).then_inc(rep_cp.sem, 1)

            def delta_act(i, last):
                for h in range(CPT):
                    if h == 0:
                        copy_rep(i, 1)
                    elif not last:
                        copy_rep(i + 1, 0)
                    act.wait_ge(o3_mm.sem, o3_mm.at(i, h))
                    o3v = hist[0].rearrange("p (b t) -> p b t", b=SEQS)
                    act.activation(o3v[:, :, bass.ds(i * NSTEP + h * STEPS, STEPS)],
                                   ps[4 + h][:, 0:STEPS * SEQS].rearrange("p (b t) -> p b t", b=SEQS),
                                   ACT.Identity, bias=col(BO3)).then_inc(o3.sem, 1)

            copy_rep(0, 0)
            with act.Fori(0, TURNS - 1) as i:
                delta_act(i, False)
            delta_act(TURNS - 1, True)
            with act.Fori(0, NBLK) as i:
                act.wait_ge(o3.sem, CPT * TURNS)
                act.activation(room[0][:, :], hist[0][:, bass.ds(i * BLK, BLK)], ACT.Copy).then_inc(o3_st.sem, 1)
                norm_copy(act, n4, i, 0, x_t, ps[6])
                act.wait_ge(sig3_in.sem, sig3_in.at(i))
                act.activation(score_r[:, :, :], score[:, :, :], ACT.Sigmoid).then_inc(sig3.sem, 1)
                for p in range(E // 2 + 1):
                    act.wait_ge(up3_mm.sem, up3_mm.at(i, p))
                    if p < E // 2:
                        act.activation(room[1 + p][:, :], ps[p % 2][:, :], ACT.Gelu,
                                       bias=b1_3[:, p:p + 1]).then_inc(h3.sem, 1)
                    else:
                        act.activation(room[1 + p][0:64, :], ps[p % 2][0:64, :], ACT.Gelu,
                                       bias=cols[0:64, BS3:BS3 + 1]).then_inc(h3.sem, 1)
                act.wait_ge(gt3_mm.sem, gt3_mm.at(i))
                act.activation(gt[0:E, :], ps[4][0:E, :], ACT.Copy).then_inc(gt3.sem, 1)

        @block.tensor
        def _(pe):
            pe.wait_ge(w_small, 16 * 22)
            for p in range(PAIRS):
                src = (room[1] if p < 4 else room[2])[:, (p % 4) * P:(p % 4 + 1) * P]
                for j in range(2):
                    rows = slice(j * 64, j * 64 + 64)
                    last = pe.matmul(ps[p // 4][rows, (p % 4) * P:(p % 4 + 1) * P],
                                     room[0][rows, p * RANK0:(p + 1) * RANK0], src[rows, :],
                                     start=True, stop=True)
            last.then_inc(vo_mm, 1)
            pe.wait_ge(vo_done, 2)
            with pe.Fori(0, NBLK) as i:
                norm_transpose(pe, n1, i, 0, 0, x_new, ps[6])
                pe.wait_ge(n1.xt.sem, n1.xt.at(i, 0))
                pe.matmul(ps[7][:, :], wd0[:, :], h_t[:, :], start=True, stop=True)
                for k in range(TPB):
                    last = pe.matmul(ps[5][:, k * RANK0:(k + 1) * RANK0], h_t[:, k * P:(k + 1) * P],
                                     wd0[:, RANK0:2 * RANK0], start=True, stop=True)
                last.then_inc(c_mm.sem, 1)
                pe.wait_ge(c_cp.sem, c_cp.at(i))

                def project(p):
                    for w in range(2):
                        rows = slice(w * 64, w * 64 + 64)
                        if p >= 1:
                            pe.wait_ge(qk_cp.sem, qk_cp.at(i, 2 * (p - 1) + w))
                        pe.matmul(ps[w][:, :], wup0[rows, p * P:(p + 1) * P], c_t[rows, :],
                                  start=True, stop=True).then_inc(qk_mm.sem, 1)

                project(0)
                for n in range(UNITS + 6):
                    if n < UNITS:
                        p, j, s = n // 4, (n // 2) % 2, n % 2
                        rows = slice(j * 64, j * 64 + 64)
                        pe.wait_ge(qk_rot.sem, qk_rot.at(i, 2 * p + 1))
                        if n >= 2:
                            pe.wait_ge(pr_exp.sem, pr_exp.at(i, n - 2))
                        q_r, k_r = rot[0][p % 2], rot[1][p % 2]
                        for q in range(2):
                            last = pe.matmul(ps[2 + n % 2][:, q * SEQ:(q + 1) * SEQ],
                                             q_r[rows, s * SEQ + q * P:s * SEQ + (q + 1) * P],
                                             k_r[rows, s * SEQ:(s + 1) * SEQ], start=True, stop=True)
                        last.then_inc(sc_mm.sem, 1)
                        if n % 4 == 0 and p + 1 < PAIRS:
                            project(p + 1)
                    if 0 <= n - 2 < UNITS:
                        m = n - 2
                        pe.wait_ge(pr_norm.sem, pr_norm.at(i, m))
                        if m >= 2:
                            pe.wait_ge(pt_cp.sem, pt_cp.at(i, m - 2))
                        for kt in range(2):
                            for q in range(2):
                                last = pe.transpose(ps[4 + m % 2][:, kt * SEQ + q * P:kt * SEQ + (q + 1) * P],
                                                    ex[m % 2][:, q * SEQ + kt * P:q * SEQ + (kt + 1) * P],
                                                    ident[:, :])
                        last.then_inc(pt_mm.sem, 1)
                    if 0 <= n - 3 < UNITS:
                        m = n - 3
                        p, j, s = m // 4, (m // 2) % 2, m % 2
                        pe.wait_ge(pt_cp.sem, pt_cp.at(i, m))
                        if m % 4 == 0 and p >= 1:
                            pe.wait_ge(ov_cp.sem, ov_cp.at(i, p - 1))
                        for kt in range(2):
                            last = pe.matmul(ps[6][j * 64:j * 64 + 64, s * SEQ:(s + 1) * SEQ],
                                             ck[:, (2 * s + kt) * RANK0:(2 * s + kt + 1) * RANK0],
                                             pts[m % 2][:, kt * SEQ:(kt + 1) * SEQ],
                                             start=(kt == 0), stop=(kt == 1))
                        last.then_inc(pv_mm.sem, 1)
                    if n >= 5 and (n - 5) % 4 == 3 and n - 5 < UNITS:
                        p = (n - 5) // 4
                        pe.wait_ge(ov_cp.sem, ov_cp.at(i, p))
                        for k in range(TPB):
                            last = pe.matmul(ps[7][:, k * P:(k + 1) * P], ovs[:, k * P:(k + 1) * P],
                                             vo0[:, p, :], start=(p == 0 and k == 0), stop=(p == PAIRS - 1),
                                             skip_group_check=True)
                        last.then_inc(y0_mm.sem, 1)
                norm_transpose(pe, n1, i, 2, 1, x_new, ps[6])
                pe.wait_ge(n1.xt.sem, n1.xt.at(i, 1))
                router_mm(pe, x_t, wr0, ps[7], r0_mm)
                pe.wait_ge(w_l0, 32)

                def up_0(e):
                    for c in range(2):
                        n = 2 * e + c
                        if n >= 2:
                            pe.wait_ge(h0.sem, h0.at(i, n - 2))
                        for g in range(2):
                            last = pe.matmul(ps[2 * c + g][:, :], up0[:, e, 2 * g + c, :], x_t[:, :],
                                             start=True, stop=True)
                        last.then_inc(up0_mm.sem, 1)

                up_0(0)
                for e in range(E):
                    if e + 1 < E:
                        up_0(e + 1)
                    if e >= 2:
                        pe.wait_ge(acc0.sem, acc0.at(i, e - 2))
                    for c in range(2):
                        pe.wait_ge(h0.sem, h0.at(i, 2 * e + c))
                        for k in range(TPB):
                            last = pe.matmul(ps[4 + e % 2][:, k * P:(k + 1) * P],
                                             room[2 + 2 * (e % 2) + c][:, k * P:(k + 1) * P], dn0[:, e, c, :],
                                             start=(c == 0 and k == 0), stop=(c == 1), skip_group_check=True)
                    last.then_inc(dn0_mm.sem, 1)
                norm_transpose(pe, n1, i, 3, 2, x_tok, ps[6])
                pe.wait_ge(n1.xt.sem, n1.xt.at(i, 2))
                for w in range(3):
                    pe.matmul(ps[w][:, :], w1a[:, w, :], x_t[:, :], start=True, stop=True).then_inc(qkv1_mm.sem, 1)
                pe.wait_ge(qk1.sem, qk1.at(i))
                pe.matmul(ps[3][:, :], head_ones[:, :], room[0][:, :], start=True, stop=True).then_inc(co1_mm.sem, 1)
                pe.wait_ge(ov1.sem, ov1.at(i))
                for k in range(TPB):
                    last = pe.matmul(ps[4][:, k * P:(k + 1) * P], room[5][:, k * P:(k + 1) * P], w1a[:, 3, :],
                                     start=True, stop=True)
                last.then_inc(y1_mm.sem, 1)
                norm_transpose(pe, n1, i, 4, 3, x_tok, ps[6])
                pe.wait_ge(n1.xt.sem, n1.xt.at(i, 3))
                router_mm(pe, x_t, wr1, ps[7], r1_mm)
                pe.wait_ge(w_l1, 32)

                def up_1(x):
                    for c in range(CH1):
                        n = CH1 * x + c
                        if n >= CH1:
                            pe.wait_ge(h1.sem, h1.at(i, n - CH1))
                        pe.matmul(ps[n % 4][:, :], up1[:, x, c, :], x_t[:, :],
                                  start=True, stop=True).then_inc(up1_mm.sem, 1)

                up_1(0)
                for x in range(NE1):
                    if x + 1 < NE1:
                        up_1(x + 1)
                    o = max(x - 1, 0)
                    if o >= 2 and x >= 2:
                        pe.wait_ge(acc1.sem, acc1.at(i, o - 2))
                    for c in range(CH1):
                        pe.wait_ge(h1.sem, h1.at(i, CH1 * x + c))
                        for k in range(TPB):
                            last = pe.matmul(ps[4 + o % 2][:, k * P:(k + 1) * P],
                                             room[(CH1 * x + c) % (2 * CH1)][:, k * P:(k + 1) * P],
                                             dn1[:, x, c, :], start=(c == 0 and k == 0 and x != 1),
                                             stop=(c == CH1 - 1), skip_group_check=True)
                    last.then_inc(dn1_mm.sem, 1)
                norm_transpose(pe, n1, i, 5, 4, x_tok, ps[6])
                pe.wait_ge(n1.xt.sem, n1.xt.at(i, 4))
                for w, wt in enumerate((w2a[:, 0, :], w2a[:, 1, :], wg2[:, :])):
                    pe.matmul(ps[w][:, :], wt, x_t[:, :], start=True, stop=True).then_inc(qk2_mm.sem, 1)

                def value_2(j):
                    if j >= 2:
                        pe.wait_ge(kv2.sem, kv2.at(i, j - 2))
                    pe.matmul(ps[3 + j % 2][:, :], wv2[:, j, :], x_t[:, :], start=True, stop=True).then_inc(v2_mm.sem, 1)

                value_2(0)
                value_2(1)
                for j in range(DH):
                    if j + 2 < DH:
                        value_2(j + 2)
                    pe.wait_ge(qs2.sem, qs2.at(i, j))
                    for k in range(TPB):
                        last = pe.matmul(ps[7][:, k * P:(k + 1) * P], room[9 + j % 2][:, k * P:(k + 1) * P],
                                         wo2[:, j, :], start=(j == 0 and k == 0), stop=(j == DH - 1),
                                         skip_group_check=True)
                    last.then_inc(y2_mm.sem, 1)
                norm_transpose(pe, n1, i, 6, 5, x_tok, ps[6])
                pe.wait_ge(n1.xt.sem, n1.xt.at(i, 5))
                router_mm(pe, x_t, wr2, ps[7], r2_mm)
            pe.wait_ge(s2_done, 1)
            for n in range(2):
                last = pe.matmul(ps[0][0:E, n:n + 1], load2[:, n, :], ones[:, :], start=True, stop=True)
            last.then_inc(fix_mm, 1)
            pe.wait_ge(w_late, 16 * 17)
            with pe.Fori(0, NBLK) as i:
                pe.wait_ge(taken2.sem, taken2.at(i))
                for k in range(TPB):
                    last = pe.transpose(ps[4][0:E, k * P:(k + 1) * P], gates[:, k, :], ident[:, :])
                last.then_inc(gt2_mm.sem, 1)
                pe.wait_ge(gt2.sem, gt2.at(i))
                for k in range(TPB):
                    last = pe.matmul(ps[5][:, k * P:(k + 1) * P], gt[0:E, k * P:(k + 1) * P], b2_2[:, :],
                                     start=True, stop=True)
                last.then_inc(bias2_mm.sem, 1)

                def turn_2(e):
                    pe.wait_ge(xm2.sem, xm2.at(i, e))
                    if e >= 2:
                        pe.wait_ge(xm2_cp.sem, xm2_cp.at(i, e - 2))
                    for k in range(TPB):
                        last = pe.transpose(ps[6 + e % 2][:, k * P:(k + 1) * P],
                                            room[e % 2][:, k * P:(k + 1) * P], ident[:, :])
                    last.then_inc(xm2_mm.sem, 1)

                turn_2(0)
                for e in range(E + 1):
                    if e + 1 < E:
                        turn_2(e + 1)
                    if e < E:
                        pe.wait_ge(xm2_cp.sem, xm2_cp.at(i, e))
                        if e >= 2:
                            pe.wait_ge(h2.sem, h2.at(i, e - 2))
                        pe.matmul(ps[e % 2][:, :], up2[:, e, :], room[2 + e % 2][:, :],
                                  start=True, stop=True).then_inc(up2_mm.sem, 1)
                    if e >= 1:
                        m = e - 1
                        pe.wait_ge(h2.sem, h2.at(i, m))
                        if m >= 2:
                            pe.wait_ge(acc2.sem, acc2.at(i, m - 2))
                        for k in range(TPB):
                            last = pe.matmul(ps[2 + m % 2][:, k * P:(k + 1) * P],
                                             room[4 + m % 2][:, k * P:(k + 1) * P], dn2[:, m, :],
                                             start=True, stop=True)
                        last.then_inc(dn2_mm.sem, 1)
                norm_transpose(pe, n2, i, 0, 0, x_tok, ps[6])
                pe.wait_ge(n2.xt.sem, n2.xt.at(i))
                for w in range(5):
                    wt = w3a[:, w, :] if w < 3 else wab3[:, w - 3, :]
                    pe.matmul(ps[w][:, :], wt, x_t[:, :], start=True, stop=True).then_inc(pre3_mm.sem, 1)
                pe.wait_ge(sq3.sem, sq3.at(i))
                for w in range(2):
                    for k in range(TPB):
                        last = pe.matmul(ps[5][:, w * TPB + k:w * TPB + k + 1],
                                         room[6 + w][:, k * P:(k + 1) * P], ones[:, :], start=True, stop=True)
                last.then_inc(ss3_mm.sem, 1)
                pe.wait_ge(rn3.sem, rn3.at(i))
                for w in range(2):
                    for k in range(TPB):
                        n = w * TPB + k
                        last = pe.matmul(ps[6 + w][:, k * P:(k + 1) * P], rn[:, n:n + 1].to_broadcast([P, P]),
                                         ident[:, :], start=True, stop=True)
                    last.then_inc(rb3_mm.sem, 1)

            def replicate(i, h, first):
                if first:
                    pe.wait_ge(taken3.sem, NBLK)
                else:
                    pe.wait_ge(rep_cp.sem, i * CPT + h)
                for n, src in enumerate((hist[1], hist[4])):
                    kv = src.rearrange("p (b t) -> p b t", b=SEQS)[:, :, bass.ds(i * NSTEP + h * STEPS, STEPS)]
                    for e in range(DH):
                        last = pe.matmul(ps[2 * n + e // 4][:, (e % 4) * P:(e % 4 + 1) * P], sel_e[:, e, :], kv,
                                         start=True, stop=True)
                last.then_inc(rep_mm.sem, 1)

            def project_3(i, h):
                pe.wait_ge(read.sem, read.at(i, STEPS * (h + 1) - 1))
                for e in range(DH):
                    last = pe.matmul(ps[4 + h][:, 0:STEPS * SEQS], wo3[:, e, :],
                                     wide(4 + h)[:, :, :, e].rearrange("p t b -> p b t"),
                                     start=(e == 0), stop=(e == DH - 1))
                last.then_inc(o3_mm.sem, 1)

            def delta_pe(i, last):
                replicate(i, 1, False)
                project_3(i, 0)
                if not last:
                    replicate(i + 1, 0, False)
                project_3(i, 1)

            replicate(0, 0, True)
            with pe.Fori(0, TURNS - 1) as i:
                delta_pe(i, False)
            delta_pe(TURNS - 1, True)
            with pe.Fori(0, NBLK) as i:
                pe.wait_ge(o3_st.sem, o3_st.at(i))
                for k in range(TPB):
                    last = pe.transpose(ps[6][:, k * P:(k + 1) * P], room[0][:, k * P:(k + 1) * P], ident[:, :])
                last.then_inc(o3_tr.sem, 1)
                norm_transpose(pe, n4, i, 0, 0, x_tok, ps[6])
                pe.wait_ge(n4.xt.sem, n4.xt.at(i))
                router_mm(pe, x_t, wr3, ps[7], r3_mm)
                for p in range(E // 2 + 1):
                    if p >= 2:
                        pe.wait_ge(h3.sem, h3.at(i, p - 2))
                    if p < E // 2:
                        last = pe.matmul(ps[p % 2][:, :], up3[:, p, :], x_t[:, :], start=True, stop=True)
                    else:
                        last = pe.matmul(ps[p % 2][0:64, :], ws1_3[:, :], x_t[:, :], start=True, stop=True)
                    last.then_inc(up3_mm.sem, 1)
                pe.wait_ge(g3.sem, g3.at(i))
                for k in range(TPB):
                    last = pe.transpose(ps[4][0:E, k * P:(k + 1) * P], gates[:, k, :], ident[:, :])
                last.then_inc(gt3_mm.sem, 1)
                pe.wait_ge(gt3.sem, gt3.at(i))

                def gate_rows(p):
                    if p >= 2:
                        pe.wait_ge(hg3.sem, hg3.at(i, p - 2))
                    pe.matmul(ps[2 + p % 2][:, :], sel_pair[:, p, :], gt[0:E, :],
                              start=True, stop=True).then_inc(gb3_mm.sem, 1)

                gate_rows(0)
                gate_rows(1)
                pe.wait_ge(h3.sem, h3.at(i, E // 2))
                for k in range(TPB):
                    pe.matmul(ps[5][:, k * P:(k + 1) * P], gt[0:E + 1, k * P:(k + 1) * P], b2_3[:, :],
                              start=(k == 0), stop=False, skip_group_check=True)
                for k in range(TPB):
                    last = pe.matmul(ps[5][:, k * P:(k + 1) * P], room[5][0:64, k * P:(k + 1) * P],
                                     ws2_3[:, :], start=False, stop=False, skip_group_check=True)
                last.then_inc(dn3_mm.sem, 1)
                for p in range(E // 2):
                    pe.wait_ge(hg3.sem, hg3.at(i, p))
                    if p + 2 < E // 2:
                        gate_rows(p + 2)
                    for k in range(TPB):
                        last = pe.matmul(ps[5][:, k * P:(k + 1) * P], room[6 + p][:, k * P:(k + 1) * P],
                                         dn3[:, p, :], start=False, stop=(p == E // 2 - 1),
                                         skip_group_check=True)
                    last.then_inc(dn3_mm.sem, 1)

        @block.vector
        def _(dve):
            swap = [n ^ 1 for n in range(32)]
            dve.wait_ge(w_small, 16 * 22)
            dve.wait_ge(consts, 11)
            x_tf, x_nf, x_if = (v[:, :, :].rearrange("p k m -> p (k m)") for v in (x_tok, x_new, x_in))
            with dve.Fori(0, NBLK) as i:
                st = Steps(dve, vstep, i, VPER1)
                dve.wait_ge(loaded_x.sem, i * 16 + 16)
                norm_stats(dve, st, n1, i, 0, x_in)
                norm_apply(dve, st, n1, i, 0, x_in, x_new)

                def rotate(p, w):
                    n = 2 * p + w
                    dve.wait_ge(qk_cp.sem, qk_cp.at(i, n))
                    if n >= 1:
                        dve.wait_ge(qk_rot.sem, qk_rot.at(i, n - 1))
                    st.do(dve.memset(gate_scratch[:, :], 0.0))
                    st.do(dve.stream_shuffle(sinm[:, :], qa[w][:, :], swap))
                    st.sync()
                    dve.tensor_tensor(halves(sinm2[:, :]), halves(sinm[:, :]),
                                      rope_sin[:, :].unsqueeze(1).to_broadcast([P, SPB, SEQ]),
                                      ALU.mult).then_inc(qk_sin.sem, 1)
                    dve.wait_ge(qk_sin.sem, qk_sin.at(i, n))
                    dve.wait_ge(qk_cos.sem, qk_cos.at(i, n))
                    if p >= 2:
                        dve.wait_ge(sc_mm.sem, sc_mm.at(i, 4 * (p - 2) + 3))
                    dve.tensor_tensor(rot[w][p % 2][:, :], sinm2[:, :], cosm[w][:, :],
                                      ALU.add).then_inc(qk_rot.sem, 1)

                rotate(0, 0)
                rotate(0, 1)
                for n in range(UNITS + 1):
                    if n < UNITS:
                        dve.wait_ge(sc_mm.sem, sc_mm.at(i, n))
                        if n >= 4:
                            dve.wait_ge(pr_exp.sem, pr_exp.at(i, n - 4))
                        st.do(dve.tensor_reduce(mx[:, n % 4, :], halves(ps[2 + n % 2][:, :]), AX_X, ALU.max))
                        st.sync()
                        dve.tensor_scalar(nmx[:, n % 4, :], mx[:, n % 4, :], -float(DH0) ** -0.5, None,
                                          ALU.mult).then_inc(sc_max.sem, 1)
                    if n >= 1:
                        m = n - 1
                        dve.wait_ge(pr_exp.sem, pr_exp.at(i, m))
                        st.do(dve.reciprocal(rinv[:, m % 4, :], rsum[:, m % 4, :]))
                        st.sync()
                        for q in range(2):
                            last = dve.tensor_scalar(ex[m % 2][:, q * SEQ:(q + 1) * SEQ],
                                                     ex[m % 2][:, q * SEQ:(q + 1) * SEQ],
                                                     rinv[:, m % 4, q:q + 1], None, ALU.mult)
                        last.then_inc(pr_norm.sem, 1)
                    if n % 4 in (1, 2) and n // 4 + 1 < PAIRS:
                        rotate(n // 4 + 1, n % 4 - 1)
                dve.wait_ge(y0_mm.sem, y0_mm.at(i, PAIRS - 1))
                dve.scalar_tensor_tensor(out=x_nf, in0=x_if, scalar=2.0, in1=ps[7][:, :], op0=ALU.mult,
                                         op1=ALU.add).then_inc(x_taken.sem, 1)
                dve.wait_ge(x_taken.sem, x_taken.at(i))
                norm_stats(dve, st, n1, i, 1, x_new)
                norm_apply(dve, st, n1, i, 1, x_new, x_tok)
                rms_stats(dve, st, n1, i, 2, x_tok, x_new)
                norm_apply(dve, st, n1, i, 2, x_tok, x_new, centre=False)
                st.do(dve.tensor_scalar(room[6][:, :], x_tf, 2.0, None, ALU.mult))
                dve.wait_ge(r0_mm.sem, r0_mm.at(i))
                st.do(dve.tensor_copy(score[:, :, :], ps[7][:, 0:TPB * E].rearrange("p (k e) -> p k e", e=E)))
                top_two(dve, st, score)
                soft_two(dve, st, top8[:, :, 0], top8[:, :, 1], d0)
                dve.wait_ge(s0.sem, s0.at(i))
                gate_sum(dve, st, gates[:, :, :])

                def gated_hidden(e):
                    for c in range(2):
                        n = 2 * e + c
                        dve.wait_ge(sl0.sem, sl0.at(i, n))
                        if e >= 2:
                            dve.wait_ge(dn0_mm.sem, dn0_mm.at(i, e - 2))
                        dve.tensor_tensor(room[2 + 2 * (e % 2) + c][:, :], ps[2 * c][:, :], room[n % 2][:, :],
                                          ALU.mult).then_inc(h0.sem, 1)

                gated_hidden(0)
                for e in range(E):
                    if e + 1 < E:
                        gated_hidden(e + 1)
                    dve.wait_ge(dn0_mm.sem, dn0_mm.at(i, e))
                    if e >= 1:
                        dve.wait_ge(acc0.sem, acc0.at(i, e - 1))
                    gated_add(dve, st, ps[4 + e % 2], gates[:, :, e:e + 1],
                              x_new if e else tiles(room[6][:, :]), x_new).then_inc(acc0.sem, 1)
                st.sync()
                dve.wait_ge(acc0.sem, acc0.at(i, E - 1))
                norm_stats(dve, st, n1, i, 3, x_new)
                norm_apply(dve, st, n1, i, 3, x_new, x_tok)
                st.do(dve.tensor_tensor(x_new[:, :, :], x_tok[:, :, :],
                                        bo1[:, :].unsqueeze(1).to_broadcast([P, TPB, P]), ALU.add))
                dve.wait_ge(qkv1_f.sem, qkv1_f.at(i, 1))
                dve.tensor_tensor(room[0][:, :], room[2][:, :], room[3][:, :], ALU.mult).then_inc(qk1.sem, 1)
                dve.wait_ge(qkv1_f.sem, qkv1_f.at(i, 2))
                dve.wait_ge(co1_mm.sem, co1_mm.at(i))
                dve.tensor_tensor(room[5][:, :], ps[3][:, :], room[4][:, :], ALU.mult).then_inc(ov1.sem, 1)
                st.sync()
                dve.wait_ge(y1_mm.sem, y1_mm.at(i))
                st.do(dve.tensor_tensor(x_nf, x_nf, ps[4][:, :], ALU.add))
                st.sync()
                norm_stats(dve, st, n1, i, 4, x_new)
                norm_apply(dve, st, n1, i, 4, x_new, x_tok)
                st.do(dve.tensor_scalar(x_nf, x_tf, 2.0, None, ALU.mult))
                dve.wait_ge(r1_mm.sem, r1_mm.at(i))
                raw = ps[7][:, 0:TPB * E].rearrange("p (k e) -> p k e", e=E)
                st.do(dve.tensor_copy(score_r[:, :, :], raw))
                st.sync()
                dve.tensor_tensor(score[:, :, :], raw, rb1[:, :].unsqueeze(1).to_broadcast([P, TPB, E]),
                                  ALU.add).then_inc(rt1.sem, 1)
                dve.wait_ge(rsig1.sem, rsig1.at(i))
                top_two(dve, st, score)
                pick_two(dve, st, score_r)
                soft_two(dve, st, two[:, 0, :], two[:, 1, :], d1)
                dve.wait_ge(s1.sem, s1.at(i))
                gate_sum(dve, st, gates[:, :, :])
                st.sync()
                dve.wait_ge(dn1_mm.sem, dn1_mm.at(i, 1))
                dve.tensor_tensor(x_nf, x_nf, ps[4][:, :], ALU.add).then_inc(acc1.sem, 1)
                for e in range(E):
                    dve.wait_ge(dn1_mm.sem, dn1_mm.at(i, e + NSH))
                    dve.wait_ge(acc1.sem, acc1.at(i, e))
                    gated_add(dve, st, ps[4 + (e + 1) % 2], gates[:, :, e:e + 1], x_new,
                              x_new).then_inc(acc1.sem, 1)
                st.sync()
                dve.wait_ge(acc1.sem, acc1.at(i, E))
                norm_stats(dve, st, n1, i, 5, x_new)
                norm_apply(dve, st, n1, i, 5, x_new, x_tok)
                for w in range(2):
                    dve.wait_ge(qk2_cp.sem, qk2_cp.at(i, w))
                    dve.tensor_scalar(room[1 + w][:, :], room[3 + w][:, :], 0.0, None,
                                      ALU.min).then_inc(qk2_min.sem, 1)
                for w in range(2):
                    dve.wait_ge(qk2_exp.sem, qk2_exp.at(i, w))
                    dve.scalar_tensor_tensor(out=room[1 + w][:, :], in0=room[3 + w][:, :], scalar=0.0,
                                             in1=room[5 + w][:, :], op0=ALU.max,
                                             op1=ALU.add).then_inc(qk2_f.sem, 1)
                dve.wait_ge(qk2_cp.sem, qk2_cp.at(i, 2))
                for s in range(SPB):
                    st.do(dve.memset(room[0][:, s * SEQ:s * SEQ + 1], 0.0))
                dve.wait_ge(qk2_f.sem, qk2_f.at(i, 1))

                def key_value(j):
                    dve.wait_ge(v2_mm.sem, v2_mm.at(i, j))
                    if j >= 2:
                        dve.wait_ge(sc2.sem, sc2.at(i, j - 2))
                    dve.tensor_tensor(room[11 + j % 2][:, :], ps[3 + j % 2][:, :], room[2][:, :],
                                      ALU.mult).then_inc(kv2.sem, 1)

                key_value(0)
                st.sync()
                for j in range(DH):
                    if j + 1 < DH:
                        key_value(j + 1)
                    dve.wait_ge(kv2.sem, kv2.at(i, j))
                    if j >= 2:
                        dve.wait_ge(qs2.sem, qs2.at(i, j - 2))
                    dve.tensor_tensor_scan(room[7 + j % 2][:, :], room[0][:, :], room[11 + j % 2][:, :], 0.0,
                                           ALU.mult, ALU.add).then_inc(sc2.sem, 1)
                dve.wait_ge(y2_mm.sem, y2_mm.at(i, DH - 1))
                st.do(dve.tensor_tensor(x_nf, x_tf, ps[7][:, :], ALU.add))
                st.sync()
                norm_stats(dve, st, n1, i, 6, x_new)
                norm_apply(dve, st, n1, i, 6, x_new, x_tok)
                st.do(dve.tensor_scalar(keep[:, bass.ds(i * TPB, TPB), :], x_tok[:, :, :], 1.0, None, ALU.mult))
                dve.wait_ge(r2_mm.sem, r2_mm.at(i))
                st.do(dve.tensor_tensor(score[:, :, :], ps[7][:, 0:TPB * E].rearrange("p (k e) -> p k e", e=E),
                                        rb2[:, :].unsqueeze(1).to_broadcast([P, TPB, E]), ALU.add))
                top_two(dve, st, score)
                soft_two(dve, st, top8[:, :, 0], top8[:, :, 1], d2)
                dve.wait_ge(s2.sem, s2.at(i))
                gate_sum(dve, st, gate2[:, bass.ds(i * TPB, TPB), :])
                st.do(dve.tensor_reduce(load2_b[:, :, :].rearrange("p n e -> p (n e)"),
                                        ohs[:, :, :, :].rearrange("p n t e -> p n e t"), AX_X, ALU.add))
                st.sync()
                st.do(dve.tensor_tensor(load2[:, :, :], load2[:, :, :], load2_b[:, :, :], ALU.add))
                st.sync()
                st.end()
            dve.memset(gate_scratch[:, :], 0.0).then_inc(s2_done, 1)
            dve.wait_ge(s2_done, 1)
            dve.wait_ge(fix_mm, 1)
            dve.tensor_tensor(gate2[0:E, 0, 0:2], gate2[0:E, 0, 0:2], ps[0][0:E, 0:2], ALU.add).then_inc(fixed, 1)
            dve.wait_ge(fixed, 1)
            dve.tensor_scalar(gate2[:, :, :], gate2[:, :, :], float(CAP), None, ALU.min).then_inc(fixed, 1)
            dve.wait_ge(fixed, 2)
            for g in range(2):
                for n in range(2):
                    dve.memset(st3[g][n][:, :, :], 1.0).then_inc(fixed, 1)
            dve.wait_ge(fixed, 6)
            for g in range(2):
                dve.memset(st3[g][0][:, :, 0:DH], 0.0).then_inc(state[g].sem, 1)
            dve.wait_ge(w_late, 16 * 17)
            with dve.Fori(0, NBLK) as i:
                st = Steps(dve, vstep2, i, VPER2)
                st.do(dve.tensor_scalar(gates[:, :, :], gate2[:, bass.ds(i * TPB, TPB), :], 1.0, None, ALU.mult))
                dve.tensor_scalar(x_tok[:, :, :], keep[:, bass.ds(i * TPB, TPB), :], 1.0, None, ALU.mult).then_inc(taken2.sem, 1)
                dve.wait_ge(taken2.sem, taken2.at(i))
                dve.wait_ge(bias2_mm.sem, bias2_mm.at(i))
                st.do(dve.tensor_tensor(x_nf, x_tf, ps[5][:, :], ALU.add))
                for e in range(E):
                    dve.wait_ge(dn2_mm.sem, dn2_mm.at(i, e))
                    if e >= 1:
                        dve.wait_ge(acc2.sem, acc2.at(i, e - 1))
                    gated_add(dve, st, ps[2 + e % 2], gates[:, :, e:e + 1], x_new, x_new).then_inc(acc2.sem, 1)
                st.sync()
                dve.wait_ge(acc2.sem, acc2.at(i, E - 1))
                norm_stats(dve, st, n2, i, 0, x_new)
                norm_apply(dve, st, n2, i, 0, x_new, x_tok)
                st.do(dve.tensor_scalar(keep[:, bass.ds(i * TPB, TPB), :], x_tok[:, :, :], 1.0, None, ALU.mult))
                for w in range(3):
                    dve.wait_ge(pre3.sem, pre3.at(i, w))
                    y = halves(room[6 + w][:, :])
                    st.do(dve.tensor_scalar(y, padded[w][:, :, 0:SEQ], conv3[:, w, 0:1], None, ALU.mult))
                    for k in range(1, 4):
                        st.sync()
                        last = dve.scalar_tensor_tensor(out=y, in0=padded[w][:, :, k:k + SEQ],
                                                        scalar=conv3[:, w, k:k + 1], in1=y,
                                                        op0=ALU.mult, op1=ALU.add)
                        if k < 3:
                            st.do(last)
                        else:
                            last.then_inc(conv.sem, 1)
                dve.wait_ge(ss3_mm.sem, ss3_mm.at(i))
                dve.tensor_copy(ss[:, :], ps[5][:, 0:8]).then_inc(ss3.sem, 1)
                dve.wait_ge(nr3.sem, nr3.at(i))
                dve.reciprocal(rn[:, :], nre[:, :]).then_inc(rn3.sem, 1)
                dve.wait_ge(pre3.sem, pre3.at(i, 4))
                st.do(dve.tensor_scalar(hist[3][:, bass.ds(i * BLK, BLK)], room[9][:, :], 1.0, None, ALU.mult))
                st.do(dve.scalar_tensor_tensor(out=room[8][:, :], in0=room[9][:, :],
                                               scalar=-1.0, in1=room[10][:, :], op0=ALU.mult, op1=ALU.mult))
                for w in range(2):
                    dve.wait_ge(rb3_mm.sem, rb3_mm.at(i, w))
                    last = dve.tensor_tensor(hist[w][:, bass.ds(i * BLK, BLK)], ps[6 + w][:, :],
                                             room[3 + w][:, :], ALU.mult)
                    st.do(last)
                st.sync()
                st.do(dve.tensor_tensor(hist[4][:, bass.ds(i * BLK, BLK)], hist[1][:, bass.ds(i * BLK, BLK)],
                                        room[8][:, :], ALU.mult))
                st.sync()
                dve.wait_ge(bv3.sem, bv3.at(i))
                dve.memset(gate_scratch[:, :], 0.0).then_inc(taken3.sem, 1)
                dve.wait_ge(taken3.sem, taken3.at(i))
                st.end()

            def delta_dve(i):
                st = [Steps(dve, vstep3[g], i, VPER3) for g in range(2)]
                for n in range(NSTEP):
                    h, k = n // STEPS, n % STEPS
                    if k == 0:
                        dve.wait_ge(rep_cp.sem, rep_cp.at(i, h))
                    now = [st3[g][n % 2] for g in range(2)]
                    new = [st3[g][(n + 1) % 2] for g in range(2)]
                    rows = [slice(g * HS, (g + 1) * HS) for g in range(2)]
                    for g in range(2):
                        dve.wait_ge(state[g].sem, i * NSTEP + (n + 1))
                        st[g].do(dve.tensor_tensor(prod[g][:, :, :], now[g][:, :, :],
                                                   gated_keys[h][:, k, rows[g], :], ALU.mult))
                    for g in range(2):
                        st[g].sync()
                        st[g].do(dve.tensor_reduce(uu[g][:, :], prod[g][:, :, :], AX_X, ALU.add))
                    for g in range(2):
                        st[g].sync()
                        st[g].do(dve.tensor_tensor(upd[g][:, :, :], uu[g][:, :].unsqueeze(2).to_broadcast([P, HS, DH]),
                                                   wide(h)[:, k, rows[g], :], ALU.mult))
                    for g in range(2):
                        st[g].sync()
                        dve.wait_ge(decay[g].sem, decay[g].at(i, n))
                        dve.tensor_tensor(new[g][:, :, 0:DH], upd[g][:, :, :], decayed[g][:, :, :],
                                          ALU.add).then_inc(state[g].sem, 1)
                for g in range(2):
                    st[g].end()

            with dve.Fori(0, TURNS) as i:
                delta_dve(i)
            dve.memset(gate_scratch[:, :], 0.0).then_inc(stored, 1)
            with dve.Fori(0, NBLK) as i:
                st = Steps(dve, vstep4, i, VPER4)
                dve.wait_ge(o3_tr.sem, o3_tr.at(i))
                st.do(dve.tensor_tensor(x_new[:, :, :], keep[:, bass.ds(i * TPB, TPB), :], tiles(ps[6][:, :]),
                                        ALU.add))
                st.sync()
                norm_stats(dve, st, n4, i, 0, x_new)
                norm_apply(dve, st, n4, i, 0, x_new, x_tok)
                dve.wait_ge(r3_mm.sem, r3_mm.at(i))
                dve.tensor_copy(score[:, :, :],
                                ps[7][:, 0:TPB * E].rearrange("p (k e) -> p k e", e=E)).then_inc(sig3_in.sem, 1)
                dve.wait_ge(sig3.sem, sig3.at(i))
                st.do(dve.tensor_scalar(score[:, :, :], score_r[:, :, :], col(RS3), None, ALU.mult))
                top_two(dve, st, score)
                st.do(dve.tensor_tensor(dif[:, :], top8[:, :, 0], top8[:, :, 1], ALU.add))
                st.sync()
                st.do(dve.reciprocal(dif[:, :], dif[:, :]))
                st.sync()
                for n in range(2):
                    st.do(dve.tensor_tensor(wts[:, n, :], top8[:, :, n], dif[:, :], ALU.mult))
                st.sync()
                gate_sum(dve, st, gates[:, :, :])
                st.sync()
                dve.memset(gate_scratch[:, :], 0.0).then_inc(g3.sem, 1)
                for p in range(E // 2):
                    dve.wait_ge(h3.sem, h3.at(i, p))
                    dve.wait_ge(gb3_mm.sem, gb3_mm.at(i, p))
                    dve.tensor_tensor(room[6 + p][:, :], ps[2 + p % 2][:, :], room[1 + p][:, :],
                                      ALU.mult).then_inc(hg3.sem, 1)
                dve.wait_ge(dn3_mm.sem, dn3_mm.at(i, E // 2))
                st.do(dve.tensor_tensor(x_nf, x_tf, ps[5][:, :], ALU.add))
                st.sync()
                norm_stats(dve, st, n4, i, 1, x_new)
                dve.wait_ge(stored, i * 16 + 1)
                norm_apply(dve, st, n4, i, 1, x_new, x_out[:, :, :])
                st.end()


def rope_tables():
    import numpy as np
    inv = 1.0 / 10000.0 ** (np.arange(0, DH0, 2, dtype=np.float32) / DH0)
    freqs = np.outer(np.arange(SEQ, dtype=np.float32), inv)
    cos = np.concatenate([np.cos(freqs), np.cos(freqs)], -1)[:, ::2]
    sin = np.concatenate([np.sin(freqs), np.sin(freqs)], -1)[:, ::2]
    cos_rows = np.repeat(cos.T, 2, axis=0)
    sin_rows = np.repeat(sin.T, 2, axis=0)
    sin_rows[0::2] *= -1.0
    return (np.tile(cos_rows, (2, 1)).astype(np.float32), np.tile(sin_rows, (2, 1)).astype(np.float32))


def kernel(**inputs):
    import numpy as np
    import concourse.bacc as bacc
    from concourse.bass_utils import run_bass_kernel_spmd as run

    g = {k: np.asarray(v) for k, v in inputs.items()}
    a = {}

    def rows(v):
        return np.broadcast_to(v, (P,) + v.shape)

    def column(v):
        return np.broadcast_to(v.reshape(-1, 1), (v.size, 1)) if v.size == P else rows(v.reshape(1))

    cos, sin = rope_tables()
    eye = np.eye(P, dtype=np.float32)
    head = np.arange(P) // DH
    a["x"] = g["L0_attn_x"]
    a["ident"] = eye
    a["rope_cos"], a["rope_sin"] = cos, sin
    a["iota8"] = rows(np.arange(E, dtype=np.float32))
    a["head_ones"] = (head[:, None] == head[None, :]).astype(np.float32)
    a["sel_e"] = np.stack([((head[:, None] == head[None, :]) & (np.arange(P)[:, None] % DH == e))
                           for e in range(DH)], 1).astype(np.float32)
    a["sel_pair"] = np.stack([np.arange(E)[:, None] == 2 * p + np.arange(P)[None, :] // 64
                              for p in range(E // 2)], 1).astype(np.float32)
    per_head = lambda v: np.repeat(v, DH, axis=0)
    cols = [g["L0_attn_ln_scale"], g["L0_attn_ln_bias"], g["L0_ffn_norm_scale"], g["L1_attn_bq"], g["L1_attn_bk"],
            g["L1_attn_bv"], per_head(g["L2_attn_bg"]), g["L3_attn_bq"], g["L3_attn_bk"], g["L3_attn_bv"],
            per_head(g["L3_attn_ba"]), per_head(g["L3_attn_bb"]), g["L3_attn_bo"],
            np.concatenate([g["L3_ffn_bs1"], g["L3_ffn_bs1"]]),
            np.broadcast_to(g["L3_ffn_route_scale"], (P,))]
    cols += [np.zeros(P, np.float32)] * (24 - len(cols))
    a["cols"] = np.stack(cols, 1)
    a["wd0"] = np.concatenate([g["L0_attn_w_down_q"].T, g["L0_attn_w_down_kv"].T], 1)
    a["wup0"] = np.concatenate([g["L0_attn_w_up_q"].T, g["L0_attn_w_up_k"].T], 0)
    a["wv0"] = g["L0_attn_w_up_v"].reshape(PAIRS, P, RANK0).transpose(1, 0, 2).reshape(P, PAIRS * RANK0)
    wo = g["L0_attn_w_out"].T.reshape(PAIRS, P, D).transpose(1, 0, 2)
    a["wo0a"], a["wo0b"] = wo[:, 0:4].reshape(P, -1), wo[:, 4:8].reshape(P, -1)
    a["wr0"] = g["L0_ffn_w_router"].T
    a["up0"] = g["L0_ffn_w_up"].reshape(E, CH0, P, D).transpose(3, 0, 1, 2)
    a["dn0"] = g["L0_ffn_w_down"].reshape(E, D, 2, P).transpose(3, 0, 2, 1)
    a["w1a"] = np.stack([g["L1_attn_Wq"], g["L1_attn_Wk"], g["L1_attn_Wv"], g["L1_attn_Wo"]], 1)
    a["bo1"] = rows(g["L1_attn_bo"])
    a["wr1"] = g["L1_ffn_centroids"].T
    a["rb1"] = rows(g["L1_ffn_routing_bias"])
    up1 = np.concatenate([g["L1_ffn_Wfc_sh"], g["L1_ffn_Wfc_r"]], 0)
    dn1 = np.concatenate([g["L1_ffn_Wproj_sh"], g["L1_ffn_Wproj_r"]], 0)
    a["up1"] = up1.reshape(E + NSH, CH1, P, D).transpose(3, 0, 1, 2)
    a["dn1"] = dn1.reshape(E + NSH, D, CH1, P).transpose(3, 0, 2, 1)
    a["w2a"] = np.stack([g["L2_attn_Wq"].T, g["L2_attn_Wk"].T], 1)
    a["wv2"] = np.repeat(g["L2_attn_Wv"].T.reshape(D, P // DH, DH).transpose(0, 2, 1), DH, axis=2)
    a["wg2"] = per_head(g["L2_attn_Wg"]).T
    spread = lambda w: np.stack([np.repeat(w.T.reshape(P // DH, DH, D)[:, j], DH, axis=0) for j in range(DH)], 1)
    a["wo2"] = spread(g["L2_attn_Wo"])
    a["wr2"], a["rb2"] = g["L2_ffn_router_w"], rows(g["L2_ffn_router_b"])
    a["up2"] = g["L2_ffn_w1"].transpose(1, 0, 2)
    a["dn2"] = g["L2_ffn_w2"].transpose(1, 0, 2)
    a["b1_2"], a["b2_2"] = g["L2_ffn_b1"].T, g["L2_ffn_b2"]
    a["w3a"] = np.stack([g["L3_attn_Wq"].T, g["L3_attn_Wk"].T, g["L3_attn_Wv"].T], 1)
    a["wab3"] = np.stack([per_head(g["L3_attn_Wa"]).T, per_head(g["L3_attn_Wb"]).T], 1)
    a["conv3"] = np.stack([g["L3_attn_conv_q"][:, 0], g["L3_attn_conv_k"][:, 0], g["L3_attn_conv_v"][:, 0]], 1)
    a["wo3"] = spread(g["L3_attn_Wo"])
    a["wr3"] = g["L3_ffn_gate_W"]
    a["up3"] = g["L3_ffn_W1"].reshape(E // 2, 2, D, 64).transpose(2, 0, 1, 3)
    a["dn3"] = g["L3_ffn_W2"].reshape(E // 2, P, D).transpose(1, 0, 2)
    a["b1_3"] = g["L3_ffn_b1"].reshape(E // 2, P).T
    a["b2_3"] = np.concatenate([g["L3_ffn_b2"], g["L3_ffn_bs2"][None]], 0)
    a["ws1_3"], a["ws2_3"] = g["L3_ffn_Ws1"], g["L3_ffn_Ws2"]

    nc = bacc.Bacc("TRN2", target_bir_lowering=False, num_devices=1)
    t, arrays = {}, {}
    for name, v in a.items():
        if name == "up3":
            v = v.reshape(D, E // 2, P)
        v = np.ascontiguousarray(v)
        arrays["in_" + name] = v
        t[name] = nc.dram_tensor("in_" + name, v.shape, F32, kind="ExternalInput").ap()
    out = nc.dram_tensor("out", (SEQS, SEQ, D), F32, kind="ExternalOutput").ap()
    build(nc, t, out)
    return run(nc, [arrays], core_ids=[0]).results[0]["out"]
```

```python
from contextlib import ExitStack

import concourse.bass as bass
from concourse import mybir
from concourse.alu_op_type import AluOpType as ALU

F32 = mybir.dt.float32
F16 = mybir.dt.float16
U32 = mybir.dt.uint32
ACT = mybir.ActivationFunctionType
AX_X = mybir.AxisListType.X

P = 128
D = 128
SEQS, SEQ = 16, 256
TOK = SEQS * SEQ
BLK = 512
TPB = BLK // P
NBLK = TOK // BLK
SPB = BLK // SEQ
E = 8
HEADS0, DH0, RANK0 = 16, 64, 64
PAIRS = HEADS0 // 2
UNITS = PAIRS * 2 * SPB
DH = 8
CH0 = 4
CH1 = 4
NSH = 2
CAP = max(int(TOK * 1.25 / E), 4)
STEPS = 8
CPT = 2
TURNS = SEQ // (STEPS * CPT)
NSTEP = STEPS * CPT
LN_EPS = 1e-5
UNIT_FILL = (0, 1, 1, 1)
NORM_FILL = (24, 30, 18, 16, 18, 16)
TURNED_FILL = 4
SCAN_FILL = 14
RMS_EPS = 1e-6
L2_EPS = 1e-6
NEG = -1.0e30


VPER1, VPER2, VPER3, VPER4 = 249, 49, 48, 39
PPER1, PPER2, PPER4 = 7, 2, 2


class Count:

    def __init__(self, sem, per=1):
        self.sem, self.per = sem, per

    def at(self, turn, n=0):
        return turn * self.per + (n + 1)


class Steps:

    def __init__(self, eng, sem, turn, per):
        self.eng, self.sem, self.turn, self.per, self.n = eng, sem, turn, per, 0

    def do(self, instruction):
        instruction.then_inc(self.sem, 1)
        self.n += 1

    def sync(self):
        self.eng.wait_ge(self.sem, self.turn * self.per + self.n)

    def end(self):
        assert self.n == self.per, (self.n, self.per)


def build(nc, t, out):
    with ExitStack() as ctx:
        def sb(name, shape, dt=F32):
            return ctx.enter_context(nc.sbuf_tensor(name, shape, dt))

        def sem(name):
            return ctx.enter_context(nc.semaphore(name))

        ident = sb("ident", [P, P])
        rope_sin = sb("rope_sin", [P, SEQ])
        head_ones = sb("head_ones", [P, P])
        iota8 = sb("iota8", [P, E])
        sel_pair = sb("sel_pair", [E, E // 2, P])
        cols = sb("cols", [P, 24])
        wd0 = sb("wd0", [P, P])
        big1 = sb("big1", [P, CPT * STEPS * SEQS * (DH + 1)])
        wup0 = big1[:, 0:HEADS0 * DH0]
        vo0 = big1[:, HEADS0 * DH0:2 * HEADS0 * DH0].rearrange("p (a m) -> p a m", a=PAIRS)
        rope_cos = big1[:, 2 * HEADS0 * DH0:2 * HEADS0 * DH0 + SEQ]
        gated_keys = [big1[:, h * STEPS * SEQS * (DH + 1):(h + 1) * STEPS * SEQS * (DH + 1)]
                      .rearrange("p (t b e) -> p t b e", t=STEPS, b=SEQS) for h in range(CPT)]
        wr0 = sb("wr0", [P, E])
        big0 = sb("big0", [P, 5 * TOK])

        def parts(o, e, c):
            both = big0[:, o:o + e * c * P].bitcast(F16)
            return [both[:, n * e * c * P:(n + 1) * e * c * P].rearrange("p (e c m) -> p e c m", e=e, c=c)
                    for n in range(2)]

        up0 = parts(0, E, CH0)
        o = E * CH0 * P
        dn0 = parts(o, E, 2)
        o += E * 2 * P
        NE1 = E + NSH
        up1 = parts(o, NE1, CH1)
        o += NE1 * CH1 * P
        dn1 = parts(o, NE1, CH1)
        o += NE1 * CH1 * P
        up0_raw = big0[:, o:o + E * CH0 * P]
        dn0_raw = big0[:, o:o + E * 2 * P]
        assert o + E * CH0 * P <= 5 * TOK
        hist = [big0[:, n * TOK:(n + 1) * TOK] for n in range(5)]
        w1a = sb("w1a", [P, 4, P])
        bo1 = sb("bo1", [P, P])
        wr1 = sb("wr1", [P, E])
        rb1 = sb("rb1", [P, E])
        w2a = sb("w2a", [P, 2, P])
        wv2 = sb("wv2", [P, DH, P])
        wg2 = sb("wg2", [P, P])
        wo2 = sb("wo2", [P, DH, P])
        wr2 = sb("wr2", [P, E])
        rb2 = sb("rb2", [P, E])
        up2 = sb("up2", [P, E, P])
        dn2 = sb("dn2", [P, E, P])
        b1_2 = sb("b1_2", [P, E])
        b2_2 = sb("b2_2", [E, P])
        w3a = sb("w3a", [P, 3, P])
        wab3 = sb("wab3", [P, 2, P])
        conv3 = sb("conv3", [P, 3, 4])
        wo3 = sb("wo3", [P, DH, P])
        wr3 = sb("wr3", [P, E])
        up3 = sb("up3", [P, E // 2, P])
        dn3 = sb("dn3", [P, E // 2, P])
        b1_3 = sb("b1_3", [P, E // 2])
        b2_3 = sb("b2_3", [E + 1, P])
        ws1_3 = sb("ws1_3", [P, 64])
        ws2_3 = sb("ws2_3", [64, P])
        sel_e = sb("sel_e", [P, DH, P])

        LNS, LNB, RMSW, BQ1, BK1, BV1, BG2, BQ3, BK3, BV3, BA3, BB3, BO3, BS3, RS3 = range(15)

        def col(n):
            return cols[:, n:n + 1]

        x_tok = sb("x_tok", [P, TPB, P])
        x_new = sb("x_new", [P, TPB, P])
        x_t = sb("x_t", [P, BLK])
        x_in = sb("x_in", [P, TPB, P])
        x_out = sb("x_out", [P, TPB, P])
        x_parts = x_out[:, :, :].rearrange("p t m -> p (t m)").bitcast(F16)
        x_h, x_l = x_parts[:, 0:BLK], x_parts[:, BLK:2 * BLK]
        keep = sb("keep", [P, TOK // P, P])
        gate2 = sb("gate2", [P, TOK // P, E])
        stats = sb("stats", [P, TPB, 6])
        mv = sb("mv", [P, TPB, 2])
        vare = sb("vare", [P, TPB])
        rstd = sb("rstd", [P, TPB])
        eps_ln = sb("eps_ln", [P, TPB])
        eps_rms = sb("eps_rms", [P, TPB])
        mhalf = sb("mhalf", [P, 8])
        phalf = sb("phalf", [P, 8])
        ones = sb("ones", [P, 1])
        euler = sb("euler", [P, TPB])
        table_scratch = sb("table_scratch", [P, 8])
        gate_scratch = sb("gate_scratch", [P, 1])
        score = sb("score", [P, TPB, E])
        score_r = sb("score_r", [P, TPB, E])
        top8 = sb("top8", [P, TPB, E])
        top8i = sb("top8i", [P, TPB, E], U32)
        top8f = sb("top8f", [P, TPB, 2])
        oh = sb("oh", [P, 2, TPB, E])
        ohs = sb("ohs", [P, 2, TPB, E])
        two = sb("two", [P, 2, TPB])
        dif = sb("dif", [P, TPB])
        wts = sb("wts", [P, 2, TPB])
        gates = sb("gates", [P, TPB, E])
        wides = [sb(f"wide{n}", [P, 2 * BLK]) for n in range(8)]
        room = [wides[n // 2][:, (n % 2) * BLK:(n % 2 + 1) * BLK] for n in range(16)]

        up1_raw = wides[8 - NE1 // 2:]
        keep_f = keep[:, :, :].rearrange("p k m -> p (k m)")
        dn1_raw = [keep_f[:, n * 2 * CH1 * P:(n + 1) * 2 * CH1 * P] for n in range(E // 2)] + [wides[2][:, :]]
        assert len(dn1_raw) == NE1 // 2 and 8 - NE1 // 2 > 2

        ps = [ctx.enter_context(nc.psum_tensor(f"ps{n}", [P, BLK], F32)) for n in range(8)]

        def tiles(ap):
            return ap.rearrange("p (t m) -> p t m", t=TPB)

        def halves(ap):
            return ap.rearrange("p (s q) -> p s q", s=2)

        loaded_x = Count(sem("loaded_x"))
        w_small = sem("w_small")
        w_up = [sem(f"w_up{n}") for n in range(1 + (E + NSH) // 2)]
        w_dn = [sem(f"w_dn{n}") for n in range(1 + (E + NSH) // 2)]
        w_late = sem("w_late")
        consts = sem("consts")
        vo_mm = sem("vo_mm")
        vo_done = sem("vo_done")
        x_taken = Count(sem("x_taken"))
        high_done, split_done, pool_split = sem("high_done"), sem("split_done"), sem("pool_split")

        class Norms:
            def __init__(self, tag, calls, turned):
                self.var = Count(sem(tag + "_var"), calls)
                self.rstd = Count(sem(tag + "_rstd"), calls)
                self.x = Count(sem(tag + "_x"), calls * TPB)
                self.tr = Count(sem(tag + "_tr"), turned)
                self.xt = Count(sem(tag + "_xt"), turned)

        def norm_stats(dve, st, nm, i, c, src):
            for k in range(TPB):
                st.do(dve.bn_stats(stats[:, k, :], src[:, k, :]))
            st.sync()
            st.do(dve.memset(gate_scratch[:, :], 0.0))
            for k in range(TPB):
                last = dve.bn_aggr(mv[:, k, :], stats[:, k, :])
                if k < TPB - 1:
                    st.do(last)
                else:
                    last.then_inc(nm.var.sem, 1)

        def rms_stats(dve, st, nm, i, c, src, sq):
            for k in range(TPB):
                last = dve.tensor_tensor_reduce(out=sq[:, k, :], in0=src[:, k, :], in1=src[:, k, :],
                                                scale=1.0 / D, scalar=0.0, op0=ALU.mult, op1=ALU.add,
                                                accum_out=mv[:, k, 1:2])
                if k < TPB - 1:
                    st.do(last)
                else:
                    last.then_inc(nm.var.sem, 1)

        def norm_rstd(pool, st, nm, i, c, eps):
            pool.wait_ge(nm.var.sem, nm.var.at(i, c))
            st.do(pool.tensor_tensor(vare[:, :], mv[:, :, 1], eps[:, :], ALU.add))
            st.sync()
            pool.tensor_tensor(rstd[:, :], vare[:, :], mhalf[:, 0:TPB], ALU.pow).then_inc(nm.rstd.sem, 1)

        def norm_apply(dve, st, nm, i, c, src, dst, centre=True):
            dve.wait_ge(nm.var.sem, nm.var.at(i, c))
            dve.wait_ge(nm.rstd.sem, nm.rstd.at(i, c))
            for k in range(TPB):
                if centre:
                    last = dve.tensor_scalar(dst[:, k, :], src[:, k, :], mv[:, k, 0:1], rstd[:, k:k + 1],
                                             ALU.subtract, ALU.mult)
                else:
                    last = dve.tensor_scalar(dst[:, k, :], src[:, k, :], rstd[:, k:k + 1], None, ALU.mult)
                last.then_inc(nm.x.sem, 1)
            dve.wait_ge(nm.x.sem, nm.x.at(i, TPB * c + TPB - 1))

        def norm_transpose(pe, nm, i, c, r, src, bank):
            if nm is n1:
                keep_warm(pe, bank, NORM_FILL[r])
            elif nm is n2:
                keep_warm_32(pe, bank, 5)
            else:
                keep_warm_32(pe, ps[3], 9)
            for k in range(TPB):
                pe.wait_ge(nm.x.sem, nm.x.at(i, TPB * c + k))
                last = pe.transpose(bank[:, k * P:(k + 1) * P], src[:, k, :], ident[:, :])
            last.then_inc(nm.tr.sem, 1)
            if nm is n1:
                keep_warm(pe, ps[7], TURNED_FILL)
            else:
                keep_warm_32(pe, ps[7], 1)

        def load_table(act, n, function):
            act.activation(table_scratch[:, n:n + 1], ones[:, :], function)

        def norm_copy(act, nm, i, r, dst, bank, scale=None, bias=None):
            act.wait_ge(nm.tr.sem, nm.tr.at(i, r))
            if scale is None:
                last = act.activation(dst[:, :], bank[:, :], ACT.Copy)
            else:
                last = act.activation(dst[:, :], bank[:, :], ACT.Identity, scale=scale,
                                      bias=0.0 if bias is None else bias)
            last.then_inc(nm.xt.sem, 1)

        def raw_parts():
            flat = lambda v: v.rearrange("p e c m -> p (e c m)")
            yield w_up[0], up0_raw, flat(up0[0]), flat(up0[1])
            for raws, arrived, w in ((up1_raw, w_up[1:], up1), (dn1_raw, w_dn[1:], dn1)):
                for n, raw in enumerate(raws):
                    two_e = slice(2 * n, 2 * n + 2)
                    yield arrived[n], raw[:, :], flat(w[0][:, two_e]), flat(w[1][:, two_e])
            yield w_dn[0], dn0_raw, flat(dn0[0]), flat(dn0[1])

        RAWS, POOL_RAWS = 2 + 2 * (NE1 // 2), 3

        def by_pool(n):
            return 1 <= n <= POOL_RAWS

        def hidden_parts(n):
            both = room[n].bitcast(F16)
            return both[:, 0:BLK], both[:, BLK:2 * BLK]

        def split_down(pe, bank, n, w, first, last_chunk, high, low):
            h_h, h_l = hidden_parts(n)
            pe.wait_ge(*high)
            for k in range(TPB):
                for m in range(2):
                    pe.matmul(bank[:, k * P:(k + 1) * P], h_h[:, k * P:(k + 1) * P], w[m],
                              start=(first and k == 0 and m == 0), stop=False, skip_group_check=True)
            pe.wait_ge(*low)
            for k in range(TPB):
                last = pe.matmul(bank[:, k * P:(k + 1) * P], h_l[:, k * P:(k + 1) * P], w[0],
                                 start=False, stop=last_chunk, skip_group_check=True)
            return last

        def low_1_done(i, n):
            if n < CH1:
                return h1_first.sem, h1_first.at(i, n)
            return h1_l[n % 2].sem, h1_l[n % 2].at(i, (n - CH1) // 2)

        def low_1(eng, i, x, odd):
            for n in range(CH1 * x + odd, CH1 * (x + 1), 2) if x else range(CH1):
                eng.wait_ge(h1.sem, h1.at(i, n))
                high, low = hidden_parts(n % (2 * CH1))
                if n < CH1 * x + 2 and x >= 2:
                    eng.wait_ge(dn1_mm.sem, dn1_mm.at(i, x - 2))
                eng.tensor_tensor(low, room[8 + n % 4][:, :], high, ALU.subtract).then_inc(low_1_done(i, n)[0], 1)

        def high_x(act, i, c):
            act.wait_ge(n1.xt.sem, n1.xt.at(i, 1 if c == 0 else 3))
            act.activation(x_h[:, :], x_t[:, :], ACT.Copy).then_inc(xh.sem, 1)

        def low_x(dve, i, c):
            dve.wait_ge(xh.sem, xh.at(i, c))
            dve.tensor_tensor(x_l[:, :], x_t[:, :], x_h[:, :], ALU.subtract).then_inc(xl.sem, 1)

        def split_mm(pe, bank, w, e, c, i, call, first):
            if first:
                pe.wait_ge(xh.sem, xh.at(i, call))
            pe.matmul(bank[:, :], w[0][:, e, c, :], x_h[:, :], start=True, stop=False)
            pe.matmul(bank[:, :], w[1][:, e, c, :], x_h[:, :], start=False, stop=False)
            if first:
                pe.wait_ge(xl.sem, xl.at(i, call))
            return pe.matmul(bank[:, :], w[0][:, e, c, :], x_l[:, :], start=False, stop=True)

        def keep_warm(pe, bank, count):
            for _ in range(count):
                pe.matmul(bank[:, :], up0[0][:, 0, 0, :], up0[0][:, 0, :, :], start=True, stop=True)

        def keep_warm_32(pe, bank, count):
            for _ in range(count):
                pe.matmul(bank[:, :], ident[:, :], sel_e[:, 0:4, :], start=True, stop=True)

        def router_mm(pe, src_t, w, bank, done):
            for k in range(TPB):
                last = pe.matmul(bank[:, k * E:(k + 1) * E], src_t[:, k * P:(k + 1) * P], w[:, :],
                                 start=True, stop=True)
            last.then_inc(done.sem, 1)

        def top_two(dve, st, src):
            st.sync()
            st.do(dve.memset(gate_scratch[:, :], 0.0))
            for k in range(TPB):
                st.do(dve.max(top8[:, k, :], src[:, k, :]))
            st.sync()
            st.do(dve.memset(gate_scratch[:, :], 0.0))
            for k in range(TPB):
                st.do(dve.max_index(top8i[:, k, :], top8[:, k, :], src[:, k, :]))
            st.sync()
            st.do(dve.tensor_copy(top8f[:, :, :], top8i[:, :, 0:2]))
            st.sync()
            for n in range(2):
                st.do(dve.tensor_tensor(oh[:, n, :, :], iota8[:, :].unsqueeze(1).to_broadcast([P, TPB, E]),
                                        top8f[:, :, n:n + 1].to_broadcast([P, TPB, E]), ALU.is_equal))

        def pick_two(dve, st, src):
            st.sync()
            for n in range(2):
                st.do(dve.tensor_tensor(ohs[:, n, :, :], oh[:, n, :, :], src[:, :, :], ALU.mult))
            st.sync()
            st.do(dve.tensor_reduce(two[:, :, :].rearrange("p n t -> p (n t)"),
                                    ohs[:, :, :, :].rearrange("p n t e -> p (n t) e"), AX_X, ALU.add))

        def soft_two(dve, st, first, second, done):
            st.sync()
            dve.tensor_tensor(dif[:, :], first, second, ALU.subtract).then_inc(done.sem, 1)

        def soft_act(act, i, dif_done, done):
            act.wait_ge(dif_done.sem, dif_done.at(i))
            act.activation(wts[:, 0, :], dif[:, :], ACT.Sigmoid)
            act.activation(wts[:, 1, :], dif[:, :], ACT.Sigmoid, scale=-1.0).then_inc(done.sem, 1)

        def soft_in(dve, st, first, second, done):
            st.sync()
            dve.tensor_tensor(dif[:, :], second, first, ALU.subtract).then_inc(done.sem, 1)

        def soft_pool(pool, i, dif_done, done):
            pool.wait_ge(dif_done.sem, dif_done.at(i))
            pool.tensor_tensor(wts[:, 1, :], euler[:, 0:TPB], dif[:, :], ALU.pow).then_inc(done.sem, 1)

        def soft_out(dve, st, i, done):
            dve.wait_ge(done.sem, done.at(i))
            st.do(dve.tensor_scalar(dif[:, :], wts[:, 1, :], 1.0, None, ALU.add))
            st.sync()
            st.do(dve.reciprocal(wts[:, 0, :], dif[:, :]))
            st.sync()
            st.do(dve.tensor_tensor(wts[:, 1, :], wts[:, 1, :], wts[:, 0, :], ALU.mult))
            st.sync()

        def gate_sum(dve, st, dst):
            for n in range(2):
                st.do(dve.tensor_tensor(ohs[:, n, :, :], oh[:, n, :, :],
                                        wts[:, n, :].unsqueeze(2).to_broadcast([P, TPB, E]), ALU.mult))
            st.sync()
            st.do(dve.tensor_tensor(dst, ohs[:, 0, :, :], ohs[:, 1, :, :], ALU.add))

        def gated_add(dve, st, y, gate, src, dst):
            st.sync()
            for k in range(TPB):
                last = dve.scalar_tensor_tensor(out=dst[:, k, :], in0=y[:, k * P:(k + 1) * P],
                                                scalar=gate[:, k, :], in1=src[:, k, :],
                                                op0=ALU.mult, op1=ALU.add)
                if k < TPB - 1:
                    st.do(last)
            return last

        n1 = Norms("n1", 7, 6)
        xh, xl = Count(sem("xh"), 2), Count(sem("xl"), 2)
        c_mm, c_cp = Count(sem("c_mm")), Count(sem("c_cp"))
        qk_mm = Count(sem("qk_mm"), 2 * PAIRS)
        qk_cp = Count(sem("qk_cp"), 2 * PAIRS)
        qk_cos = Count(sem("qk_cos"), 2 * PAIRS)
        qk_swap = Count(sem("qk_swap"), 2 * PAIRS)
        qk_sin = Count(sem("qk_sin"), 2 * PAIRS)
        qk_rot = Count(sem("qk_rot"), 2 * PAIRS)
        sc_mm = Count(sem("sc_mm"), UNITS)
        sc_max = Count(sem("sc_max"), UNITS)
        pr_exp = Count(sem("pr_exp"), UNITS)
        pr_norm = Count(sem("pr_norm"), UNITS)
        pt_mm = Count(sem("pt_mm"), UNITS)
        pt_cp = Count(sem("pt_cp"), UNITS)
        pv_mm = Count(sem("pv_mm"), UNITS)
        ov_cp = Count(sem("ov_cp"), PAIRS)
        y0_mm = Count(sem("y0_mm"), PAIRS)
        r0_mm, d0, s0 = Count(sem("r0_mm")), Count(sem("d0")), Count(sem("s0"))
        up0_mm = Count(sem("up0_mm"), 2 * E)
        sl0 = Count(sem("sl0"), 2 * E)
        h0 = Count(sem("h0"), 2 * E)
        h0_h, h0_l = Count(sem("h0_h"), 2 * E), Count(sem("h0_l"), 2 * E)
        dn0_mm = Count(sem("dn0_mm"), E)
        acc0 = Count(sem("acc0"), E)
        qkv1_mm = Count(sem("qkv1_mm"), 3)
        qkv1_sq = Count(sem("qkv1_sq"), 2)
        qkv1_f = Count(sem("qkv1_f"), 3)
        qk1, co1_mm, ov1, y1_mm = Count(sem("qk1")), Count(sem("co1_mm")), Count(sem("ov1")), Count(sem("y1_mm"))
        r1_mm, rt1, rsig1 = Count(sem("r1_mm")), Count(sem("rt1")), Count(sem("rsig1"))
        d1, s1 = Count(sem("d1")), Count(sem("s1"))
        up1_mm = Count(sem("up1_mm"), CH1 * NE1)
        h1 = Count(sem("h1"), CH1 * NE1)
        h1_first = Count(sem("h1_first"), CH1)
        h1_l = [Count(sem(f"h1_l{v}"), CH1 * (NE1 - 1) // 2) for v in range(2)]
        dn1_mm = Count(sem("dn1_mm"), NE1)
        acc1 = Count(sem("acc1"), E + 1)
        qk2_mm = Count(sem("qk2_mm"), 3)
        qk2_cp = Count(sem("qk2_cp"), 3)
        qk2_min = Count(sem("qk2_min"), 2)
        qk2_exp = Count(sem("qk2_exp"), 2)
        qk2_f = Count(sem("qk2_f"), 2)
        v2_mm = Count(sem("v2_mm"), DH)
        kv2 = Count(sem("kv2"), DH)
        sc2 = Count(sem("sc2"), DH)
        qs2 = Count(sem("qs2"), DH)
        y2_mm = Count(sem("y2_mm"), DH)
        r2_mm, d2, s2 = Count(sem("r2_mm")), Count(sem("d2")), Count(sem("s2"))
        done1 = Count(sem("done1"))
        vstep, pstep = sem("vstep"), sem("pstep")
        
        h_t, c_t, ck = room[0], room[1], room[2]
        qa = [room[3], room[4]]
        cosm = [room[5], room[6]]
        rot = [[room[7], room[8]], [room[9], room[10]]]
        ex = [room[11], room[12]]
        pts = [room[13], room[14]]
        ovs = room[15]
        sinm = [sb(f"sinm{w}", [P, BLK]) for w in range(2)]
        mx = sb("mx", [P, 4, 2])
        nmx = sb("nmx", [P, 4, 2])
        rsum = sb("rsum", [P, 4, 2])
        rinv = sb("rinv", [P, 4, 2])

        n2 = Norms("n2", 1, 1)
        fix_mm, fixed, s2_done = sem("fix_mm"), sem("fixed"), sem("s2_done")
        taken2 = Count(sem("taken2"))
        gt2_mm, gt2, bias2_mm = Count(sem("gt2_mm")), Count(sem("gt2")), Count(sem("bias2_mm"))
        xm2 = Count(sem("xm2"), E)
        xm2_mm = Count(sem("xm2_mm"), E)
        xm2_cp = Count(sem("xm2_cp"), E)
        up2_mm = Count(sem("up2_mm"), E)
        h2 = Count(sem("h2"), E)
        dn2_mm = Count(sem("dn2_mm"), E)
        acc2 = Count(sem("acc2"), E)
        pre3_mm = Count(sem("pre3_mm"), 5)
        pre3 = Count(sem("pre3"), 5)
        conv = Count(sem("conv"), 3)
        csl = Count(sem("csl"), 3)
        sq3, ss3_mm, ss3 = Count(sem("sq3")), Count(sem("ss3_mm")), Count(sem("ss3"))
        nr3, rn3, rb3_mm = Count(sem("nr3")), Count(sem("rn3")), Count(sem("rb3_mm"), 2)
        bv3, taken3 = Count(sem("bv3")), Count(sem("taken3"))
        rep_mm = Count(sem("rep_mm"), CPT)
        rep_cp = Count(sem("rep_cp"), CPT)
        decay = [Count(sem(f"decay{g}"), NSTEP) for g in range(2)]
        state = [Count(sem(f"state{g}"), NSTEP) for g in range(2)]
        read = Count(sem("read"), NSTEP)
        o3_mm = Count(sem("o3_mm"), CPT)
        o3 = Count(sem("o3"), CPT)
        n4 = Norms("n4", 2, 1)
        o3_st, o3_tr = Count(sem("o3_st")), Count(sem("o3_tr"))
        r3_mm, sig3_in, sig3 = Count(sem("r3_mm")), Count(sem("sig3_in")), Count(sem("sig3"))
        g3, gt3_mm, gt3 = Count(sem("g3")), Count(sem("gt3_mm")), Count(sem("gt3"))
        up3_mm = Count(sem("up3_mm"), E // 2 + 1)
        h3 = Count(sem("h3"), E // 2 + 1)
        gb3_mm = Count(sem("gb3_mm"), E // 2)
        hg3 = Count(sem("hg3"), E // 2)
        dn3_mm = Count(sem("dn3_mm"), E // 2 + 1)
        stored = sem("stored")
        vstep2, vstep4 = sem("vstep2"), sem("vstep4")
        vstep3 = [sem("vstep3a"), sem("vstep3b")]
        pstep2, pstep4 = sem("pstep2"), sem("pstep4")

        padded = [sb(f"padded{w}", [P, SPB, SEQ + 3]) for w in range(3)]
        load2 = sb("load2", [P, 2, E])
        load2_b = sb("load2_b", [P, 2, E])
        gt = sb("gt", [E + 1, BLK])
        ss = sb("ss", [P, 8])
        nr = sb("nr", [P, 8])
        nre = sb("nre", [P, 8])
        rn = sb("rn", [P, 8])
        eps_l2 = sb("eps_l2", [P, 8])
        HS = SEQS // 2
        st3 = [[sb(f"st3_{g}_{n}", [P, HS, DH + 1]) for n in range(2)] for g in range(2)]
        decayed = [sb(f"decayed{g}", [P, HS, DH]) for g in range(2)]
        prod = [sb(f"prod{g}", [P, HS, DH + 1]) for g in range(2)]
        uu = [sb(f"uu{g}", [P, HS]) for g in range(2)]
        upd = [sb(f"upd{g}", [P, HS, DH]) for g in range(2)]

        def wide(n):
            return wides[n][:, :].rearrange("p (t b e) -> p t b e", t=STEPS, b=SEQS)

        block = ctx.enter_context(nc.Block())

        @block.sync
        def _(sp):
            xv = t["x"].rearrange("b s d -> (b s) d").rearrange("(k p) d -> p k d", p=P)
            sp.dma_start(x_in[:, :, :], xv[:, 0:TPB, :]).then_inc(loaded_x.sem, 16)
            for name, dst in (("ident", ident[:, :]), ("cols", cols[:, :]), ("rope_cos", rope_cos[:, :]),
                              ("rope_sin", rope_sin[:, :]), ("iota8", iota8[:, :]), ("wd0", wd0[:, :]),
                              ("wup0", wup0[:, :]), ("wv0", room[0][:, 0:PAIRS * RANK0]),
                              ("wo0a", room[1][:, :]), ("wo0b", room[2][:, :]), ("wr0", wr0[:, :]),
                              ("head_ones", head_ones[:, :]), ("w1a", w1a[:, :, :]), ("bo1", bo1[:, :]),
                              ("wr1", wr1[:, :]), ("rb1", rb1[:, :]), ("w2a", w2a[:, :, :]), ("wv2", wv2[:, :, :]),
                              ("wg2", wg2[:, :]), ("wo2", wo2[:, :, :]), ("wr2", wr2[:, :]), ("rb2", rb2[:, :])):
                sp.dma_start(dst, t[name]).then_inc(w_small, 16)
            sp.dma_start(up0_raw, t["up0"].rearrange("p e c m -> p (e c m)")).then_inc(w_up[0], 16)
            for name, raws, arrived in (("up1", up1_raw, w_up[1:]), ("dn1", dn1_raw, w_dn[1:])):
                for n, raw in enumerate(raws):
                    sp.dma_start(raw[:, :], t[name][:, 2 * n:2 * n + 2, :, :].rearrange("p e c m -> p (e c m)")
                                 ).then_inc(arrived[n], 16)
            sp.wait_ge(split_done, 1)
            sp.dma_start(dn0_raw, t["dn0"].rearrange("p e c m -> p (e c m)")).then_inc(w_dn[0], 16)
            for name, dst in (("up2", up2[:, :, :]), ("dn2", dn2[:, :, :]), ("b1_2", b1_2[:, :]),
                              ("b2_2", b2_2[:, :]), ("w3a", w3a[:, :, :]), ("wab3", wab3[:, :, :]),
                              ("conv3", conv3[:, :, :]), ("wo3", wo3[:, :, :]), ("wr3", wr3[:, :]),
                              ("up3", up3[:, :, :]), ("dn3", dn3[:, :, :]), ("b1_3", b1_3[:, :]),
                              ("b2_3", b2_3[:, :]), ("ws1_3", ws1_3[:, :]), ("ws2_3", ws2_3[:, :]),
                              ("sel_e", sel_e[:, :, :]), ("sel_pair", sel_pair[:, :, :])):
                sp.dma_start(dst, t[name]).then_inc(w_late, 16)
            with sp.Fori(0, NBLK - 1) as i:
                sp.wait_ge(x_taken.sem, x_taken.at(i))
                sp.dma_start(x_in[:, :, :], xv[:, bass.ds(i * TPB + TPB, TPB), :]).then_inc(loaded_x.sem, 16)
            ov = out.rearrange("b s d -> (b s) d").rearrange("(k p) d -> p k d", p=P)
            with sp.Fori(0, NBLK) as i:
                sp.wait_ge(n4.x.sem, n4.x.at(i, 2 * TPB - 1))
                sp.dma_start(ov[:, bass.ds(i * TPB, TPB), :], x_out[:, :, :]).then_inc(stored, 16)
            sp.wait_ge(stored, 16 * NBLK + 1)

        @block.gpsimd
        def _(pool):
            for buf, value in ((eps_ln, LN_EPS), (eps_rms, RMS_EPS), (mhalf, -0.5), (phalf, 0.5), (ones, 1.0),
                               (euler, 2.718281828459045)):
                pool.memset(buf[:, :], value).then_inc(consts, 1)
            pool.memset(eps_l2[:, :], L2_EPS).then_inc(consts, 1)
            for w in range(3):
                pool.memset(padded[w][:, :, :], 0.0).then_inc(consts, 1)
            pool.memset(gt[:, :], 1.0).then_inc(consts, 1)
            pool.memset(load2[:, :, :], 0.0).then_inc(consts, 1)
            pool.wait_ge(consts, 12)
            for n, (_, raw, high, low) in enumerate(raw_parts()):
                if by_pool(n):
                    pool.wait_ge(high_done, n + 1)
                    pool.tensor_tensor(low, raw, high, ALU.subtract).then_inc(pool_split, 1)
            pool.wait_ge(w_small, 16 * 22)
            with pool.Fori(0, NBLK) as i:
                st = Steps(pool, pstep, i, PPER1)
                norm_rstd(pool, st, n1, i, 0, eps_ln)
                for p in range(PAIRS):
                    for w in range(2):
                        n = 2 * p + w
                        pool.wait_ge(qk_cp.sem, qk_cp.at(i, n))
                        if n >= 2:
                            pool.wait_ge(qk_rot.sem, qk_rot.at(i, n - 2))
                        pool.tensor_tensor(halves(cosm[w][:, :]), halves(qa[w][:, :]),
                                           rope_cos[:, :].unsqueeze(1).to_broadcast([P, SPB, SEQ]),
                                           ALU.mult).then_inc(qk_cos.sem, 1)
                        if p >= 1:
                            pool.wait_ge(qk_swap.sem, qk_swap.at(i, n))
                            pool.tensor_tensor(halves(sinm[w][:, :]), halves(sinm[w][:, :]),
                                               rope_sin[:, :].unsqueeze(1).to_broadcast([P, SPB, SEQ]),
                                               ALU.mult).then_inc(qk_sin.sem, 1)
                norm_rstd(pool, st, n1, i, 1, eps_ln)
                norm_rstd(pool, st, n1, i, 2, eps_rms)
                soft_pool(pool, i, d0, s0)
                for n in range(2 * E):
                    pool.wait_ge(h0.sem, h0.at(i, n))
                    pool.wait_ge(h0_h.sem, h0_h.at(i, n))
                    if n >= 4:
                        pool.wait_ge(dn0_mm.sem, dn0_mm.at(i, n // 2 - 2))
                    pool.tensor_tensor(hidden_parts(2 + n % 4)[1], room[8 + n % 4][:, :],
                                       hidden_parts(2 + n % 4)[0], ALU.subtract).then_inc(h0_l.sem, 1)
                norm_rstd(pool, st, n1, i, 3, eps_ln)
                norm_rstd(pool, st, n1, i, 4, eps_ln)
                low_1(pool, i, 0, 1)
                soft_pool(pool, i, d1, s1)
                for x in range(1, NE1):
                    low_1(pool, i, x, 1)
                norm_rstd(pool, st, n1, i, 5, eps_ln)
                q2, sc = room[1], [room[7], room[8]]
                qsb = [room[9], room[10]]
                pool.wait_ge(qk2_f.sem, qk2_f.at(i, 0))
                for j in range(DH):
                    pool.wait_ge(sc2.sem, sc2.at(i, j))
                    if j >= 2:
                        pool.wait_ge(y2_mm.sem, y2_mm.at(i, j - 2))
                    pool.tensor_tensor(qsb[j % 2][:, :], sc[j % 2][:, :], q2[:, :], ALU.mult).then_inc(qs2.sem, 1)
                norm_rstd(pool, st, n1, i, 6, eps_ln)
                st.end()
            with pool.Fori(0, NBLK) as i:
                st = Steps(pool, pstep2, i, PPER2)
                pool.wait_ge(taken2.sem, taken2.at(i))
                for e in range(E):
                    if e >= 2:
                        pool.wait_ge(xm2_mm.sem, xm2_mm.at(i, e - 2))
                    pool.tensor_tensor(tiles(room[e % 2][:, :]), x_tok[:, :, :],
                                       gates[:, :, e:e + 1].to_broadcast([P, TPB, P]),
                                       ALU.mult).then_inc(xm2.sem, 1)
                norm_rstd(pool, st, n2, i, 0, eps_ln)
                pool.wait_ge(ss3.sem, ss3.at(i))
                st.do(pool.tensor_tensor(nr[:, :], ss[:, :], phalf[:, :], ALU.pow))
                st.sync()
                pool.tensor_tensor(nre[:, :], nr[:, :], eps_l2[:, :], ALU.add).then_inc(nr3.sem, 1)
                pool.wait_ge(csl.sem, csl.at(i, 2))
                pool.wait_ge(pre3.sem, pre3.at(i, 4))
                pool.tensor_tensor(hist[2][:, bass.ds(i * BLK, BLK)], room[5][:, :], room[10][:, :],
                                   ALU.mult).then_inc(bv3.sem, 1)
                st.end()

            def per_seq(n, t, g):
                v = hist[n].rearrange("p (b t) -> p b t", b=SEQS)[:, g * HS:(g + 1) * HS, bass.ds(t, 1)]
                return v.to_broadcast([P, HS, DH])

            def read_out(i, n):
                h, k = n // STEPS, n % STEPS
                for g in range(2):
                    last = pool.tensor_tensor(wide(4 + h)[:, k, g * HS:(g + 1) * HS, :],
                                              st3[g][(n + 1) % 2][:, :, 0:DH],
                                              per_seq(0, i * NSTEP + n, g), ALU.mult)
                last.then_inc(read.sem, 1)

            def delta_pool(i):
                for n in range(NSTEP):
                    for g in range(2):
                        pool.wait_ge(state[g].sem, i * NSTEP + (n + 1))
                        pool.tensor_tensor(decayed[g][:, :, :], st3[g][n % 2][:, :, 0:DH],
                                           per_seq(3, i * NSTEP + n, g), ALU.mult).then_inc(decay[g].sem, 1)
                    if n >= 1:
                        read_out(i, n - 1)
                for g in range(2):
                    pool.wait_ge(state[g].sem, i * NSTEP + (NSTEP + 1))
                read_out(i, NSTEP - 1)

            pool.wait_ge(taken3.sem, NBLK)
            with pool.Fori(0, TURNS) as i:
                delta_pool(i)
            with pool.Fori(0, NBLK) as i:
                st = Steps(pool, pstep4, i, PPER4)
                for c in range(2):
                    norm_rstd(pool, st, n4, i, c, eps_ln)
                st.end()

        @block.scalar
        def _(act):
            act.wait_ge(w_small, 16 * 22)
            act.wait_ge(consts, 12)
            act.wait_ge(vo_mm, 1)
            act.activation(vo0[:, 0:4, :].rearrange("p a m -> p (a m)"), ps[0][:, :], ACT.Copy).then_inc(vo_done, 1)
            act.activation(vo0[:, 4:8, :].rearrange("p a m -> p (a m)"), ps[1][:, :], ACT.Copy).then_inc(vo_done, 1)
            for arrived, raw, high, low in raw_parts():
                act.wait_ge(arrived, 16)
                act.activation(high, raw, ACT.Copy).then_inc(high_done, 1)
            act.wait_ge(split_done, RAWS - POOL_RAWS)
            act.wait_ge(pool_split, POOL_RAWS)
            with act.Fori(0, NBLK) as i:
                load_table(act, 0, ACT.Exp)
                norm_copy(act, n1, i, 0, h_t, ps[6], scale=col(LNS), bias=col(LNB))
                act.wait_ge(c_mm.sem, c_mm.at(i))
                act.activation(c_t[:, :], ps[7][:, :], ACT.Copy)
                act.activation(ck[:, 0:TPB * RANK0], ps[5][:, 0:TPB * RANK0], ACT.Copy).then_inc(c_cp.sem, 1)

                def copy_qk(p, w):
                    n = 2 * p + w
                    act.wait_ge(qk_mm.sem, qk_mm.at(i, n))
                    if n >= 2:
                        act.wait_ge(qk_rot.sem, qk_rot.at(i, n - 2))
                        act.wait_ge(qk_cos.sem, qk_cos.at(i, n - 2))
                    act.activation(qa[w][:, :], ps[w][:, :], ACT.Copy).then_inc(qk_cp.sem, 1)

                copy_qk(0, 0)
                copy_qk(0, 1)
                for n in range(UNITS + 6):
                    if n >= 4 and (n - 4) % 4 == 3 and n - 4 < UNITS:
                        p = (n - 4) // 4
                        act.wait_ge(pv_mm.sem, pv_mm.at(i, n - 4))
                        if p >= 1:
                            act.wait_ge(y0_mm.sem, y0_mm.at(i, p - 1))
                        act.activation(ovs[:, :], ps[6][:, :], ACT.Copy).then_inc(ov_cp.sem, 1)
                    if n < UNITS:
                        if n % 4 in (0, 1) and n // 4 + 1 < PAIRS:
                            copy_qk(n // 4 + 1, n % 4)
                        act.wait_ge(sc_max.sem, sc_max.at(i, n))
                        if n >= 2:
                            act.wait_ge(pt_mm.sem, pt_mm.at(i, n - 2))
                        for q in range(2):
                            last = act.activation(ex[n % 2][:, q * SEQ:(q + 1) * SEQ],
                                                  ps[2 + n % 2][:, q * SEQ:(q + 1) * SEQ], ACT.Exp,
                                                  bias=nmx[:, n % 4, q:q + 1], scale=float(DH0) ** -0.5,
                                                  accum_out=rsum[:, n % 4, q:q + 1])
                        last.then_inc(pr_exp.sem, 1)
                    if 0 <= n - 2 < UNITS:
                        m = n - 2
                        act.wait_ge(pt_mm.sem, pt_mm.at(i, m))
                        if m >= 2:
                            act.wait_ge(pv_mm.sem, pv_mm.at(i, m - 2))
                        act.activation(pts[m % 2][:, :], ps[4 + m % 2][:, :], ACT.Copy).then_inc(pt_cp.sem, 1)
                load_table(act, 1, ACT.Silu)
                norm_copy(act, n1, i, 1, x_t, ps[6], scale=col(RMSW))
                high_x(act, i, 0)
                for n in range(2 * E + 1):
                    if n < 2 * E:
                        act.wait_ge(up0_mm.sem, up0_mm.at(i, n))
                        if n >= 2:
                            act.wait_ge(h0.sem, h0.at(i, n - 2))
                        act.activation(room[n % 2][:, :], ps[2 * (n % 2) + 1][:, :],
                                       ACT.Silu).then_inc(sl0.sem, 1)
                    if n >= 1:
                        m = n - 1
                        act.wait_ge(h0.sem, h0.at(i, m))
                        if m >= 4:
                            act.wait_ge(dn0_mm.sem, dn0_mm.at(i, m // 2 - 2))
                        act.activation(hidden_parts(2 + m % 4)[0], room[8 + m % 4][:, :],
                                       ACT.Copy).then_inc(h0_h.sem, 1)
                load_table(act, 2, ACT.Exp)
                norm_copy(act, n1, i, 2, x_t, ps[6])
                for w, b in enumerate((BQ1, BK1)):
                    act.wait_ge(qkv1_mm.sem, qkv1_mm.at(i, w))
                    act.activation(room[w][:, :], ps[w][:, :], ACT.Square, bias=col(b)).then_inc(qkv1_sq.sem, 1)
                act.wait_ge(qkv1_sq.sem, qkv1_sq.at(i, 1))
                for w in range(2):
                    act.activation(room[2 + w][:, :], room[w][:, :], ACT.Exp, scale=-0.5).then_inc(qkv1_f.sem, 1)
                act.wait_ge(qkv1_mm.sem, qkv1_mm.at(i, 2))
                act.activation(room[4][:, :], ps[2][:, :], ACT.Identity, bias=col(BV1)).then_inc(qkv1_f.sem, 1)
                load_table(act, 3, ACT.Sigmoid)
                norm_copy(act, n1, i, 3, x_t, ps[6])
                high_x(act, i, 1)
                act.wait_ge(rt1.sem, rt1.at(i))
                act.activation(score_r[:, :, :], score_r[:, :, :], ACT.Sigmoid)
                act.activation(score[:, :, :], score[:, :, :], ACT.Sigmoid).then_inc(rsig1.sem, 1)

                def gelu_1(x):
                    for n in range(CH1 * x, CH1 * (x + 1)):
                        act.wait_ge(up1_mm.sem, up1_mm.at(i, n))
                        if x >= 2 and n % CH1 == 0:
                            act.wait_ge(dn1_mm.sem, dn1_mm.at(i, x - 2))
                        if n >= 4:
                            act.wait_ge(*low_1_done(i, n - 4))
                        act.activation(room[8 + n % 4][:, :], ps[n % 4][:, :], ACT.Gelu)
                        act.activation(hidden_parts(n % (2 * CH1))[0], ps[n % 4][:, :],
                                       ACT.Gelu).then_inc(h1.sem, 1)

                for x in range(NE1):
                    gelu_1(x)
                load_table(act, 4, ACT.Exp)
                norm_copy(act, n1, i, 4, x_t, ps[6])
                for w in range(2):
                    act.wait_ge(qk2_mm.sem, qk2_mm.at(i, w))
                    act.activation(room[3 + w][:, :], ps[w][:, :], ACT.Copy,
                                   scale=(float(DH) ** -0.5 if w == 0 else 1.0)).then_inc(qk2_cp.sem, 1)
                for w in range(2):
                    act.wait_ge(qk2_min.sem, qk2_min.at(i, w))
                    act.activation(room[5 + w][:, :], room[1 + w][:, :], ACT.Exp).then_inc(qk2_exp.sem, 1)
                act.wait_ge(qk2_mm.sem, qk2_mm.at(i, 2))
                act.activation(room[0][:, :], ps[2][:, :], ACT.Sigmoid, bias=col(BG2)).then_inc(qk2_cp.sem, 1)
                norm_copy(act, n1, i, 5, x_t, ps[6])
                soft_act(act, i, d2, s2)
            act.wait_ge(w_late, 16 * 17)
            with act.Fori(0, NBLK) as i:
                for e in range(E):
                    act.wait_ge(xm2_mm.sem, xm2_mm.at(i, e))
                    if e >= 2:
                        act.wait_ge(up2_mm.sem, up2_mm.at(i, e - 2))
                    act.activation(room[2 + e % 2][:, :], ps[6 + e % 2][:, :], ACT.Copy).then_inc(xm2_cp.sem, 1)
                    if e == 0:
                        act.wait_ge(gt2_mm.sem, gt2_mm.at(i))
                        act.activation(gt[0:E, :], ps[4][0:E, :], ACT.Copy).then_inc(gt2.sem, 1)
                    act.wait_ge(up2_mm.sem, up2_mm.at(i, e))
                    if e >= 2:
                        act.wait_ge(dn2_mm.sem, dn2_mm.at(i, e - 2))
                    act.activation(room[4 + e % 2][:, :], ps[e % 2][:, :], ACT.Gelu,
                                   bias=b1_2[:, e:e + 1]).then_inc(h2.sem, 1)
                load_table(act, 5, ACT.Silu)
                norm_copy(act, n2, i, 0, x_t, ps[6])
                for w, b in enumerate((BQ3, BK3, BV3)):
                    act.wait_ge(pre3_mm.sem, pre3_mm.at(i, w))
                    act.activation(padded[w][:, :, 2:2 + SEQ], halves(ps[w][:, :]), ACT.Silu,
                                   bias=col(b)).then_inc(pre3.sem, 1)
                for w in range(2):
                    act.wait_ge(conv.sem, conv.at(i, w))
                    act.activation(room[3 + w][:, :], room[6 + w][:, :], ACT.Silu).then_inc(csl.sem, 1)
                act.wait_ge(csl.sem, csl.at(i, 1))
                act.activation(room[6][:, :], room[3][:, :], ACT.Square)
                act.activation(room[7][:, :], room[4][:, :], ACT.Square).then_inc(sq3.sem, 1)
                act.wait_ge(conv.sem, conv.at(i, 2))
                act.activation(room[5][:, :], room[8][:, :], ACT.Silu).then_inc(csl.sem, 1)
                for w, b in enumerate((BA3, BB3)):
                    act.wait_ge(pre3_mm.sem, pre3_mm.at(i, 3 + w))
                    act.activation(room[9 + w][:, :], ps[3 + w][:, :], ACT.Sigmoid,
                                   bias=col(b)).then_inc(pre3.sem, 1)

            def copy_rep(i, h):
                act.wait_ge(rep_mm.sem, rep_mm.at(i, h))
                for g in range(2):
                    for e in range(4):
                        for dst, bank in ((wide(h), ps[g]), (gated_keys[h], ps[2 + g])):
                            act.activation(dst[:, :, :, 4 * g + e],
                                           bank[:, e * P:(e + 1) * P].rearrange("p (b t) -> p t b", b=SEQS),
                                           ACT.Copy)
                bvv = hist[2].rearrange("p (b t) -> p t b", b=SEQS)
                act.activation(gated_keys[h][:, :, :, DH], bvv[:, bass.ds(i * NSTEP + h * STEPS, STEPS), :],
                               ACT.Copy).then_inc(rep_cp.sem, 1)

            def delta_act(i, last):
                for h in range(CPT):
                    if h == 0:
                        copy_rep(i, 1)
                    elif not last:
                        copy_rep(i + 1, 0)
                    act.wait_ge(o3_mm.sem, o3_mm.at(i, h))
                    o3v = hist[0].rearrange("p (b t) -> p b t", b=SEQS)
                    act.activation(o3v[:, :, bass.ds(i * NSTEP + h * STEPS, STEPS)],
                                   ps[4 + h][:, 0:STEPS * SEQS].rearrange("p (b t) -> p b t", b=SEQS),
                                   ACT.Identity, bias=col(BO3)).then_inc(o3.sem, 1)

            copy_rep(0, 0)
            with act.Fori(0, TURNS - 1) as i:
                delta_act(i, False)
            delta_act(TURNS - 1, True)
            with act.Fori(0, NBLK) as i:
                act.wait_ge(o3.sem, CPT * TURNS)
                act.activation(room[0][:, :], hist[0][:, bass.ds(i * BLK, BLK)], ACT.Copy).then_inc(o3_st.sem, 1)
                norm_copy(act, n4, i, 0, x_t, ps[6])
                act.wait_ge(sig3_in.sem, sig3_in.at(i))
                act.activation(score_r[:, :, :], score[:, :, :], ACT.Sigmoid).then_inc(sig3.sem, 1)
                for p in range(E // 2 + 1):
                    act.wait_ge(up3_mm.sem, up3_mm.at(i, p))
                    if p < E // 2:
                        act.activation(room[1 + p][:, :], ps[p % 2][:, :], ACT.Gelu,
                                       bias=b1_3[:, p:p + 1]).then_inc(h3.sem, 1)
                    else:
                        act.activation(room[1 + p][0:64, :], ps[p % 2][0:64, :], ACT.Gelu,
                                       bias=cols[0:64, BS3:BS3 + 1]).then_inc(h3.sem, 1)
                act.wait_ge(gt3_mm.sem, gt3_mm.at(i))
                act.activation(gt[0:E, :], ps[4][0:E, :], ACT.Copy).then_inc(gt3.sem, 1)

        @block.tensor
        def _(pe):
            pe.wait_ge(w_small, 16 * 22)
            for p in range(PAIRS):
                src = (room[1] if p < 4 else room[2])[:, (p % 4) * P:(p % 4 + 1) * P]
                for j in range(2):
                    rows = slice(j * 64, j * 64 + 64)
                    last = pe.matmul(ps[p // 4][rows, (p % 4) * P:(p % 4 + 1) * P],
                                     room[0][rows, p * RANK0:(p + 1) * RANK0], src[rows, :],
                                     start=True, stop=True)
            last.then_inc(vo_mm, 1)
            pe.wait_ge(vo_done, 2)
            pe.wait_ge(split_done, RAWS - POOL_RAWS)
            pe.wait_ge(pool_split, POOL_RAWS)
            with pe.Fori(0, NBLK) as i:
                norm_transpose(pe, n1, i, 0, 0, x_new, ps[6])
                pe.wait_ge(n1.xt.sem, n1.xt.at(i, 0))
                pe.matmul(ps[7][:, :], wd0[:, :], h_t[:, :], start=True, stop=True)
                for k in range(TPB):
                    last = pe.matmul(ps[5][:, k * RANK0:(k + 1) * RANK0], h_t[:, k * P:(k + 1) * P],
                                     wd0[:, RANK0:2 * RANK0], start=True, stop=True)
                last.then_inc(c_mm.sem, 1)
                pe.wait_ge(c_cp.sem, c_cp.at(i))

                def project(p, w):
                    rows = slice(w * 64, w * 64 + 64)
                    if p >= 1:
                        pe.wait_ge(qk_cp.sem, qk_cp.at(i, 2 * (p - 1) + w))
                    pe.matmul(ps[w][:, :], wup0[rows, p * P:(p + 1) * P], c_t[rows, :],
                              start=True, stop=True).then_inc(qk_mm.sem, 1)

                project(0, 0)
                project(0, 1)
                project(1, 0)
                for n in range(UNITS + 6):
                    if n < UNITS:
                        p, j, s = n // 4, (n // 2) % 2, n % 2
                        rows = slice(j * 64, j * 64 + 64)
                        pe.wait_ge(qk_rot.sem, qk_rot.at(i, 2 * p + 1))
                        if n >= 2:
                            pe.wait_ge(pr_exp.sem, pr_exp.at(i, n - 2))
                        q_r, k_r = rot[0][p % 2], rot[1][p % 2]
                        for q in range(2):
                            last = pe.matmul(ps[2 + n % 2][:, q * SEQ:(q + 1) * SEQ],
                                             q_r[rows, s * SEQ + q * P:s * SEQ + (q + 1) * P],
                                             k_r[rows, s * SEQ:(s + 1) * SEQ], start=True, stop=True)
                        last.then_inc(sc_mm.sem, 1)
                    if 0 <= n - 2 < UNITS:
                        m = n - 2
                        if m >= 2:
                            pe.wait_ge(pt_cp.sem, pt_cp.at(i, m - 2))
                        keep_warm(pe, ps[4 + m % 2], UNIT_FILL[n % 4])
                        pe.wait_ge(pr_norm.sem, pr_norm.at(i, m))
                        for kt in range(2):
                            for q in range(2):
                                last = pe.transpose(ps[4 + m % 2][:, kt * SEQ + q * P:kt * SEQ + (q + 1) * P],
                                                    ex[m % 2][:, q * SEQ + kt * P:q * SEQ + (kt + 1) * P],
                                                    ident[:, :])
                        last.then_inc(pt_mm.sem, 1)
                    if 0 <= n - 3 < UNITS:
                        m = n - 3
                        p, j, s = m // 4, (m // 2) % 2, m % 2
                        pe.wait_ge(pt_cp.sem, pt_cp.at(i, m))
                        if m % 4 == 0 and p >= 1:
                            pe.wait_ge(ov_cp.sem, ov_cp.at(i, p - 1))
                        for kt in range(2):
                            last = pe.matmul(ps[6][j * 64:j * 64 + 64, s * SEQ:(s + 1) * SEQ],
                                             ck[:, (2 * s + kt) * RANK0:(2 * s + kt + 1) * RANK0],
                                             pts[m % 2][:, kt * SEQ:(kt + 1) * SEQ],
                                             start=(kt == 0), stop=(kt == 1))
                        last.then_inc(pv_mm.sem, 1)
                    if n % 4 == 0 and n // 4 + 1 < PAIRS:
                        project(n // 4 + 1, 1)
                    if n % 4 == 3 and n // 4 + 2 < PAIRS:
                        project(n // 4 + 2, 0)
                    if n >= 6 and (n - 6) % 4 == 3 and n - 6 < UNITS:
                        p = (n - 6) // 4
                        pe.wait_ge(ov_cp.sem, ov_cp.at(i, p))
                        for k in range(TPB):
                            last = pe.matmul(ps[7][:, k * P:(k + 1) * P], ovs[:, k * P:(k + 1) * P],
                                             vo0[:, p, :], start=(p == 0 and k == 0), stop=(p == PAIRS - 1),
                                             skip_group_check=True)
                        last.then_inc(y0_mm.sem, 1)
                norm_transpose(pe, n1, i, 2, 1, x_new, ps[6])
                pe.wait_ge(n1.xt.sem, n1.xt.at(i, 1))
                router_mm(pe, x_t, wr0, ps[7], r0_mm)

                def up_0(e):
                    for c in range(2):
                        n = 2 * e + c
                        if n >= 2:
                            pe.wait_ge(h0.sem, h0.at(i, n - 2))
                        for g in range(2):
                            last = split_mm(pe, ps[2 * c + g], up0, e, 2 * g + c, i, 0, n == 0 and g == 0)
                        last.then_inc(up0_mm.sem, 1)

                up_0(0)
                for e in range(E):
                    if e + 1 < E:
                        up_0(e + 1)
                    if e >= 2:
                        pe.wait_ge(acc0.sem, acc0.at(i, e - 2))
                    for c in range(2):
                        n = 2 * e + c
                        last = split_down(pe, ps[4 + e % 2], 2 + n % 4, [w[:, e, c, :] for w in dn0],
                                          c == 0, c == 1, (h0_h.sem, h0_h.at(i, n)), (h0_l.sem, h0_l.at(i, n)))
                    last.then_inc(dn0_mm.sem, 1)
                norm_transpose(pe, n1, i, 3, 2, x_tok, ps[6])
                pe.wait_ge(n1.xt.sem, n1.xt.at(i, 2))
                for w in range(3):
                    pe.matmul(ps[w][:, :], w1a[:, w, :], x_t[:, :], start=True, stop=True).then_inc(qkv1_mm.sem, 1)
                pe.wait_ge(qk1.sem, qk1.at(i))
                pe.matmul(ps[3][:, :], head_ones[:, :], room[0][:, :], start=True, stop=True).then_inc(co1_mm.sem, 1)
                pe.wait_ge(ov1.sem, ov1.at(i))
                for k in range(TPB):
                    last = pe.matmul(ps[4][:, k * P:(k + 1) * P], room[5][:, k * P:(k + 1) * P], w1a[:, 3, :],
                                     start=True, stop=True)
                last.then_inc(y1_mm.sem, 1)
                norm_transpose(pe, n1, i, 4, 3, x_tok, ps[6])
                pe.wait_ge(n1.xt.sem, n1.xt.at(i, 3))
                router_mm(pe, x_t, wr1, ps[7], r1_mm)

                def up_1(x):
                    for c in range(CH1):
                        n = CH1 * x + c
                        if n >= CH1:
                            pe.wait_ge(h1.sem, h1.at(i, n - CH1))
                        split_mm(pe, ps[n % 4], up1, x, c, i, 1, n == 0).then_inc(up1_mm.sem, 1)

                up_1(0)
                for x in range(NE1):
                    if x + 1 < NE1:
                        up_1(x + 1)
                    o = max(x - 1, 0)
                    if o >= 2 and x >= 2:
                        pe.wait_ge(acc1.sem, acc1.at(i, o - 2))
                    for c in range(CH1):
                        n = CH1 * x + c
                        last = split_down(pe, ps[4 + o % 2], n % (2 * CH1), [w[:, x, c, :] for w in dn1],
                                          c == 0 and x != 1, c == CH1 - 1,
                                          (h1.sem, h1.at(i, n)), low_1_done(i, n))
                    last.then_inc(dn1_mm.sem, 1)
                norm_transpose(pe, n1, i, 5, 4, x_tok, ps[6])
                pe.wait_ge(n1.xt.sem, n1.xt.at(i, 4))
                for w, wt in enumerate((w2a[:, 0, :], w2a[:, 1, :], wg2[:, :])):
                    pe.matmul(ps[w][:, :], wt, x_t[:, :], start=True, stop=True).then_inc(qk2_mm.sem, 1)

                def value_2(j):
                    if j >= 2:
                        pe.wait_ge(kv2.sem, kv2.at(i, j - 2))
                    pe.matmul(ps[3 + j % 2][:, :], wv2[:, j, :], x_t[:, :], start=True, stop=True).then_inc(v2_mm.sem, 1)

                value_2(0)
                value_2(1)
                for j in range(DH):
                    if j + 2 < DH:
                        value_2(j + 2)
                    if j == 0:
                        keep_warm(pe, ps[7], SCAN_FILL)
                    pe.wait_ge(qs2.sem, qs2.at(i, j))
                    for k in range(TPB):
                        last = pe.matmul(ps[7][:, k * P:(k + 1) * P], room[9 + j % 2][:, k * P:(k + 1) * P],
                                         wo2[:, j, :], start=(j == 0 and k == 0), stop=(j == DH - 1),
                                         skip_group_check=True)
                    last.then_inc(y2_mm.sem, 1)
                norm_transpose(pe, n1, i, 6, 5, x_tok, ps[6])
                pe.wait_ge(n1.xt.sem, n1.xt.at(i, 5))
                router_mm(pe, x_t, wr2, ps[7], r2_mm)
            pe.wait_ge(s2_done, 1)
            for n in range(2):
                last = pe.matmul(ps[0][0:E, n:n + 1], load2[:, n, :], ones[:, :], start=True, stop=True)
            last.then_inc(fix_mm, 1)
            pe.wait_ge(w_late, 16 * 17)
            with pe.Fori(0, NBLK) as i:
                def turn_2(e):
                    pe.wait_ge(xm2.sem, xm2.at(i, e))
                    if e >= 2:
                        pe.wait_ge(xm2_cp.sem, xm2_cp.at(i, e - 2))
                    for k in range(TPB):
                        last = pe.transpose(ps[6 + e % 2][:, k * P:(k + 1) * P],
                                            room[e % 2][:, k * P:(k + 1) * P], ident[:, :])
                    last.then_inc(xm2_mm.sem, 1)

                keep_warm_32(pe, ps[1], 4)
                turn_2(0)
                for k in range(TPB):
                    last = pe.transpose(ps[4][0:E, k * P:(k + 1) * P], gates[:, k, :], ident[:, :])
                last.then_inc(gt2_mm.sem, 1)
                for e in range(E + 1):
                    if e + 1 < E:
                        turn_2(e + 1)
                    if e == 1:
                        pe.wait_ge(gt2.sem, gt2.at(i))
                        for k in range(TPB):
                            last = pe.matmul(ps[5][:, k * P:(k + 1) * P], gt[0:E, k * P:(k + 1) * P],
                                             b2_2[:, :], start=True, stop=True)
                        last.then_inc(bias2_mm.sem, 1)
                    if e < E:
                        pe.wait_ge(xm2_cp.sem, xm2_cp.at(i, e))
                        if e >= 2:
                            pe.wait_ge(h2.sem, h2.at(i, e - 2))
                        pe.matmul(ps[e % 2][:, :], up2[:, e, :], room[2 + e % 2][:, :],
                                  start=True, stop=True).then_inc(up2_mm.sem, 1)
                    if e >= 1:
                        m = e - 1
                        pe.wait_ge(h2.sem, h2.at(i, m))
                        if m >= 2:
                            pe.wait_ge(acc2.sem, acc2.at(i, m - 2))
                        for k in range(TPB):
                            last = pe.matmul(ps[2 + m % 2][:, k * P:(k + 1) * P],
                                             room[4 + m % 2][:, k * P:(k + 1) * P], dn2[:, m, :],
                                             start=True, stop=True)
                        last.then_inc(dn2_mm.sem, 1)
                norm_transpose(pe, n2, i, 0, 0, x_tok, ps[6])
                pe.wait_ge(n2.xt.sem, n2.xt.at(i))
                for w in range(5):
                    wt = w3a[:, w, :] if w < 3 else wab3[:, w - 3, :]
                    pe.matmul(ps[w][:, :], wt, x_t[:, :], start=True, stop=True).then_inc(pre3_mm.sem, 1)
                pe.wait_ge(sq3.sem, sq3.at(i))
                for w in range(2):
                    for k in range(TPB):
                        last = pe.matmul(ps[5][:, w * TPB + k:w * TPB + k + 1],
                                         room[6 + w][:, k * P:(k + 1) * P], ones[:, :], start=True, stop=True)
                last.then_inc(ss3_mm.sem, 1)
                pe.wait_ge(rn3.sem, rn3.at(i))
                for w in range(2):
                    for k in range(TPB):
                        n = w * TPB + k
                        last = pe.matmul(ps[6 + w][:, k * P:(k + 1) * P], rn[:, n:n + 1].to_broadcast([P, P]),
                                         ident[:, :], start=True, stop=True)
                    last.then_inc(rb3_mm.sem, 1)

            def replicate(i, h, first):
                if first:
                    pe.wait_ge(taken3.sem, NBLK)
                else:
                    pe.wait_ge(rep_cp.sem, i * CPT + h)
                for n, src in enumerate((hist[1], hist[4])):
                    kv = src.rearrange("p (b t) -> p b t", b=SEQS)[:, :, bass.ds(i * NSTEP + h * STEPS, STEPS)]
                    for e in range(DH):
                        last = pe.matmul(ps[2 * n + e // 4][:, (e % 4) * P:(e % 4 + 1) * P], sel_e[:, e, :], kv,
                                         start=True, stop=True)
                last.then_inc(rep_mm.sem, 1)

            def project_3(i, h):
                pe.wait_ge(read.sem, read.at(i, STEPS * (h + 1) - 1))
                for e in range(DH):
                    last = pe.matmul(ps[4 + h][:, 0:STEPS * SEQS], wo3[:, e, :],
                                     wide(4 + h)[:, :, :, e].rearrange("p t b -> p b t"),
                                     start=(e == 0), stop=(e == DH - 1))
                last.then_inc(o3_mm.sem, 1)

            def delta_pe(i, last):
                replicate(i, 1, False)
                project_3(i, 0)
                if not last:
                    replicate(i + 1, 0, False)
                project_3(i, 1)

            replicate(0, 0, True)
            with pe.Fori(0, TURNS - 1) as i:
                delta_pe(i, False)
            delta_pe(TURNS - 1, True)
            with pe.Fori(0, NBLK) as i:
                pe.wait_ge(o3_st.sem, o3_st.at(i))
                for k in range(TPB):
                    last = pe.transpose(ps[6][:, k * P:(k + 1) * P], room[0][:, k * P:(k + 1) * P], ident[:, :])
                last.then_inc(o3_tr.sem, 1)
                norm_transpose(pe, n4, i, 0, 0, x_tok, ps[6])
                pe.wait_ge(n4.xt.sem, n4.xt.at(i))
                router_mm(pe, x_t, wr3, ps[7], r3_mm)
                for p in range(E // 2 + 1):
                    if p >= 2:
                        pe.wait_ge(h3.sem, h3.at(i, p - 2))
                    if p < E // 2:
                        last = pe.matmul(ps[p % 2][:, :], up3[:, p, :], x_t[:, :], start=True, stop=True)
                    else:
                        last = pe.matmul(ps[p % 2][0:64, :], ws1_3[:, :], x_t[:, :], start=True, stop=True)
                    last.then_inc(up3_mm.sem, 1)
                pe.wait_ge(g3.sem, g3.at(i))
                for k in range(TPB):
                    last = pe.transpose(ps[4][0:E, k * P:(k + 1) * P], gates[:, k, :], ident[:, :])
                last.then_inc(gt3_mm.sem, 1)
                pe.wait_ge(gt3.sem, gt3.at(i))

                def gate_rows(p):
                    if p >= 2:
                        pe.wait_ge(hg3.sem, hg3.at(i, p - 2))
                    pe.matmul(ps[2 + p % 2][:, :], sel_pair[:, p, :], gt[0:E, :],
                              start=True, stop=True).then_inc(gb3_mm.sem, 1)

                gate_rows(0)
                gate_rows(1)
                pe.wait_ge(h3.sem, h3.at(i, E // 2))
                for k in range(TPB):
                    pe.matmul(ps[5][:, k * P:(k + 1) * P], gt[0:E + 1, k * P:(k + 1) * P], b2_3[:, :],
                              start=(k == 0), stop=False, skip_group_check=True)
                for k in range(TPB):
                    last = pe.matmul(ps[5][:, k * P:(k + 1) * P], room[5][0:64, k * P:(k + 1) * P],
                                     ws2_3[:, :], start=False, stop=False, skip_group_check=True)
                last.then_inc(dn3_mm.sem, 1)
                for p in range(E // 2):
                    pe.wait_ge(hg3.sem, hg3.at(i, p))
                    if p + 2 < E // 2:
                        gate_rows(p + 2)
                    for k in range(TPB):
                        last = pe.matmul(ps[5][:, k * P:(k + 1) * P], room[6 + p][:, k * P:(k + 1) * P],
                                         dn3[:, p, :], start=False, stop=(p == E // 2 - 1),
                                         skip_group_check=True)
                    last.then_inc(dn3_mm.sem, 1)

        @block.vector
        def _(dve):
            swap = [n ^ 1 for n in range(32)]
            dve.wait_ge(w_small, 16 * 22)
            dve.wait_ge(consts, 12)
            for n, (_, raw, high, low) in enumerate(raw_parts()):
                if not by_pool(n):
                    dve.wait_ge(high_done, n + 1)
                    dve.tensor_tensor(low, raw, high, ALU.subtract).then_inc(split_done, 1)
            dve.wait_ge(split_done, RAWS - POOL_RAWS)
            dve.wait_ge(pool_split, POOL_RAWS)
            x_tf, x_nf, x_if = (v[:, :, :].rearrange("p k m -> p (k m)") for v in (x_tok, x_new, x_in))
            with dve.Fori(0, NBLK) as i:
                st = Steps(dve, vstep, i, VPER1)
                dve.wait_ge(loaded_x.sem, i * 16 + 16)
                norm_stats(dve, st, n1, i, 0, x_in)
                norm_apply(dve, st, n1, i, 0, x_in, x_new)

                def swapped(p, w):
                    n = 2 * p + w
                    dve.wait_ge(qk_cp.sem, qk_cp.at(i, n))
                    if n >= 2:
                        dve.wait_ge(qk_rot.sem, qk_rot.at(i, n - 2))
                    st.sync()
                    st.do(dve.memset(gate_scratch[:, :], 0.0))
                    dve.stream_shuffle(sinm[w][:, :], qa[w][:, :], swap).then_inc(qk_swap.sem, 1)

                def rotate(p, w):
                    n = 2 * p + w
                    dve.wait_ge(qk_cos.sem, qk_cos.at(i, n))
                    dve.wait_ge(qk_sin.sem, qk_sin.at(i, n))
                    if p >= 2:
                        dve.wait_ge(sc_mm.sem, sc_mm.at(i, 4 * (p - 2) + 3))
                    dve.tensor_tensor(rot[w][p % 2][:, :], sinm[w][:, :], cosm[w][:, :],
                                      ALU.add).then_inc(qk_rot.sem, 1)

                for w in range(2):
                    swapped(0, w)
                for w in range(2):
                    dve.wait_ge(qk_swap.sem, qk_swap.at(i, w))
                    dve.tensor_tensor(halves(sinm[w][:, :]), halves(sinm[w][:, :]),
                                      rope_sin[:, :].unsqueeze(1).to_broadcast([P, SPB, SEQ]),
                                      ALU.mult).then_inc(qk_sin.sem, 1)
                for w in range(2):
                    rotate(0, w)
                for n in range(UNITS + 1):
                    if n < UNITS:
                        dve.wait_ge(sc_mm.sem, sc_mm.at(i, n))
                        if n >= 4:
                            dve.wait_ge(pr_exp.sem, pr_exp.at(i, n - 4))
                        st.do(dve.tensor_reduce(mx[:, n % 4, :], halves(ps[2 + n % 2][:, :]), AX_X, ALU.max))
                        st.sync()
                        dve.tensor_scalar(nmx[:, n % 4, :], mx[:, n % 4, :], -float(DH0) ** -0.5, None,
                                          ALU.mult).then_inc(sc_max.sem, 1)
                    if n >= 1:
                        m = n - 1
                        dve.wait_ge(pr_exp.sem, pr_exp.at(i, m))
                        st.do(dve.reciprocal(rinv[:, m % 4, :], rsum[:, m % 4, :]))
                        st.sync()
                        for q in range(2):
                            last = dve.tensor_scalar(ex[m % 2][:, q * SEQ:(q + 1) * SEQ],
                                                     ex[m % 2][:, q * SEQ:(q + 1) * SEQ],
                                                     rinv[:, m % 4, q:q + 1], None, ALU.mult)
                        last.then_inc(pr_norm.sem, 1)
                    if n // 4 + 1 < PAIRS and n % 4 in (0, 1):
                        swapped(n // 4 + 1, n % 4)
                    if n // 4 + 1 < PAIRS and n % 4 in (2, 3):
                        rotate(n // 4 + 1, n % 4 - 2)
                dve.wait_ge(y0_mm.sem, y0_mm.at(i, PAIRS - 1))
                dve.scalar_tensor_tensor(out=x_nf, in0=x_if, scalar=2.0, in1=ps[7][:, :], op0=ALU.mult,
                                         op1=ALU.add).then_inc(x_taken.sem, 1)
                dve.wait_ge(x_taken.sem, x_taken.at(i))
                norm_stats(dve, st, n1, i, 1, x_new)
                norm_apply(dve, st, n1, i, 1, x_new, x_tok)
                rms_stats(dve, st, n1, i, 2, x_tok, x_new)
                norm_apply(dve, st, n1, i, 2, x_tok, x_new, centre=False)
                st.do(dve.tensor_scalar(room[6][:, :], x_tf, 2.0, None, ALU.mult))
                low_x(dve, i, 0)
                dve.wait_ge(r0_mm.sem, r0_mm.at(i))
                st.do(dve.tensor_copy(score[:, :, :], ps[7][:, 0:TPB * E].rearrange("p (k e) -> p k e", e=E)))
                top_two(dve, st, score)
                soft_in(dve, st, top8[:, :, 0], top8[:, :, 1], d0)

                def gated_hidden(e):
                    for c in range(2):
                        n = 2 * e + c
                        dve.wait_ge(sl0.sem, sl0.at(i, n))
                        if n >= 4:
                            dve.wait_ge(h0_h.sem, h0_h.at(i, n - 4))
                            dve.wait_ge(h0_l.sem, h0_l.at(i, n - 4))
                        dve.tensor_tensor(room[8 + n % 4][:, :], ps[2 * c][:, :], room[n % 2][:, :],
                                          ALU.mult).then_inc(h0.sem, 1)

                gated_hidden(0)
                soft_out(dve, st, i, s0)
                gate_sum(dve, st, gates[:, :, :])
                for e in range(E):
                    if e + 1 < E:
                        gated_hidden(e + 1)
                    dve.wait_ge(dn0_mm.sem, dn0_mm.at(i, e))
                    if e >= 1:
                        dve.wait_ge(acc0.sem, acc0.at(i, e - 1))
                    gated_add(dve, st, ps[4 + e % 2], gates[:, :, e:e + 1],
                              x_new if e else tiles(room[6][:, :]), x_new).then_inc(acc0.sem, 1)
                st.sync()
                dve.wait_ge(acc0.sem, acc0.at(i, E - 1))
                norm_stats(dve, st, n1, i, 3, x_new)
                norm_apply(dve, st, n1, i, 3, x_new, x_tok)
                st.do(dve.tensor_tensor(x_new[:, :, :], x_tok[:, :, :],
                                        bo1[:, :].unsqueeze(1).to_broadcast([P, TPB, P]), ALU.add))
                dve.wait_ge(qkv1_f.sem, qkv1_f.at(i, 1))
                dve.tensor_tensor(room[0][:, :], room[2][:, :], room[3][:, :], ALU.mult).then_inc(qk1.sem, 1)
                dve.wait_ge(qkv1_f.sem, qkv1_f.at(i, 2))
                dve.wait_ge(co1_mm.sem, co1_mm.at(i))
                dve.tensor_tensor(room[5][:, :], ps[3][:, :], room[4][:, :], ALU.mult).then_inc(ov1.sem, 1)
                st.sync()
                dve.wait_ge(y1_mm.sem, y1_mm.at(i))
                st.do(dve.tensor_tensor(x_nf, x_nf, ps[4][:, :], ALU.add))
                st.sync()
                norm_stats(dve, st, n1, i, 4, x_new)
                norm_apply(dve, st, n1, i, 4, x_new, x_tok)
                st.do(dve.tensor_scalar(x_nf, x_tf, 2.0, None, ALU.mult))
                low_x(dve, i, 1)
                dve.wait_ge(r1_mm.sem, r1_mm.at(i))
                raw = ps[7][:, 0:TPB * E].rearrange("p (k e) -> p k e", e=E)
                st.do(dve.tensor_copy(score_r[:, :, :], raw))
                st.sync()
                dve.tensor_tensor(score[:, :, :], raw, rb1[:, :].unsqueeze(1).to_broadcast([P, TPB, E]),
                                  ALU.add).then_inc(rt1.sem, 1)

                dve.wait_ge(rsig1.sem, rsig1.at(i))
                top_two(dve, st, score)
                pick_two(dve, st, score_r)
                soft_in(dve, st, two[:, 0, :], two[:, 1, :], d1)
                soft_out(dve, st, i, s1)
                gate_sum(dve, st, gates[:, :, :])
                st.sync()
                for x in range(1, NSH + 1):
                    low_1(dve, i, x, 0)
                dve.wait_ge(dn1_mm.sem, dn1_mm.at(i, 1))
                dve.tensor_tensor(x_nf, x_nf, ps[4][:, :], ALU.add).then_inc(acc1.sem, 1)
                for e in range(E):
                    if e + NSH + 1 < NE1:
                        low_1(dve, i, e + NSH + 1, 0)
                    dve.wait_ge(dn1_mm.sem, dn1_mm.at(i, e + NSH))
                    dve.wait_ge(acc1.sem, acc1.at(i, e))
                    gated_add(dve, st, ps[4 + (e + 1) % 2], gates[:, :, e:e + 1], x_new,
                              x_new).then_inc(acc1.sem, 1)
                st.sync()
                dve.wait_ge(acc1.sem, acc1.at(i, E))
                norm_stats(dve, st, n1, i, 5, x_new)
                norm_apply(dve, st, n1, i, 5, x_new, x_tok)
                for w in range(2):
                    dve.wait_ge(qk2_cp.sem, qk2_cp.at(i, w))
                    dve.tensor_scalar(room[1 + w][:, :], room[3 + w][:, :], 0.0, None,
                                      ALU.min).then_inc(qk2_min.sem, 1)
                for w in range(2):
                    dve.wait_ge(qk2_exp.sem, qk2_exp.at(i, w))
                    dve.scalar_tensor_tensor(out=room[1 + w][:, :], in0=room[3 + w][:, :], scalar=0.0,
                                             in1=room[5 + w][:, :], op0=ALU.max,
                                             op1=ALU.add).then_inc(qk2_f.sem, 1)
                dve.wait_ge(qk2_cp.sem, qk2_cp.at(i, 2))
                for s in range(SPB):
                    st.do(dve.memset(room[0][:, s * SEQ:s * SEQ + 1], 0.0))
                dve.wait_ge(qk2_f.sem, qk2_f.at(i, 1))

                def key_value(j):
                    dve.wait_ge(v2_mm.sem, v2_mm.at(i, j))
                    if j >= 2:
                        dve.wait_ge(sc2.sem, sc2.at(i, j - 2))
                    dve.tensor_tensor(room[11 + j % 2][:, :], ps[3 + j % 2][:, :], room[2][:, :],
                                      ALU.mult).then_inc(kv2.sem, 1)

                key_value(0)
                st.sync()
                for j in range(DH):
                    if j + 1 < DH:
                        key_value(j + 1)
                    dve.wait_ge(kv2.sem, kv2.at(i, j))
                    if j >= 2:
                        dve.wait_ge(qs2.sem, qs2.at(i, j - 2))
                    dve.tensor_tensor_scan(room[7 + j % 2][:, :], room[0][:, :], room[11 + j % 2][:, :], 0.0,
                                           ALU.mult, ALU.add).then_inc(sc2.sem, 1)
                dve.wait_ge(y2_mm.sem, y2_mm.at(i, DH - 1))
                st.do(dve.tensor_tensor(x_nf, x_tf, ps[7][:, :], ALU.add))
                st.sync()
                norm_stats(dve, st, n1, i, 6, x_new)
                norm_apply(dve, st, n1, i, 6, x_new, x_tok)
                st.do(dve.tensor_scalar(keep[:, bass.ds(i * TPB, TPB), :], x_tok[:, :, :], 1.0, None, ALU.mult))
                dve.wait_ge(r2_mm.sem, r2_mm.at(i))
                st.do(dve.tensor_tensor(score[:, :, :], ps[7][:, 0:TPB * E].rearrange("p (k e) -> p k e", e=E),
                                        rb2[:, :].unsqueeze(1).to_broadcast([P, TPB, E]), ALU.add))
                top_two(dve, st, score)
                soft_two(dve, st, top8[:, :, 0], top8[:, :, 1], d2)
                dve.wait_ge(s2.sem, s2.at(i))
                gate_sum(dve, st, gate2[:, bass.ds(i * TPB, TPB), :])
                st.do(dve.tensor_reduce(load2_b[:, :, :].rearrange("p n e -> p (n e)"),
                                        ohs[:, :, :, :].rearrange("p n t e -> p n e t"), AX_X, ALU.add))
                st.sync()
                st.do(dve.tensor_tensor(load2[:, :, :], load2[:, :, :], load2_b[:, :, :], ALU.add))
                st.sync()
                st.end()
            dve.memset(gate_scratch[:, :], 0.0).then_inc(s2_done, 1)
            dve.wait_ge(s2_done, 1)
            dve.wait_ge(fix_mm, 1)
            dve.tensor_tensor(gate2[0:E, 0, 0:2], gate2[0:E, 0, 0:2], ps[0][0:E, 0:2], ALU.add).then_inc(fixed, 1)
            dve.wait_ge(fixed, 1)
            dve.tensor_scalar(gate2[:, :, :], gate2[:, :, :], float(CAP), None, ALU.min).then_inc(fixed, 1)
            dve.wait_ge(fixed, 2)
            for g in range(2):
                for n in range(2):
                    dve.memset(st3[g][n][:, :, :], 1.0).then_inc(fixed, 1)
            dve.wait_ge(fixed, 6)
            for g in range(2):
                dve.memset(st3[g][0][:, :, 0:DH], 0.0).then_inc(state[g].sem, 1)
            dve.wait_ge(w_late, 16 * 17)
            with dve.Fori(0, NBLK) as i:
                st = Steps(dve, vstep2, i, VPER2)
                st.do(dve.tensor_scalar(gates[:, :, :], gate2[:, bass.ds(i * TPB, TPB), :], 1.0, None, ALU.mult))
                dve.tensor_scalar(x_tok[:, :, :], keep[:, bass.ds(i * TPB, TPB), :], 1.0, None, ALU.mult).then_inc(taken2.sem, 1)
                dve.wait_ge(taken2.sem, taken2.at(i))
                dve.wait_ge(bias2_mm.sem, bias2_mm.at(i))
                st.do(dve.tensor_tensor(x_nf, x_tf, ps[5][:, :], ALU.add))
                for e in range(E):
                    dve.wait_ge(dn2_mm.sem, dn2_mm.at(i, e))
                    if e >= 1:
                        dve.wait_ge(acc2.sem, acc2.at(i, e - 1))
                    gated_add(dve, st, ps[2 + e % 2], gates[:, :, e:e + 1], x_new, x_new).then_inc(acc2.sem, 1)
                st.sync()
                dve.wait_ge(acc2.sem, acc2.at(i, E - 1))
                norm_stats(dve, st, n2, i, 0, x_new)
                norm_apply(dve, st, n2, i, 0, x_new, x_tok)
                st.do(dve.tensor_scalar(keep[:, bass.ds(i * TPB, TPB), :], x_tok[:, :, :], 1.0, None, ALU.mult))
                for w in range(3):
                    dve.wait_ge(pre3.sem, pre3.at(i, w))
                    y = halves(room[6 + w][:, :])
                    st.do(dve.tensor_scalar(y, padded[w][:, :, 0:SEQ], conv3[:, w, 0:1], None, ALU.mult))
                    for k in range(1, 4):
                        if w == 2 and k == 3:
                            dve.wait_ge(ss3_mm.sem, ss3_mm.at(i))
                            dve.tensor_copy(ss[:, :], ps[5][:, 0:8]).then_inc(ss3.sem, 1)
                        st.sync()
                        last = dve.scalar_tensor_tensor(out=y, in0=padded[w][:, :, k:k + SEQ],
                                                        scalar=conv3[:, w, k:k + 1], in1=y,
                                                        op0=ALU.mult, op1=ALU.add)
                        if k < 3:
                            st.do(last)
                        else:
                            last.then_inc(conv.sem, 1)
                dve.wait_ge(nr3.sem, nr3.at(i))
                dve.reciprocal(rn[:, :], nre[:, :]).then_inc(rn3.sem, 1)
                dve.wait_ge(pre3.sem, pre3.at(i, 4))
                st.do(dve.tensor_scalar(hist[3][:, bass.ds(i * BLK, BLK)], room[9][:, :], 1.0, None, ALU.mult))
                st.do(dve.scalar_tensor_tensor(out=room[8][:, :], in0=room[9][:, :],
                                               scalar=-1.0, in1=room[10][:, :], op0=ALU.mult, op1=ALU.mult))
                for w in range(2):
                    dve.wait_ge(rb3_mm.sem, rb3_mm.at(i, w))
                    last = dve.tensor_tensor(hist[w][:, bass.ds(i * BLK, BLK)], ps[6 + w][:, :],
                                             room[3 + w][:, :], ALU.mult)
                    st.do(last)
                st.sync()
                st.do(dve.tensor_tensor(hist[4][:, bass.ds(i * BLK, BLK)], hist[1][:, bass.ds(i * BLK, BLK)],
                                        room[8][:, :], ALU.mult))
                st.sync()
                dve.wait_ge(bv3.sem, bv3.at(i))
                dve.memset(gate_scratch[:, :], 0.0).then_inc(taken3.sem, 1)
                dve.wait_ge(taken3.sem, taken3.at(i))
                st.end()

            def delta_dve(i):
                st = [Steps(dve, vstep3[g], i, VPER3) for g in range(2)]
                for n in range(NSTEP):
                    h, k = n // STEPS, n % STEPS
                    if k == 0:
                        dve.wait_ge(rep_cp.sem, rep_cp.at(i, h))
                    now = [st3[g][n % 2] for g in range(2)]
                    new = [st3[g][(n + 1) % 2] for g in range(2)]
                    rows = [slice(g * HS, (g + 1) * HS) for g in range(2)]
                    for g in range(2):
                        dve.wait_ge(state[g].sem, i * NSTEP + (n + 1))
                        st[g].do(dve.tensor_tensor(prod[g][:, :, :], now[g][:, :, :],
                                                   gated_keys[h][:, k, rows[g], :], ALU.mult))
                    for g in range(2):
                        st[g].sync()
                        st[g].do(dve.tensor_reduce(uu[g][:, :], prod[g][:, :, :], AX_X, ALU.add))
                    for g in range(2):
                        st[g].sync()
                        st[g].do(dve.tensor_tensor(upd[g][:, :, :], uu[g][:, :].unsqueeze(2).to_broadcast([P, HS, DH]),
                                                   wide(h)[:, k, rows[g], :], ALU.mult))
                    for g in range(2):
                        st[g].sync()
                        dve.wait_ge(decay[g].sem, decay[g].at(i, n))
                        dve.tensor_tensor(new[g][:, :, 0:DH], upd[g][:, :, :], decayed[g][:, :, :],
                                          ALU.add).then_inc(state[g].sem, 1)
                for g in range(2):
                    st[g].end()

            with dve.Fori(0, TURNS) as i:
                delta_dve(i)
            dve.memset(gate_scratch[:, :], 0.0).then_inc(stored, 1)
            with dve.Fori(0, NBLK) as i:
                st = Steps(dve, vstep4, i, VPER4)
                dve.wait_ge(o3_tr.sem, o3_tr.at(i))
                st.do(dve.tensor_tensor(x_new[:, :, :], keep[:, bass.ds(i * TPB, TPB), :], tiles(ps[6][:, :]),
                                        ALU.add))
                st.sync()
                norm_stats(dve, st, n4, i, 0, x_new)
                norm_apply(dve, st, n4, i, 0, x_new, x_tok)
                dve.wait_ge(r3_mm.sem, r3_mm.at(i))
                dve.tensor_copy(score[:, :, :],
                                ps[7][:, 0:TPB * E].rearrange("p (k e) -> p k e", e=E)).then_inc(sig3_in.sem, 1)
                dve.wait_ge(sig3.sem, sig3.at(i))
                st.do(dve.tensor_scalar(score[:, :, :], score_r[:, :, :], col(RS3), None, ALU.mult))
                top_two(dve, st, score)
                st.do(dve.tensor_tensor(dif[:, :], top8[:, :, 0], top8[:, :, 1], ALU.add))
                st.sync()
                st.do(dve.reciprocal(dif[:, :], dif[:, :]))
                st.sync()
                for n in range(2):
                    st.do(dve.tensor_tensor(wts[:, n, :], top8[:, :, n], dif[:, :], ALU.mult))
                st.sync()
                gate_sum(dve, st, gates[:, :, :])
                st.sync()
                dve.memset(gate_scratch[:, :], 0.0).then_inc(g3.sem, 1)
                for p in range(E // 2):
                    dve.wait_ge(h3.sem, h3.at(i, p))
                    dve.wait_ge(gb3_mm.sem, gb3_mm.at(i, p))
                    dve.tensor_tensor(room[6 + p][:, :], ps[2 + p % 2][:, :], room[1 + p][:, :],
                                      ALU.mult).then_inc(hg3.sem, 1)
                dve.wait_ge(dn3_mm.sem, dn3_mm.at(i, E // 2))
                st.do(dve.tensor_tensor(x_nf, x_tf, ps[5][:, :], ALU.add))
                st.sync()
                norm_stats(dve, st, n4, i, 1, x_new)
                dve.wait_ge(stored, i * 16 + 1)
                norm_apply(dve, st, n4, i, 1, x_new, x_out[:, :, :])
                st.end()


def rope_tables():
    import numpy as np
    inv = 1.0 / 10000.0 ** (np.arange(0, DH0, 2, dtype=np.float32) / DH0)
    freqs = np.outer(np.arange(SEQ, dtype=np.float32), inv)
    cos = np.concatenate([np.cos(freqs), np.cos(freqs)], -1)[:, ::2]
    sin = np.concatenate([np.sin(freqs), np.sin(freqs)], -1)[:, ::2]
    cos_rows = np.repeat(cos.T, 2, axis=0)
    sin_rows = np.repeat(sin.T, 2, axis=0)
    sin_rows[0::2] *= -1.0
    return (np.tile(cos_rows, (2, 1)).astype(np.float32), np.tile(sin_rows, (2, 1)).astype(np.float32))


def kernel(**inputs):
    import numpy as np
    import concourse.bacc as bacc
    from concourse.bass_utils import run_bass_kernel_spmd as run

    g = {k: np.asarray(v) for k, v in inputs.items()}
    a = {}

    def rows(v):
        return np.broadcast_to(v, (P,) + v.shape)

    def column(v):
        return np.broadcast_to(v.reshape(-1, 1), (v.size, 1)) if v.size == P else rows(v.reshape(1))

    cos, sin = rope_tables()
    eye = np.eye(P, dtype=np.float32)
    head = np.arange(P) // DH
    a["x"] = g["L0_attn_x"]
    a["ident"] = eye
    a["rope_cos"], a["rope_sin"] = cos, sin
    a["iota8"] = rows(np.arange(E, dtype=np.float32))
    a["head_ones"] = (head[:, None] == head[None, :]).astype(np.float32)
    a["sel_e"] = np.stack([((head[:, None] == head[None, :]) & (np.arange(P)[:, None] % DH == e))
                           for e in range(DH)], 1).astype(np.float32)
    a["sel_pair"] = np.stack([np.arange(E)[:, None] == 2 * p + np.arange(P)[None, :] // 64
                              for p in range(E // 2)], 1).astype(np.float32)
    per_head = lambda v: np.repeat(v, DH, axis=0)
    cols = [g["L0_attn_ln_scale"], g["L0_attn_ln_bias"], g["L0_ffn_norm_scale"], g["L1_attn_bq"], g["L1_attn_bk"],
            g["L1_attn_bv"], per_head(g["L2_attn_bg"]), g["L3_attn_bq"], g["L3_attn_bk"], g["L3_attn_bv"],
            per_head(g["L3_attn_ba"]), per_head(g["L3_attn_bb"]), g["L3_attn_bo"],
            np.concatenate([g["L3_ffn_bs1"], g["L3_ffn_bs1"]]),
            np.broadcast_to(g["L3_ffn_route_scale"], (P,))]
    cols += [np.zeros(P, np.float32)] * (24 - len(cols))
    a["cols"] = np.stack(cols, 1)
    a["wd0"] = np.concatenate([g["L0_attn_w_down_q"].T, g["L0_attn_w_down_kv"].T], 1)
    a["wup0"] = np.concatenate([g["L0_attn_w_up_q"].T, g["L0_attn_w_up_k"].T], 0)
    a["wv0"] = g["L0_attn_w_up_v"].reshape(PAIRS, P, RANK0).transpose(1, 0, 2).reshape(P, PAIRS * RANK0)
    wo = g["L0_attn_w_out"].T.reshape(PAIRS, P, D).transpose(1, 0, 2)
    a["wo0a"], a["wo0b"] = wo[:, 0:4].reshape(P, -1), wo[:, 4:8].reshape(P, -1)
    a["wr0"] = g["L0_ffn_w_router"].T
    a["up0"] = g["L0_ffn_w_up"].reshape(E, CH0, P, D).transpose(3, 0, 1, 2)
    a["dn0"] = g["L0_ffn_w_down"].reshape(E, D, 2, P).transpose(3, 0, 2, 1)
    a["w1a"] = np.stack([g["L1_attn_Wq"], g["L1_attn_Wk"], g["L1_attn_Wv"], g["L1_attn_Wo"]], 1)
    a["bo1"] = rows(g["L1_attn_bo"])
    a["wr1"] = g["L1_ffn_centroids"].T
    a["rb1"] = rows(g["L1_ffn_routing_bias"])
    up1 = np.concatenate([g["L1_ffn_Wfc_sh"], g["L1_ffn_Wfc_r"]], 0)
    dn1 = np.concatenate([g["L1_ffn_Wproj_sh"], g["L1_ffn_Wproj_r"]], 0)
    a["up1"] = up1.reshape(E + NSH, CH1, P, D).transpose(3, 0, 1, 2)
    a["dn1"] = dn1.reshape(E + NSH, D, CH1, P).transpose(3, 0, 2, 1)
    a["w2a"] = np.stack([g["L2_attn_Wq"].T, g["L2_attn_Wk"].T], 1)
    a["wv2"] = np.repeat(g["L2_attn_Wv"].T.reshape(D, P // DH, DH).transpose(0, 2, 1), DH, axis=2)
    a["wg2"] = per_head(g["L2_attn_Wg"]).T
    spread = lambda w: np.stack([np.repeat(w.T.reshape(P // DH, DH, D)[:, j], DH, axis=0) for j in range(DH)], 1)
    a["wo2"] = spread(g["L2_attn_Wo"])
    a["wr2"], a["rb2"] = g["L2_ffn_router_w"], rows(g["L2_ffn_router_b"])
    a["up2"] = g["L2_ffn_w1"].transpose(1, 0, 2)
    a["dn2"] = g["L2_ffn_w2"].transpose(1, 0, 2)
    a["b1_2"], a["b2_2"] = g["L2_ffn_b1"].T, g["L2_ffn_b2"]
    a["w3a"] = np.stack([g["L3_attn_Wq"].T, g["L3_attn_Wk"].T, g["L3_attn_Wv"].T], 1)
    a["wab3"] = np.stack([per_head(g["L3_attn_Wa"]).T, per_head(g["L3_attn_Wb"]).T], 1)
    a["conv3"] = np.stack([g["L3_attn_conv_q"][:, 0], g["L3_attn_conv_k"][:, 0], g["L3_attn_conv_v"][:, 0]], 1)
    a["wo3"] = spread(g["L3_attn_Wo"])
    a["wr3"] = g["L3_ffn_gate_W"]
    a["up3"] = g["L3_ffn_W1"].reshape(E // 2, 2, D, 64).transpose(2, 0, 1, 3)
    a["dn3"] = g["L3_ffn_W2"].reshape(E // 2, P, D).transpose(1, 0, 2)
    a["b1_3"] = g["L3_ffn_b1"].reshape(E // 2, P).T
    a["b2_3"] = np.concatenate([g["L3_ffn_b2"], g["L3_ffn_bs2"][None]], 0)
    a["ws1_3"], a["ws2_3"] = g["L3_ffn_Ws1"], g["L3_ffn_Ws2"]

    nc = bacc.Bacc("TRN2", target_bir_lowering=False, num_devices=1)
    t, arrays = {}, {}
    for name, v in a.items():
        if name == "up3":
            v = v.reshape(D, E // 2, P)
        v = np.ascontiguousarray(v)
        arrays["in_" + name] = v
        t[name] = nc.dram_tensor("in_" + name, v.shape, F32, kind="ExternalInput").ap()
    out = nc.dram_tensor("out", (SEQS, SEQ, D), F32, kind="ExternalOutput").ap()
    build(nc, t, out)
    return run(nc, [arrays], core_ids=[0]).results[0]["out"]
```
